# Optimizing a Trainium2 kernel written in Bass

```python
import numpy as np
import jax
import jax.numpy as jnp

def _softmax(x, axis=-1):
    return jax.nn.softmax(x, axis=axis)

def _gelu(x):
    return jax.nn.gelu(x, approximate=True)

def _silu(x):
    return jax.nn.silu(x)

def _sigmoid(x):
    return jax.nn.sigmoid(x)

def _layernorm(x, axis=-1, eps=1e-05):
    m = jnp.mean(x, axis=axis, keepdims=True)
    v = jnp.var(x, axis=axis, keepdims=True)
    return (x - m) / jnp.sqrt(v + eps)

def _scatter_add(tgt, idx, src, axis=0):
    return tgt.at[idx].add(src)

def _segment_sum(src, seg, n):
    return jax.ops.segment_sum(src, seg, n)
kernel_name = 'mk_recurrent_d4_jaxref_r8_0dc3a9'

def setup_inputs(seed: int=0):
    np.random.seed(seed)
    _w = jnp.asarray

    def _L0_attn_setup():
        import jax, jax.numpy as jnp
        import numpy as np
        B, L, D_INNER, N_STATE, DT_RANK = (2, 128, 256, 16, 64)
        key = jax.random.key(seed)
        k0, k1, k2, k3 = jax.random.split(key, 4)
        x = jax.random.normal(k0, (B, L, D_INNER), dtype=jnp.float32)
        W_x = jax.random.normal(k1, (DT_RANK + 2 * N_STATE, D_INNER), dtype=jnp.float32) * 0.02
        W_dt = jax.random.uniform(k2, (D_INNER, DT_RANK), minval=-0.1, maxval=0.1, dtype=jnp.float32)
        inv_dt_min = float(np.log(np.expm1(0.001)))
        inv_dt_max = float(np.log(np.expm1(0.1)))
        b_dt = jax.random.uniform(k3, (D_INNER,), minval=inv_dt_min, maxval=inv_dt_max, dtype=jnp.float32)
        A_log = jnp.log(jnp.broadcast_to(jnp.arange(1, N_STATE + 1, dtype=jnp.float32), (D_INNER, N_STATE)))
        D = jnp.ones((D_INNER,), dtype=jnp.float32)
        return {'x': x, 'W_x': W_x, 'W_dt': W_dt, 'b_dt': b_dt, 'A_log': A_log, 'D': D}
    _L0_attn_in = _L0_attn_setup()

    def _L0_ffn_setup():
        import jax, jax.numpy as jnp
        import numpy as np
        NUM_EXPERTS = 8
        TOP_K = 2
        MODEL_DIM = 256
        INTER_DIM = 128
        GATE_SCALE = 1.0
        UP_SCALE = 0.0
        key = jax.random.key(seed)
        k1, k2, k3, k4 = jax.random.split(key, 4)
        hidden_states = jax.random.normal(k1, (2, 256, MODEL_DIM), jnp.float32)
        router_gate = jax.random.normal(k2, (NUM_EXPERTS, MODEL_DIM), jnp.float32) * 0.02
        expert_gate_up = jax.random.normal(k3, (NUM_EXPERTS, MODEL_DIM, 2 * INTER_DIM), jnp.float32) * 0.02
        expert_down = jax.random.normal(k4, (NUM_EXPERTS, INTER_DIM, MODEL_DIM), jnp.float32) * 0.02
        return {'hidden_states': hidden_states, 'router_gate': router_gate, 'expert_gate_up': expert_gate_up, 'expert_down': expert_down}
    _L0_ffn_in = _L0_ffn_setup()

    def _L1_attn_setup():
        import jax, jax.numpy as jnp
        import numpy as np
        B, S, D_IN = (1, 128, 256)
        H_QK, H_V, DK, DV = (8, 16, 128, 128)
        KCONV = 4
        D_OUT = H_QK * DK
        D_OUT_VG = H_V * DV
        FUSED = 2 * D_OUT + D_OUT_VG
        EPS = 1e-06

        def l2_norm(t):
            return t / jnp.sqrt(jnp.sum(t * t, axis=-1, keepdims=True) + EPS)

        def rms_norm(t, w):
            var = jnp.mean(t * t, axis=-1, keepdims=True)
            return t * jax.lax.rsqrt(var + EPS) * w

        def gated_delta_rule(q, k, v, beta, alpha):
            q = q * q.shape[-1] ** (-0.5)
            S0 = jnp.zeros(q.shape[:2] + (q.shape[-1], v.shape[-1]), q.dtype)

            def step(Sm, inp):
                q_t, k_t, v_t, b_t, a_t = inp
                Sm = Sm * a_t[..., None, None]
                kv = jnp.einsum('bhk,bhkv->bhv', k_t, Sm)
                u = (v_t - kv) * b_t[..., None]
                Sm = Sm + k_t[..., None] * u[:, :, None, :]
                o = jnp.einsum('bhk,bhkv->bhv', q_t, Sm)
                return (Sm, o)
            xs = (jnp.moveaxis(q, 2, 0), jnp.moveaxis(k, 2, 0), jnp.moveaxis(v, 2, 0), jnp.moveaxis(beta, 2, 0), jnp.moveaxis(alpha, 2, 0))
            Sf, outs = jax.lax.scan(step, S0, xs)
            return (jnp.moveaxis(outs, 0, 2), Sf)
        key = jax.random.key(seed)
        ks = jax.random.split(key, 8)
        return {'x': jax.random.normal(ks[0], (B, S, D_IN), jnp.float32), 'w_qkv': jax.random.normal(ks[1], (FUSED, D_IN), jnp.float32) * 0.02, 'w_gate': jax.random.normal(ks[2], (D_OUT_VG, D_IN), jnp.float32) * 0.02, 'w_beta': jax.random.normal(ks[3], (H_V, D_IN), jnp.float32) * 0.02, 'w_alpha': jax.random.normal(ks[4], (H_V, D_IN), jnp.float32) * 0.02, 'log_A': jnp.log(jax.random.uniform(ks[5], (H_V,), jnp.float32, 0.001, 16.0)), 'dt_bias': jnp.ones((H_V,), jnp.float32), 'conv_w': jax.random.normal(ks[6], (FUSED, 1, KCONV), jnp.float32) * 0.1, 'rms_w': jnp.ones((DV,), jnp.float32), 'w_out': jax.random.normal(ks[7], (D_IN, D_OUT_VG), jnp.float32) * 0.02}
    _L1_attn_in = _L1_attn_setup()

    def _L1_ffn_setup():
        import jax, jax.numpy as jnp
        import numpy as np
        BLOCK_SIZE = 32
        HIDDEN_SIZE = 256
        MLP_DIM = 2048
        NVFP4_LUT = jnp.array([0.0, 0.5, 1.0, 1.5, 2.0, 3.0, 4.0, 6.0, 0.0, -0.5, -1.0, -1.5, -2.0, -3.0, -4.0, -6.0], dtype=jnp.float32)

        def dequant_nvfp4(W_packed, scales, block=BLOCK_SIZE):
            N = W_packed.shape[0]
            low = W_packed & 15
            high = W_packed >> 4 & 15
            idx = jnp.stack([low, high], axis=-1).reshape(N, -1)
            vals = NVFP4_LUT[idx]
            K = vals.shape[1]
            vals = vals.reshape(N, K // block, block) * scales[:, :, None]
            return vals.reshape(N, K)
        key = jax.random.key(seed)
        ks = jax.random.split(key, 7)
        x = jax.random.normal(ks[0], (4, 32, HIDDEN_SIZE), dtype=jnp.float32)
        gate_W_packed = jax.random.randint(ks[1], (MLP_DIM, HIDDEN_SIZE // 2), 0, 32, dtype=jnp.int32)
        gate_scales = jax.random.uniform(ks[2], (MLP_DIM, HIDDEN_SIZE // BLOCK_SIZE), dtype=jnp.float32) * 0.1 + 0.001
        up_W_packed = jax.random.randint(ks[3], (MLP_DIM, HIDDEN_SIZE // 2), 0, 32, dtype=jnp.int32)
        up_scales = jax.random.uniform(ks[4], (MLP_DIM, HIDDEN_SIZE // BLOCK_SIZE), dtype=jnp.float32) * 0.1 + 0.001
        down_W_packed = jax.random.randint(ks[5], (HIDDEN_SIZE, MLP_DIM // 2), 0, 32, dtype=jnp.int32)
        down_scales = jax.random.uniform(ks[6], (HIDDEN_SIZE, MLP_DIM // BLOCK_SIZE), dtype=jnp.float32) * 0.1 + 0.001
        return {'x': x, 'gate_W_packed': gate_W_packed, 'gate_scales': gate_scales, 'up_W_packed': up_W_packed, 'up_scales': up_scales, 'down_W_packed': down_W_packed, 'down_scales': down_scales}
    _L1_ffn_in = _L1_ffn_setup()

    def _L2_attn_setup():
        import jax, jax.numpy as jnp
        import numpy as np
        D_MODEL = 256
        N_HEADS = 16
        D_K = D_MODEL // N_HEADS
        EPS = 1e-06
        key = jax.random.key(seed)
        ks = jax.random.split(key, 9)
        s = 1.0 / np.sqrt(D_MODEL)
        return {'x': jax.random.normal(ks[0], (4, 512, D_MODEL), dtype=jnp.float32), 'Wq': jax.random.normal(ks[1], (D_MODEL, D_MODEL), dtype=jnp.float32) * s, 'bq': jnp.zeros((D_MODEL,), dtype=jnp.float32), 'Wk': jax.random.normal(ks[2], (D_MODEL, D_MODEL), dtype=jnp.float32) * s, 'bk': jnp.zeros((D_MODEL,), dtype=jnp.float32), 'Wv': jax.random.normal(ks[3], (D_MODEL, D_MODEL), dtype=jnp.float32) * s, 'bv': jnp.zeros((D_MODEL,), dtype=jnp.float32), 'Wo': jax.random.normal(ks[4], (D_MODEL, D_MODEL), dtype=jnp.float32) * s, 'bo': jnp.zeros((D_MODEL,), dtype=jnp.float32)}
    _L2_attn_in = _L2_attn_setup()

    def _L2_ffn_setup():
        import jax, jax.numpy as jnp
        import numpy as np
        TOPK = 2

        def _mlp(x, w1, w2, w3):
            a = jnp.dot(x, w1.T).astype(jnp.float32)
            b = jnp.dot(x, w3.T).astype(jnp.float32)
            h = (jax.nn.silu(a) * b).astype(x.dtype)
            return jnp.dot(h, w2.T)
        key = jax.random.key(seed)
        ks = jax.random.split(key, 8)
        B, S, D, I, E = (4, 256, 256, 176, 16)
        SI = I * 2
        sc = 0.02
        return {'x': jax.random.normal(ks[0], (B, S, D), jnp.bfloat16), 'gate_w': jax.random.normal(ks[1], (E, D), jnp.float32) * sc, 'w1': jax.random.normal(ks[2], (E, I, D), jnp.bfloat16) * sc, 'w2': jax.random.normal(ks[3], (E, D, I), jnp.bfloat16) * sc, 'w3': jax.random.normal(ks[4], (E, I, D), jnp.bfloat16) * sc, 'sw1': jax.random.normal(ks[5], (SI, D), jnp.bfloat16) * sc, 'sw2': jax.random.normal(ks[6], (D, SI), jnp.bfloat16) * sc, 'sw3': jax.random.normal(ks[7], (SI, D), jnp.bfloat16) * sc}
    _L2_ffn_in = _L2_ffn_setup()

    def _L3_attn_setup():
        import math
        import jax, jax.numpy as jnp
        import numpy as np
        B, S, H = (1, 256, 256)
        NH = 16
        DN = 128
        DR = 64
        DV = 128
        QL = 192
        KL = 64
        EPS = 1e-06
        ROPE_BASE = 10000.0

        def _rmsnorm(x, gamma, eps=EPS):
            return x * gamma * jax.lax.rsqrt(jnp.mean(x * x, axis=-1, keepdims=True) + eps)

        def _rope_tables(seq_len, dim, dtype):
            inv_freq = 1.0 / ROPE_BASE ** (jnp.arange(0, dim, 2, dtype=jnp.float32) / dim)
            ang = jnp.arange(seq_len, dtype=jnp.float32)[:, None] * inv_freq
            cos = jnp.concatenate([jnp.cos(ang)] * 2, axis=-1).astype(dtype)
            sin = jnp.concatenate([jnp.sin(ang)] * 2, axis=-1).astype(dtype)
            return (cos[None, :, None, :], sin[None, :, None, :])

        def _rotate_half(x):
            h = x.shape[-1] // 2
            return jnp.concatenate([-x[..., h:], x[..., :h]], axis=-1)
        key = jax.random.key(seed)
        ks = jax.random.split(key, 6)
        w = 0.02
        return {'hidden': jax.random.normal(ks[0], (B, S, H), jnp.float32), 'w_kv_a': jax.random.normal(ks[1], (H, QL + KL + DR), jnp.float32) * w, 'q_a_gamma': jnp.ones((QL,), jnp.float32), 'w_qb': jax.random.normal(ks[2], (QL, NH * (DN + DR)), jnp.float32) * w, 'kv_a_gamma': jnp.ones((KL,), jnp.float32), 'w_kvb': jax.random.normal(ks[3], (KL, NH * (DN + DV)), jnp.float32) * w, 'w_o': jax.random.normal(ks[4], (NH * DV, H), jnp.float32) * w}
    _L3_attn_in = _L3_attn_setup()

    def _L3_ffn_setup():
        import jax, jax.numpy as jnp
        import numpy as np
        H = 256
        key = jax.random.key(seed)
        ks = jax.random.split(key, 10)
        s = 1.0 / np.sqrt(H)
        x = jax.random.normal(ks[0], (4, 256, H), dtype=jnp.float32)
        Wg = jax.random.uniform(ks[1], (2, H), jnp.float32, -s, s)
        W0a = jax.random.uniform(ks[2], (2 * H, H), jnp.float32, -s, s)
        b0a = jax.random.uniform(ks[3], (2 * H,), jnp.float32, -s, s)
        W0b = jax.random.uniform(ks[4], (H, 2 * H), jnp.float32, -s, s)
        b0b = jax.random.uniform(ks[5], (H,), jnp.float32, -s, s)
        W1a = jax.random.uniform(ks[6], (2 * H, H), jnp.float32, -s, s)
        b1a = jax.random.uniform(ks[7], (2 * H,), jnp.float32, -s, s)
        W1b = jax.random.uniform(ks[8], (H, 2 * H), jnp.float32, -s, s)
        b1b = jax.random.uniform(ks[9], (H,), jnp.float32, -s, s)
        return {'x': x, 'Wg': Wg, 'W0a': W0a, 'b0a': b0a, 'W0b': W0b, 'b0b': b0b, 'W1a': W1a, 'b1a': b1a, 'W1b': W1b, 'b1b': b1b}
    _L3_ffn_in = _L3_ffn_setup()
    _d = {'L0_attn_x': _L0_attn_in['x'], 'L0_attn_W_x': _L0_attn_in['W_x'], 'L0_attn_W_dt': _L0_attn_in['W_dt'], 'L0_attn_b_dt': _L0_attn_in['b_dt'], 'L0_attn_A_log': _L0_attn_in['A_log'], 'L0_attn_D': _L0_attn_in['D'], 'L0_ffn_router_gate': _L0_ffn_in['router_gate'], 'L0_ffn_expert_gate_up': _L0_ffn_in['expert_gate_up'], 'L0_ffn_expert_down': _L0_ffn_in['expert_down'], 'L1_attn_w_qkv': _L1_attn_in['w_qkv'], 'L1_attn_w_gate': _L1_attn_in['w_gate'], 'L1_attn_w_beta': _L1_attn_in['w_beta'], 'L1_attn_w_alpha': _L1_attn_in['w_alpha'], 'L1_attn_log_A': _L1_attn_in['log_A'], 'L1_attn_dt_bias': _L1_attn_in['dt_bias'], 'L1_attn_conv_w': _L1_attn_in['conv_w'], 'L1_attn_rms_w': _L1_attn_in['rms_w'], 'L1_attn_w_out': _L1_attn_in['w_out'], 'L1_ffn_gate_W_packed': _L1_ffn_in['gate_W_packed'], 'L1_ffn_gate_scales': _L1_ffn_in['gate_scales'], 'L1_ffn_up_W_packed': _L1_ffn_in['up_W_packed'], 'L1_ffn_up_scales': _L1_ffn_in['up_scales'], 'L1_ffn_down_W_packed': _L1_ffn_in['down_W_packed'], 'L1_ffn_down_scales': _L1_ffn_in['down_scales'], 'L2_attn_Wq': _L2_attn_in['Wq'], 'L2_attn_bq': _L2_attn_in['bq'], 'L2_attn_Wk': _L2_attn_in['Wk'], 'L2_attn_bk': _L2_attn_in['bk'], 'L2_attn_Wv': _L2_attn_in['Wv'], 'L2_attn_bv': _L2_attn_in['bv'], 'L2_attn_Wo': _L2_attn_in['Wo'], 'L2_attn_bo': _L2_attn_in['bo'], 'L2_ffn_gate_w': _L2_ffn_in['gate_w'], 'L2_ffn_w1': _L2_ffn_in['w1'], 'L2_ffn_w2': _L2_ffn_in['w2'], 'L2_ffn_w3': _L2_ffn_in['w3'], 'L2_ffn_sw1': _L2_ffn_in['sw1'], 'L2_ffn_sw2': _L2_ffn_in['sw2'], 'L2_ffn_sw3': _L2_ffn_in['sw3'], 'L3_attn_w_kv_a': _L3_attn_in['w_kv_a'], 'L3_attn_q_a_gamma': _L3_attn_in['q_a_gamma'], 'L3_attn_w_qb': _L3_attn_in['w_qb'], 'L3_attn_kv_a_gamma': _L3_attn_in['kv_a_gamma'], 'L3_attn_w_kvb': _L3_attn_in['w_kvb'], 'L3_attn_w_o': _L3_attn_in['w_o'], 'L3_ffn_Wg': _L3_ffn_in['Wg'], 'L3_ffn_W0a': _L3_ffn_in['W0a'], 'L3_ffn_b0a': _L3_ffn_in['b0a'], 'L3_ffn_W0b': _L3_ffn_in['W0b'], 'L3_ffn_b0b': _L3_ffn_in['b0b'], 'L3_ffn_W1a': _L3_ffn_in['W1a'], 'L3_ffn_b1a': _L3_ffn_in['b1a'], 'L3_ffn_W1b': _L3_ffn_in['W1b'], 'L3_ffn_b1b': _L3_ffn_in['b1b']}
    _x0 = _d['L0_attn_x']
    _d['L0_attn_x'] = jax.random.normal(jax.random.fold_in(jax.random.key(seed), 1), (4, 512, 256), dtype=_x0.dtype)
    del _x0
    return _d

def reference(L0_attn_x, L0_attn_W_x, L0_attn_W_dt, L0_attn_b_dt, L0_attn_A_log, L0_attn_D, L0_ffn_router_gate, L0_ffn_expert_gate_up, L0_ffn_expert_down, L1_attn_w_qkv, L1_attn_w_gate, L1_attn_w_beta, L1_attn_w_alpha, L1_attn_log_A, L1_attn_dt_bias, L1_attn_conv_w, L1_attn_rms_w, L1_attn_w_out, L1_ffn_gate_W_packed, L1_ffn_gate_scales, L1_ffn_up_W_packed, L1_ffn_up_scales, L1_ffn_down_W_packed, L1_ffn_down_scales, L2_attn_Wq, L2_attn_bq, L2_attn_Wk, L2_attn_bk, L2_attn_Wv, L2_attn_bv, L2_attn_Wo, L2_attn_bo, L2_ffn_gate_w, L2_ffn_w1, L2_ffn_w2, L2_ffn_w3, L2_ffn_sw1, L2_ffn_sw2, L2_ffn_sw3, L3_attn_w_kv_a, L3_attn_q_a_gamma, L3_attn_w_qb, L3_attn_kv_a_gamma, L3_attn_w_kvb, L3_attn_w_o, L3_ffn_Wg, L3_ffn_W0a, L3_ffn_b0a, L3_ffn_W0b, L3_ffn_b0b, L3_ffn_W1a, L3_ffn_b1a, L3_ffn_W1b, L3_ffn_b1b):

    def _L0_attn_ref(x, W_x, W_dt, b_dt, A_log, D):
        import jax, jax.numpy as jnp
        import numpy as np
        B, L, D_INNER, N_STATE, DT_RANK = (2, 128, 256, 16, 64)
        R = W_dt.shape[1]
        N = A_log.shape[1]
        x_proj = x @ W_x.T
        dt_x, Bm, Cm = jnp.split(x_proj, [R, R + N], axis=-1)
        dt = jax.nn.softplus(dt_x @ W_dt.T + b_dt)
        A = -jnp.exp(A_log)
        dA = jnp.exp(jnp.einsum('bld,dn->bldn', dt, A))
        dBx = jnp.einsum('bld,bln,bld->bldn', dt, Bm, x)

        def step(h, inp):
            dA_t, dBx_t, C_t = inp
            h = dA_t * h + dBx_t
            y_t = jnp.einsum('bdn,bn->bd', h, C_t)
            return (h, y_t)
        h0 = jnp.zeros((x.shape[0], x.shape[2], N), dtype=jnp.float32)
        _, ys = jax.lax.scan(step, h0, (dA.swapaxes(0, 1), dBx.swapaxes(0, 1), Cm.swapaxes(0, 1)))
        y = ys.swapaxes(0, 1) + x * D
        return y

    def _L0_ffn_ref(hidden_states, router_gate, expert_gate_up, expert_down):
        import jax, jax.numpy as jnp
        import numpy as np
        NUM_EXPERTS = 8
        TOP_K = 2
        MODEL_DIM = 256
        INTER_DIM = 128
        GATE_SCALE = 1.0
        UP_SCALE = 0.0
        orig_shape = hidden_states.shape
        hs = hidden_states.reshape(-1, orig_shape[-1])
        T = hs.shape[0]
        logits = hs @ router_gate.T
        probs = jax.nn.softmax(logits.astype(jnp.float32), axis=-1)
        topk_scores, topk_idx = jax.lax.top_k(probs, TOP_K)
        topk_scores = topk_scores / jnp.sum(topk_scores, axis=-1, keepdims=True)
        scores_f = topk_scores.T.reshape(-1).astype(hs.dtype)
        ids_f = topk_idx.T.reshape(-1)
        order = jnp.argsort(ids_f)
        sorted_ids = ids_f[order]
        scores_sorted = scores_f[order]
        token_slots = order % T
        x = hs[token_slots]
        inter = jnp.zeros((x.shape[0], 2 * INTER_DIM), x.dtype)
        for e in range(NUM_EXPERTS):
            m = (sorted_ids == e)[:, None]
            inter = inter + jnp.where(m, x, 0) @ expert_gate_up[e]
        gate = inter[..., 0::2]
        up = inter[..., 1::2]
        h = (up + UP_SCALE) * jax.nn.silu(gate * GATE_SCALE)
        out_rows = jnp.zeros((x.shape[0], MODEL_DIM), x.dtype)
        for e in range(NUM_EXPERTS):
            m = (sorted_ids == e)[:, None]
            out_rows = out_rows + jnp.where(m, h, 0) @ expert_down[e]
        out = jnp.zeros_like(hs).at[token_slots].add(out_rows * scores_sorted[:, None])
        return out.reshape(orig_shape)

    def _L1_attn_ref(x, w_qkv, w_gate, w_beta, w_alpha, log_A, dt_bias, conv_w, rms_w, w_out):
        import jax, jax.numpy as jnp
        import numpy as np
        B, S, D_IN = (1, 128, 256)
        H_QK, H_V, DK, DV = (8, 16, 128, 128)
        KCONV = 4
        D_OUT = H_QK * DK
        D_OUT_VG = H_V * DV
        FUSED = 2 * D_OUT + D_OUT_VG
        EPS = 1e-06

        def l2_norm(t):
            return t / jnp.sqrt(jnp.sum(t * t, axis=-1, keepdims=True) + EPS)

        def rms_norm(t, w):
            var = jnp.mean(t * t, axis=-1, keepdims=True)
            return t * jax.lax.rsqrt(var + EPS) * w

        def gated_delta_rule(q, k, v, beta, alpha):
            q = q * q.shape[-1] ** (-0.5)
            S0 = jnp.zeros(q.shape[:2] + (q.shape[-1], v.shape[-1]), q.dtype)

            def step(Sm, inp):
                q_t, k_t, v_t, b_t, a_t = inp
                Sm = Sm * a_t[..., None, None]
                kv = jnp.einsum('bhk,bhkv->bhv', k_t, Sm)
                u = (v_t - kv) * b_t[..., None]
                Sm = Sm + k_t[..., None] * u[:, :, None, :]
                o = jnp.einsum('bhk,bhkv->bhv', q_t, Sm)
                return (Sm, o)
            xs = (jnp.moveaxis(q, 2, 0), jnp.moveaxis(k, 2, 0), jnp.moveaxis(v, 2, 0), jnp.moveaxis(beta, 2, 0), jnp.moveaxis(alpha, 2, 0))
            Sf, outs = jax.lax.scan(step, S0, xs)
            return (jnp.moveaxis(outs, 0, 2), Sf)
        b, seq_len, _ = x.shape
        fused_qkv = x @ w_qkv.T
        beta = jax.nn.sigmoid(x @ w_beta.T).transpose(0, 2, 1)
        token_projs = x @ w_alpha.T
        alpha = jnp.exp(-jnp.exp(log_A) * jax.nn.softplus(token_projs + dt_bias))
        alpha = alpha.transpose(0, 2, 1)
        conv_in = fused_qkv.transpose(0, 2, 1)
        conv_out = jax.lax.conv_general_dilated(conv_in, conv_w, window_strides=(1,), padding=[(KCONV - 1, 0)], dimension_numbers=('NCH', 'OIH', 'NCH'), feature_group_count=FUSED)
        fused_qkv = jax.nn.silu(conv_out).transpose(0, 2, 1)
        query = fused_qkv[..., :D_OUT].reshape(b, seq_len, H_QK, DK).transpose(0, 2, 1, 3)
        key = fused_qkv[..., D_OUT:2 * D_OUT].reshape(b, seq_len, H_QK, DK).transpose(0, 2, 1, 3)
        value = fused_qkv[..., 2 * D_OUT:].reshape(b, seq_len, H_V, DV).transpose(0, 2, 1, 3)
        query, key = (l2_norm(query), l2_norm(key))
        rep = H_V // H_QK
        if rep > 1:
            query = jnp.repeat(query, rep, axis=1)
            key = jnp.repeat(key, rep, axis=1)
        ctx, _ = gated_delta_rule(query, key, value, beta, alpha)
        ctx = rms_norm(ctx.astype(jnp.float32), rms_w)
        ctx = ctx.transpose(0, 2, 1, 3).reshape(b, seq_len, D_OUT_VG)
        gate = jax.nn.silu(x @ w_gate.T)
        return gate * ctx @ w_out.T

    def _L1_ffn_ref(x, gate_W_packed, gate_scales, up_W_packed, up_scales, down_W_packed, down_scales):
        import jax, jax.numpy as jnp
        import numpy as np
        BLOCK_SIZE = 32
        HIDDEN_SIZE = 256
        MLP_DIM = 2048
        NVFP4_LUT = jnp.array([0.0, 0.5, 1.0, 1.5, 2.0, 3.0, 4.0, 6.0, 0.0, -0.5, -1.0, -1.5, -2.0, -3.0, -4.0, -6.0], dtype=jnp.float32)

        def dequant_nvfp4(W_packed, scales, block=BLOCK_SIZE):
            N = W_packed.shape[0]
            low = W_packed & 15
            high = W_packed >> 4 & 15
            idx = jnp.stack([low, high], axis=-1).reshape(N, -1)
            vals = NVFP4_LUT[idx]
            K = vals.shape[1]
            vals = vals.reshape(N, K // block, block) * scales[:, :, None]
            return vals.reshape(N, K)
        B, S, H = x.shape
        xt = x.reshape(B * S, H)
        Wg = dequant_nvfp4(gate_W_packed, gate_scales)
        Wu = dequant_nvfp4(up_W_packed, up_scales)
        Wd = dequant_nvfp4(down_W_packed, down_scales)
        gate = jnp.einsum('th,nh->tn', xt, Wg)
        up = jnp.einsum('th,nh->tn', xt, Wu)
        gelu = jnp.tanh(0.7978845608028654 * (gate + 0.044715 * gate ** 3)) * gate * 0.5 + gate * 0.5
        inter = gelu * up
        out = jnp.einsum('tn,hn->th', inter, Wd)
        return out.reshape(B, S, H)

    def _L2_attn_ref(x, Wq, bq, Wk, bk, Wv, bv, Wo, bo):
        import jax, jax.numpy as jnp
        import numpy as np
        D_MODEL = 256
        N_HEADS = 16
        D_K = D_MODEL // N_HEADS
        EPS = 1e-06
        b, n, _ = x.shape
        h, d = (N_HEADS, D_K)

        def proj(W, bias):
            y = jnp.einsum('bnm,dm->bnd', x, W) + bias
            return y.reshape(b, n, h, d).transpose(0, 2, 1, 3)
        Q = jax.nn.relu(proj(Wq, bq))
        K = jax.nn.relu(proj(Wk, bk))
        V = proj(Wv, bv)
        pos = jnp.arange(n, dtype=x.dtype)
        decay = jnp.exp(-pos / n)[None, None, :, None]
        Q = Q * decay
        K = K * decay
        KV = jnp.einsum('bhnd,bhne->bhde', K, V)
        Ksum = K.sum(axis=2)
        Z = 1.0 / (jnp.einsum('bhnd,bhd->bhn', Q, Ksum)[..., None] + EPS)
        out = jnp.einsum('bhnd,bhde->bhne', Q, KV) * Z
        out = out.transpose(0, 2, 1, 3).reshape(b, n, h * d)
        return jnp.einsum('bnm,dm->bnd', out, Wo) + bo

    def _L2_ffn_ref(x, gate_w, w1, w2, w3, sw1, sw2, sw3):
        import jax, jax.numpy as jnp
        import numpy as np
        TOPK = 2

        def _mlp(x, w1, w2, w3):
            a = jnp.dot(x, w1.T).astype(jnp.float32)
            b = jnp.dot(x, w3.T).astype(jnp.float32)
            h = (jax.nn.silu(a) * b).astype(x.dtype)
            return jnp.dot(h, w2.T)
        B, S, D = x.shape
        E = gate_w.shape[0]
        xf = x.reshape(-1, D)
        T = xf.shape[0]
        scores = jax.nn.sigmoid(jnp.dot(xf.astype(jnp.float32), gate_w.T))
        topv, topi = jax.lax.top_k(scores, TOPK)
        topv = topv / topv.sum(axis=-1, keepdims=True)
        dw = jnp.zeros((T, E), jnp.float32).at[jnp.arange(T)[:, None], topi].add(topv)
        y0 = _mlp(xf, sw1, sw2, sw3).astype(jnp.float32)

        def step(y, ws):
            e1, e2, e3, we = ws
            out = _mlp(xf, e1, e2, e3).astype(jnp.float32)
            return (y + out * we[:, None], None)
        y, _ = jax.lax.scan(step, y0, (w1, w2, w3, dw.T))
        return y.astype(x.dtype).reshape(B, S, D)

    def _L3_attn_ref(hidden, w_kv_a, q_a_gamma, w_qb, kv_a_gamma, w_kvb, w_o):
        import math
        import jax, jax.numpy as jnp
        import numpy as np
        B, S, H = (1, 256, 256)
        NH = 16
        DN = 128
        DR = 64
        DV = 128
        QL = 192
        KL = 64
        EPS = 1e-06
        ROPE_BASE = 10000.0

        def _rmsnorm(x, gamma, eps=EPS):
            return x * gamma * jax.lax.rsqrt(jnp.mean(x * x, axis=-1, keepdims=True) + eps)

        def _rope_tables(seq_len, dim, dtype):
            inv_freq = 1.0 / ROPE_BASE ** (jnp.arange(0, dim, 2, dtype=jnp.float32) / dim)
            ang = jnp.arange(seq_len, dtype=jnp.float32)[:, None] * inv_freq
            cos = jnp.concatenate([jnp.cos(ang)] * 2, axis=-1).astype(dtype)
            sin = jnp.concatenate([jnp.sin(ang)] * 2, axis=-1).astype(dtype)
            return (cos[None, :, None, :], sin[None, :, None, :])

        def _rotate_half(x):
            h = x.shape[-1] // 2
            return jnp.concatenate([-x[..., h:], x[..., :h]], axis=-1)
        b, s, _ = hidden.shape
        fused = hidden @ w_kv_a
        q_c = fused[..., :QL]
        kv_c = fused[..., QL:QL + KL]
        k_pe = fused[..., QL + KL:]
        q = _rmsnorm(q_c, q_a_gamma) @ w_qb
        q = q.reshape(b, s, NH, DN + DR)
        q_nope, q_pe = (q[..., :DN], q[..., DN:])
        kv = _rmsnorm(kv_c, kv_a_gamma) @ w_kvb
        kv = kv.reshape(b, s, NH, DN + DV)
        k_nope, v = (kv[..., :DN], kv[..., DN:])
        cos, sin = _rope_tables(s, DR, hidden.dtype)
        q_pe = q_pe * cos + _rotate_half(q_pe) * sin
        k_pe = k_pe[:, :, None, :]
        k_pe = k_pe * cos + _rotate_half(k_pe) * sin
        q_full = jnp.concatenate([q_nope, q_pe], axis=-1)
        k_full = jnp.concatenate([k_nope, jnp.broadcast_to(k_pe, (b, s, NH, DR))], axis=-1)
        scale = 1.0 / math.sqrt(DN + DR)
        scores = jnp.einsum('bqhd,bkhd->bhqk', q_full, k_full) * scale
        pos = jnp.arange(s)
        causal = pos[:, None] >= pos[None, :]
        scores = jnp.where(causal[None, None], scores, jnp.asarray(-1e+30, scores.dtype))
        probs = jax.nn.softmax(scores, axis=-1)
        attn = jnp.einsum('bhqk,bkhd->bqhd', probs, v)
        return attn.reshape(b, s, NH * DV) @ w_o

    def _L3_ffn_ref(x, Wg, W0a, b0a, W0b, b0b, W1a, b1a, W1b, b1b):
        import jax, jax.numpy as jnp
        import numpy as np
        H = 256
        scores = jax.nn.softmax(jnp.einsum('bsh,eh->bse', x, Wg), axis=-1)
        top_expert = jnp.argmax(scores, axis=-1)
        h0 = jax.nn.gelu(jnp.einsum('bsh,fh->bsf', x, W0a) + b0a, approximate=False)
        out0 = jnp.einsum('bsf,hf->bsh', h0, W0b) + b0b
        h1 = jax.nn.relu(jnp.einsum('bsh,fh->bsf', x, W1a) + b1a)
        out1 = jnp.einsum('bsf,hf->bsh', h1, W1b) + b1b
        mask0 = (top_expert == 0).astype(x.dtype)[..., None]
        return out0 * mask0 + out1 * (1.0 - mask0)
    x = L0_attn_x
    xn = _layernorm(x, axis=-1)
    s = _L0_attn_ref(xn, L0_attn_W_x, L0_attn_W_dt, L0_attn_b_dt, L0_attn_A_log, L0_attn_D)
    g = _silu(_L0_ffn_ref(xn, L0_ffn_router_gate, L0_ffn_expert_gate_up, L0_ffn_expert_down))
    x = x + s * g
    xn = _layernorm(x, axis=-1)
    s = _L1_attn_ref(xn, L1_attn_w_qkv, L1_attn_w_gate, L1_attn_w_beta, L1_attn_w_alpha, L1_attn_log_A, L1_attn_dt_bias, L1_attn_conv_w, L1_attn_rms_w, L1_attn_w_out)
    g = _silu(_L1_ffn_ref(xn, L1_ffn_gate_W_packed, L1_ffn_gate_scales, L1_ffn_up_W_packed, L1_ffn_up_scales, L1_ffn_down_W_packed, L1_ffn_down_scales))
    x = x + s * g
    xn = _layernorm(x, axis=-1)
    s = _L2_attn_ref(xn, L2_attn_Wq, L2_attn_bq, L2_attn_Wk, L2_attn_bk, L2_attn_Wv, L2_attn_bv, L2_attn_Wo, L2_attn_bo)
    g = _silu(_L2_ffn_ref(xn, L2_ffn_gate_w, L2_ffn_w1, L2_ffn_w2, L2_ffn_w3, L2_ffn_sw1, L2_ffn_sw2, L2_ffn_sw3))
    x = x + s * g
    xn = _layernorm(x, axis=-1)
    s = _L3_attn_ref(xn, L3_attn_w_kv_a, L3_attn_q_a_gamma, L3_attn_w_qb, L3_attn_kv_a_gamma, L3_attn_w_kvb, L3_attn_w_o)
    g = _silu(_L3_ffn_ref(xn, L3_ffn_Wg, L3_ffn_W0a, L3_ffn_b0a, L3_ffn_W0b, L3_ffn_b0b, L3_ffn_W1a, L3_ffn_b1a, L3_ffn_W1b, L3_ffn_b1b))
    x = x + s * g
    return x

_drawn_inputs = setup_inputs


def setup_inputs(seed=0):
    import zlib

    import numpy as np

    out = dict(_drawn_inputs(seed))
    spreads = {'L0_attn_D': (1.0, 0.6),
     'L1_attn_dt_bias': (1.0, 0.6),
     'L1_attn_rms_w': (1.0, 0.2),
     'L2_attn_bq': (0.0, 0.8),
     'L2_attn_bk': (0.0, 0.8),
     'L2_attn_bv': (0.0, 0.8),
     'L2_attn_bo': (0.0, 0.8),
     'L3_attn_q_a_gamma': (1.0, 0.6),
     'L3_attn_kv_a_gamma': (1.0, 0.6)}
    factors = {'L0_attn_W_x': 8.0,
     'L0_attn_W_dt': 8.0,
     'L0_attn_b_dt': 8.0,
     'L0_attn_A_log': 8.0,
     'L0_ffn_router_gate': 8.0,
     'L0_ffn_expert_gate_up': 8.0,
     'L0_ffn_expert_down': 8.0,
     'L1_attn_w_alpha': 8.0,
     'L2_attn_Wq': 8.0,
     'L2_attn_Wk': 8.0,
     'L2_attn_Wv': 8.0,
     'L2_attn_Wo': 8.0,
     'L2_ffn_gate_w': 8.0,
     'L2_ffn_w1': 8.0,
     'L2_ffn_w2': 8.0,
     'L2_ffn_w3': 8.0,
     'L2_ffn_sw1': 8.0,
     'L2_ffn_sw2': 8.0,
     'L2_ffn_sw3': 8.0,
     'L3_attn_w_kv_a': 8.0,
     'L3_attn_w_qb': 8.0,
     'L3_attn_w_kvb': 8.0,
     'L3_attn_w_o': 8.0,
     'L3_ffn_Wg': 8.0,
     'L3_ffn_W0a': 8.0,
     'L3_ffn_b0a': 24.36,
     'L3_ffn_W0b': 8.0,
     'L3_ffn_b0b': 64.0,
     'L3_ffn_W1a': 8.0,
     'L3_ffn_b1a': 8.0,
     'L3_ffn_W1b': 8.0,
     'L3_ffn_b1b': 60.223}
    for name, (base, spread) in spreads.items():
        noise = np.random.default_rng([zlib.crc32(name.encode()), seed]).standard_normal(out[name].shape)
        drawn = base * np.exp(spread * noise) if base else spread * noise
        out[name] = jnp.asarray(drawn.astype(out[name].dtype))
    for name, factor in factors.items():
        out[name] = (out[name] * factor).astype(out[name].dtype)
    return out
```

```python
from contextlib import ExitStack

import concourse.bass as bass
from concourse import mybir
import numpy as np

F32 = mybir.dt.float32
BF16 = mybir.dt.bfloat16
I32 = mybir.dt.int32
ALU = mybir.AluOpType
ACT = mybir.ActivationFunctionType
AX_X = mybir.AxisListType.X

P = 128
B, S, D = 4, 512, 256
CH = S // P
NT = B * CH
K2 = D // P
LN_EPS = 1e-5


def ds(i, n):
    return bass.ds(i, n)


def signals(nc, ctx, prefix, names):
    return {n: ctx.enter_context(nc.semaphore(prefix + "_" + n)) for n in names.split()}


def end_of_iteration(nc, sig):
    nums = sorted(x.num for x in sig.values())
    while nums:
        n = 1
        while n < len(nums) and nums[n] == nums[0] + n:
            n += 1
        nc.gpsimd.sem_clear(range(nums[0], nums[0] + n))
        nums = nums[n:]
    nc.all_engine_barrier()


class Steps:

    def __init__(self, eng, sem):
        self.eng, self.sem, self.n = eng, sem, 0

    def mark(self, ins):
        ins.then_inc(self.sem, 1)
        self.n += 1
        return self.n

    def wait(self):
        self.eng.wait_ge(self.sem, self.n)

    def link(self, ins):
        self.mark(ins)
        self.wait()


def log1p_small(dve, st, e, h):
    st.link(dve.tensor_scalar(h, e, -0.25, None, ALU.mult))
    for c in (1.0 / 3.0, -0.5, 1.0):
        st.link(dve.scalar_tensor_tensor(out=h, in0=h, scalar=c, in1=e, op0=ALU.add, op1=ALU.mult))


def log1p_join(dve, st, e, w, ln_w, h):
    st.link(dve.scalar_tensor_tensor(out=w, in0=w, scalar=1.0, in1=e, op0=ALU.subtract, op1=ALU.subtract))
    st.link(dve.tensor_tensor(w, ln_w, w, ALU.subtract))
    st.link(dve.tensor_tensor(w, w, h, ALU.subtract))
    st.link(dve.scalar_tensor_tensor(out=w, in0=e, scalar=1.0 / 64.0, in1=w, op0=ALU.is_ge, op1=ALU.mult))
    st.link(dve.tensor_tensor(h, h, w, ALU.add))


def load(nc, sig, name, pairs):
    with nc.Block() as block:
        @block.sync
        def _(sp):
            for dst, src in pairs:
                sp.dma_start(dst, src).then_inc(sig[name], 16)
            sp.wait_ge(sig[name], 16 * len(pairs))
    end_of_iteration(nc, sig)


def bc(ap, dim, n):
    shape = list(ap.shape)
    return ap.unsqueeze(dim).to_broadcast(shape[:dim] + [n] + shape[dim:])


def layer_norm(nc, g):
    with ExitStack() as ctx:
        sb = lambda n, s, t=F32: ctx.enter_context(nc.sbuf_tensor("ln%d_" % g["layer"] + n, s, t))
        st, mv = sb("st", [P, CH, 6]), sb("mv", [P, CH, 2])
        std, rstd, r2, xn = sb("std", [P, CH]), sb("rstd", [P, CH]), sb("r2", [P, CH]), sb("xn", [P, CH, D])
        sig = g["ln_sig"]
        x, xn_fm, ident, ps, eps = g["x"], g["xn_fm"], g["ident"], g["ps"], g["eps"]
        with nc.Fori(0, B) as b:
            with nc.Block() as block:
                @block.vector
                def _(dve):
                    for t in range(CH):
                        dve.bn_stats(st[:, t, :], x[:, ds(b * CH + t, 1), :]).then_inc(sig["stats"], 1)
                    for t in range(CH):
                        dve.wait_ge(sig["stats"], t + 1)
                        dve.bn_aggr(mv[:, t, :], st[:, t, :]).then_inc(sig["meanvar"], 1)
                    dve.wait_ge(sig["std"], 1)
                    so = Steps(dve, sig["rstd"])
                    so.link(dve.reciprocal(rstd[:], std[:]))
                    so.link(dve.tensor_tensor(r2[:], rstd[:], rstd[:], ALU.mult))
                    so.link(dve.scalar_tensor_tensor(out=r2[:], in0=mv[:, :, 1], scalar=LN_EPS, in1=r2[:], op0=ALU.add, op1=ALU.mult))
                    so.link(dve.tensor_scalar(r2[:], r2[:], -0.5, 1.5, ALU.mult, ALU.add))
                    so.link(dve.tensor_tensor(rstd[:], rstd[:], r2[:], ALU.mult))
                    for t in range(CH):
                        dve.tensor_scalar(xn[:, t, :], x[:, ds(b * CH + t, 1), :].squeeze(1), mv[:, t, 0:1], rstd[:, t:t + 1],
                                          ALU.subtract, ALU.mult).then_inc(sig["xn"], 1)

                @block.tensor
                def _(pe):
                    for t in range(CH):
                        pe.wait_ge(sig["xn"], t + 1)
                        for k in range(K2):
                            last = pe.transpose(ps[k][:, t * P:(t + 1) * P], xn[:, t, k::2], ident[:])
                    last.then_inc(sig["turned"], 1)

                @block.scalar
                def _(act):
                    act.wait_ge(sig["meanvar"], CH)
                    act.activation(std[:], mv[:, :, 1], ACT.Sqrt, bias=eps[:, 0:1]).then_inc(sig["std"], 1)
                    act.wait_ge(sig["turned"], 1)
                    for k in range(K2):
                        act.activation(xn_fm[:, k, ds(b * S, S)], ps[k][:], ACT.Copy)
            end_of_iteration(nc, sig)


def gated_update(nc, g, acc, gate, b):
    sig, x, s = g["up_sig"], g["x"], g["s"]
    with nc.Block() as block:
        @block.scalar
        def _(act):
            act.activation(gate[:], acc[:], ACT.Silu).then_inc(sig["silu"], 1)

        @block.vector
        def _(dve):
            dve.wait_ge(sig["silu"], 1)
            dve.tensor_tensor(gate[:], gate[:], s[:, ds(b * CH, CH), :], ALU.mult).then_inc(sig["sg"], 1)
            dve.wait_ge(sig["sg"], 1)
            dve.tensor_tensor(x[:, ds(b * CH, CH), :], x[:, ds(b * CH, CH), :], gate[:], ALU.add)
    end_of_iteration(nc, sig)


def mamba(nc, g, d):
    NS, R = 16, 64
    M = R + 2 * NS
    with ExitStack() as ctx:
        sb = lambda n, s, t=F32: ctx.enter_context(nc.sbuf_tensor("ma_" + n, s, t))
        sig = signals(nc, ctx, "ma", "load xb xp_ps xp dt_ps az ez w lz rz dt u b_bc c_bc da dbx h hc y_used y yd turned order")
        wx, wdt = sb("wx", [P, K2, M]), sb("wdt", [R, K2, P])
        bdt, na, dp = sb("bdt", [P, K2]), sb("na", [P, K2, NS]), sb("dp", [P, K2])
        xb, xp, az, rz = sb("xb", [P, K2, S]), sb("xp", [M, S]), sb("az", [P, K2, S]), sb("rz", [P, K2, S])
        dt, u = sb("dt", [P, K2, S]), sb("u", [P, K2, S])
        da, dbx, h, hc = sb("da", [P, 4, S]), sb("dbx", [P, 2, S]), sb("h", [P, 2, S]), sb("hc", [P, 4, S])
        yd, wz, lz = sb("yd", [P, K2, S]), sb("wz", [P, K2, S]), sb("lz", [P, K2, S])
        ps, ident, xn_fm, s_out = g["ps"], g["ident"], g["xn_fm"], g["s"]
        load(nc, sig, "load", [(wx[:], d["ma_wx"]), (wdt[:], d["ma_wdt"]), (bdt[:], d["ma_bdt"]),
                               (na[:], d["ma_alog"]), (dp[:], d["ma_d"])])
        with nc.Block() as block:
            @block.scalar
            def _(act):
                act.activation(na[:], na[:], ACT.Exp).then_inc(sig["order"], 1)
                act.wait_ge(sig["order"], 1)
                act.mul(na[:], na[:], -1.0)
        end_of_iteration(nc, sig)
        y_ps = [ps[1], ps[2]]
        with nc.Fori(0, B) as b:
            with nc.Block() as block:
                @block.tensor
                def _(pe):
                    pe.wait_ge(sig["xb"], 1)
                    for k in range(K2):
                        last = pe.matmul(ps[0][0:M, :], wx[:, k, :], xb[:, k, :], start=(k == 0), stop=(k == K2 - 1))
                    last.then_inc(sig["xp_ps"], 1)
                    pe.wait_ge(sig["xp"], 1)
                    for k in range(K2):
                        pe.matmul(y_ps[k][:], wdt[:, k, :], xp[0:R, :], start=True, stop=True).then_inc(sig["dt_ps"], 1)

                    def reduce(n):
                        for k in range(K2):
                            i = K2 * n + k
                            pe.wait_ge(sig["hc"], i + 1)
                            if n == 0:
                                pe.wait_ge(sig["rz"], k + 1)
                            pe.matmul(y_ps[k][:], ident[:], hc[:, i % 4, :], start=(n == 0), stop=(n == NS - 1)
                                      ).then_inc(sig["y_used"], 1)

                    for n in range(NS):
                        if n >= 2:
                            pe.wait_ge(sig["hc"], K2 * (n - 1))
                        for what, row, bank in (("b_bc", R, 3), ("c_bc", R + NS, 5)):
                            pe.matmul(ps[bank + n % 2][:], ident[0:M, row + n:row + n + 1].to_broadcast([M, P]), xp[:],
                                      start=True, stop=True).then_inc(sig[what], 1)
                        if n >= 1:
                            reduce(n - 1)
                    reduce(NS - 1)
                    for k in range(K2):
                        pe.wait_ge(sig["yd"], k + 1)
                        for t in range(CH):
                            last = pe.transpose(ps[3 + k][:, t * P:(t + 1) * P], yd[:, k, t * P:(t + 1) * P], ident[:])
                        last.then_inc(sig["turned"], 1)

                @block.scalar
                def _(act):
                    act.activation(xb[:], xn_fm[:, :, ds(b * S, S)], ACT.Copy).then_inc(sig["xb"], 1)
                    act.wait_ge(sig["xp_ps"], 1)
                    act.activation(xp[:], ps[0][0:M, :], ACT.Copy).then_inc(sig["xp"], 1)
                    for k in range(K2):
                        act.wait_ge(sig["dt_ps"], k + 1)
                        act.activation(az[:, k, :], y_ps[k][:], ACT.Abs, bias=bdt[:, k:k + 1]).then_inc(sig["az"], 1)
                        act.wait_ge(sig["az"], k + 1)
                        act.activation(az[:, k, :], az[:, k, :], ACT.Exp, scale=-1.0).then_inc(sig["ez"], 1)
                        act.wait_ge(sig["w"], k + 1)
                        act.activation(lz[:, k, :], wz[:, k, :], ACT.Ln).then_inc(sig["lz"], 1)
                    for i in range(K2 * NS):
                        n, k = i // K2, i % K2
                        if n == 0:
                            act.wait_ge(sig["dt"], k + 1)
                        if i >= 4:
                            act.wait_ge(sig["h"], i - 3)
                        act.activation(da[:, i % 4, :], dt[:, k, :], ACT.Exp, scale=na[:, k, n:n + 1]).then_inc(sig["da"], 1)
                    for k in range(K2):
                        act.wait_ge(sig["turned"], k + 1)
                        act.activation(s_out[:, ds(b * CH, CH), k::2],
                                       ps[3 + k][:].rearrange("p (t f) -> p t f", t=CH), ACT.Copy)

                @block.vector
                def _(dve):
                    st = Steps(dve, sig["order"])
                    for k in range(K2):
                        dve.wait_ge(sig["az"], k + 1)
                        dve.tensor_scalar(rz[:, k, :], y_ps[k][:], bdt[:, k:k + 1], 0.0, ALU.add, ALU.max).then_inc(sig["rz"], 1)
                        dve.wait_ge(sig["ez"], k + 1)
                        dve.tensor_scalar(wz[:, k, :], az[:, k, :], 1.0, None, ALU.add).then_inc(sig["w"], 1)
                        dve.wait_ge(sig["w"], k + 1)
                        log1p_small(dve, st, az[:, k, :], dt[:, k, :])
                    for k in range(K2):
                        dve.wait_ge(sig["lz"], k + 1)
                        log1p_join(dve, st, az[:, k, :], wz[:, k, :], lz[:, k, :], dt[:, k, :])
                        dve.tensor_tensor(dt[:, k, :], dt[:, k, :], rz[:, k, :], ALU.add).then_inc(sig["dt"], 1)
                    dve.wait_ge(sig["xb"], 1)
                    for k in range(K2):
                        dve.wait_ge(sig["dt"], k + 1)
                        dve.tensor_tensor(u[:, k, :], dt[:, k, :], xb[:, k, :], ALU.mult).then_inc(sig["u"], 1)

                    def drive(i):
                        n, k = i // K2, i % K2
                        dve.wait_ge(sig["b_bc"], n + 1)
                        if n == 0:
                            dve.wait_ge(sig["u"], k + 1)
                        if i >= 2:
                            dve.wait_ge(sig["h"], i - 1)
                        dve.tensor_tensor(dbx[:, i % 2, :], u[:, k, :], ps[3 + n % 2][:], ALU.mult).then_inc(sig["dbx"], 1)

                    def read_out(i):
                        n = i // K2
                        dve.wait_ge(sig["c_bc"], n + 1)
                        dve.wait_ge(sig["h"], i + 1)
                        if i >= 4:
                            dve.wait_ge(sig["y_used"], i - 3)
                        dve.tensor_tensor(hc[:, i % 4, :], h[:, i % 2, :], ps[5 + n % 2][:], ALU.mult).then_inc(sig["hc"], 1)

                    for i in range(K2 * NS):
                        drive(i)
                        if i >= 1:
                            read_out(i - 1)
                        dve.wait_ge(sig["da"], i + 1)
                        dve.wait_ge(sig["dbx"], i + 1)
                        if i >= 2:
                            dve.wait_ge(sig["hc"], i - 1)
                        dve.tensor_tensor_scan(h[:, i % 2, :], da[:, i % 4, :], dbx[:, i % 2, :], 0.0, ALU.mult, ALU.add
                                               ).then_inc(sig["h"], 1)
                    read_out(K2 * NS - 1)
                    for k in range(K2):
                        dve.wait_ge(sig["y_used"], K2 * (NS - 1) + k + 1)
                        dve.scalar_tensor_tensor(out=yd[:, k, :], in0=xb[:, k, :], scalar=dp[:, k:k + 1], in1=y_ps[k][:],
                                                 op0=ALU.mult, op1=ALU.add).then_inc(sig["yd"], 1)
            end_of_iteration(nc, sig)


def experts(nc, g, d, name, E, MT, M, shared, exact_parts):
    NE = E + shared
    W = 16 if E == 8 else 24
    with ExitStack() as ctx:
        sb = lambda n, s, t=F32: ctx.enter_context(nc.sbuf_tensor(name + "_" + n, s, t))
        sig = signals(nc, ctx, name, "load xb part lg top neg score w a b act h down acc order")
        NP = 3 if exact_parts else 1
        wt = BF16 if exact_parts else F32
        router = sb("router", [P, K2, E])
        w13 = sb("w13", [P, NE, K2, 2, MT * M], wt)
        w2 = sb("w2", [M, NE * MT, D])
        xb = sb("xb", [P, K2, S])
        part = sb("part", [P, 3, K2, S], BF16) if exact_parts else None
        rest = sb("rest", [P, K2, S]) if exact_parts else None
        vals, rep, mr = sb("vals", [P, CH, W]), sb("rep", [P, CH, 8]), sb("mr", [P, CH, W])
        m8, nm, ssum = sb("m8", [P, CH, 8]), sb("nm", [P, CH]), sb("ssum", [P, CH])
        w = sb("w", [P, CH, NE])
        sg, h = sb("sg", [M, 2, S]), sb("h", [M, 2, S])
        acc, gate = sb("acc", [P, CH, D]), sb("gate", [P, CH, D])
        ps, xn_fm = g["ps"], g["xn_fm"]
        srcs = [(router[:], d[name + "_router"]), (w13[:], d[name + "_w13"])]
        if exact_parts:
            with ExitStack() as c2:
                w2h = c2.enter_context(nc.sbuf_tensor(name + "_w2h", [M, NE * MT, D], BF16))
                load(nc, sig, "load", srcs + [(w2h[:], d[name + "_w2"])])
                with nc.Block() as block:
                    @block.gpsimd
                    def _(pool):
                        half = NE * MT // 2
                        pool.tensor_copy(w2[:, 0:half, :], w2h[:, 0:half, :])

                    @block.vector
                    def _(dve):
                        half = NE * MT // 2
                        dve.tensor_copy(w2[:, half:, :], w2h[:, half:, :])
                end_of_iteration(nc, sig)
        else:
            load(nc, sig, "load", srcs + [(w2[:], d[name + "_w2"])])
        with nc.Block() as block:
            @block.vector
            def _(dve):
                dve.memset(vals[:], -1.0)
                dve.memset(rep[:], -1.0)
                dve.memset(w[:], 1.0)
        end_of_iteration(nc, sig)
        NU = NE * MT
        with nc.Fori(0, B) as b:
            with nc.Block() as block:
                @block.tensor
                def _(pe):
                    pe.wait_ge(sig["xb"], 1)
                    for t in range(CH):
                        for k in range(K2):
                            last = pe.matmul(ps[7][:, t * E:(t + 1) * E], xb[:, k, t * P:(t + 1) * P], router[:, k, :],
                                             start=(k == 0), stop=(k == K2 - 1))
                    last.then_inc(sig["lg"], 1)

                    def up(u):
                        e, m = u // MT, u % MT
                        if u >= 2:
                            pe.wait_ge(sig["h"], u - 1)
                        for n, what in ((0, "a"), (1, "b")):
                            out = ps[2 * (u % 2) + n][0:M, :]
                            if exact_parts:
                                if u == 0 and n == 0:
                                    pe.wait_ge(sig["part"], 3)
                                terms = [(w13[:, e, k, n, m * M:(m + 1) * M], part[:, q, k, :]) for q in (2, 1, 0) for k in range(K2)]
                            else:
                                terms = [(w13[:, e, k, n, m * M:(m + 1) * M], xb[:, k, :]) for k in range(K2)]
                            for q, (l, r) in enumerate(terms):
                                last = pe.matmul(out, l, r, start=(q == 0), stop=(q == len(terms) - 1))
                            last.then_inc(sig[what], 1)

                    def down(u):
                        e, m = u // MT, u % MT
                        pe.wait_ge(sig["h"], u + 1)
                        if m == 0 and e >= 2:
                            pe.wait_ge(sig["acc"], CH * (e - 1))
                        if m == 0 and e == 1:
                            pe.wait_ge(sig["w"], CH)
                        for t in range(CH):
                            last = pe.matmul(ps[4 + 2 * (e % 2) + t // 2][:, (t % 2) * D:(t % 2 + 1) * D],
                                             h[:, u % 2, t * P:(t + 1) * P], w2[:, u, :],
                                             start=(m == 0 and t % 2 == 0), stop=(m == MT - 1), skip_group_check=True)
                        last.then_inc(sig["down"], 1)

                    for u in range(NU):
                        up(u)
                        if u >= 1:
                            down(u - 1)
                    down(NU - 1)

                @block.scalar
                def _(act):
                    act.activation(xb[:], xn_fm[:, :, ds(b * S, S)], ACT.Copy).then_inc(sig["xb"], 1)
                    if shared:
                        act.wait_ge(sig["lg"], 1)
                        act.activation(vals[:, :, 0:E], ps[7][:, 0:CH * E].rearrange("p (t e) -> p t e", t=CH), ACT.Sigmoid
                                       ).then_inc(sig["score"], 1)
                    else:
                        act.wait_ge(sig["neg"], 1)
                        for t in range(CH):
                            act.activation(vals[:, t, 0:E], ps[7][:, t * E:(t + 1) * E], ACT.Exp, bias=nm[:, t:t + 1]
                                           ).then_inc(sig["score"], 1)
                    for u in range(NU):
                        act.wait_ge(sig["a"], u + 1)
                        if u >= 2:
                            act.wait_ge(sig["h"], u - 1)
                        act.activation(sg[:, u % 2, :], ps[2 * (u % 2)][0:M, :], ACT.Silu).then_inc(sig["act"], 1)

                @block.vector
                def _(dve):
                    st = Steps(dve, sig["order"])
                    if exact_parts:
                        dve.wait_ge(sig["xb"], 1)
                        for q in range(3):
                            src = xb if q == 0 else rest
                            dve.tensor_copy(part[:, q, :, :], src[:]).then_inc(sig["part"], 1)
                            if q < 2:
                                dve.wait_ge(sig["part"], q + 1)
                                st.link(dve.tensor_tensor(rest[:], src[:], part[:, q, :, :], ALU.subtract))
                    else:
                        dve.wait_ge(sig["lg"], 1)
                        for t in range(CH):
                            dve.max(m8[:, t, :], ps[7][:, t * E:(t + 1) * E]).then_inc(sig["top"], 1)
                        dve.wait_ge(sig["top"], CH)
                        dve.tensor_scalar(nm[:], m8[:, :, 0], -1.0, None, ALU.mult).then_inc(sig["neg"], 1)
                    dve.wait_ge(sig["score"], 1 if shared else CH)
                    if not shared:
                        dve.wait_ge(sig["neg"], 1)
                    for t in range(CH):
                        last = dve.max(m8[:, t, :], vals[:, t, 0:E])
                    st.link(last)
                    st.mark(dve.tensor_copy(rep[:, :, 0:2], m8[:, :, 0:2]))
                    st.link(dve.tensor_tensor(ssum[:], m8[:, :, 0], m8[:, :, 1], ALU.add))
                    st.link(dve.reciprocal(ssum[:], ssum[:]))
                    for t in range(CH):
                        last = dve.match_replace(out=mr[:, t, :], in_to_replace=rep[:, t, :], in_values=vals[:, t, :], imm_value=-2.0)
                    st.link(last)
                    for t in range(CH):
                        st.mark(dve.scalar_tensor_tensor(out=mr[:, t, 0:E], in0=mr[:, t, 0:E], scalar=-1.5, in1=vals[:, t, 0:E],
                                                         op0=ALU.is_lt, op1=ALU.mult))
                    st.wait()
                    for t in range(CH):
                        dve.tensor_scalar(w[:, t, 0:E], mr[:, t, 0:E], ssum[:, t:t + 1], None, ALU.mult).then_inc(sig["w"], 1)
                    dve.wait_ge(sig["w"], CH)

                    def add(e):
                        dve.wait_ge(sig["down"], MT * (e + 1))
                        for t in range(CH):
                            y = ps[4 + 2 * (e % 2) + t // 2][:, (t % 2) * D:(t % 2 + 1) * D]
                            if e == 0:
                                dve.tensor_scalar(acc[:, t, :], y, w[:, t, 0:1], None, ALU.mult).then_inc(sig["acc"], 1)
                            else:
                                dve.wait_ge(sig["acc"], CH * (e - 1) + t + 1)
                                dve.scalar_tensor_tensor(out=acc[:, t, :], in0=y, scalar=w[:, t, e:e + 1], in1=acc[:, t, :],
                                                         op0=ALU.mult, op1=ALU.add).then_inc(sig["acc"], 1)

                    for u in range(NU):
                        dve.wait_ge(sig["act"], u + 1)
                        dve.wait_ge(sig["b"], u + 1)
                        if u >= 2:
                            dve.wait_ge(sig["down"], u - 1)
                        dve.tensor_tensor(h[:, u % 2, :], sg[:, u % 2, :], ps[2 * (u % 2) + 1][0:M, :], ALU.mult
                                          ).then_inc(sig["h"], 1)
                        if u >= 1 and u % MT == 0:
                            add(u // MT - 1)
                    add(NE - 1)
            end_of_iteration(nc, sig)
            gated_update(nc, g, acc, gate, b)


def delta_rule(nc, g, d):
    HV, HG, KG = 16, 4, 2
    NG = HV // HG
    CT = 2 * KG + HG
    LEAST = float(np.exp(-30.0))
    LV = 7
    with ExitStack() as ctx:
        sb = lambda n, s, t=F32: ctx.enter_context(nc.sbuf_tensor("dr_" + n, s, t))
        pre = signals(nc, ctx, "dp", "load xb z az ez w lz r sp be order")
        sig = signals(nc, ctx, "dr", "wnext xb proj tap0 conv silu gate sq ss rn norm kt_ps kt vt_ps vt lam d_ps kk_ps e_row g l0 a0 "
                                     "dcol l a kg w_ps w xy_ps xy ks r u_ps u o_ps o osq oss orn o3 kd dst s y_ps y order porder")
        wba, wq, cw = sb("wba", [P, K2, 2 * HV]), sb("wq", [P, K2, CT * P]), sb("cw", [P, CT, 4])
        wg, wo = sb("wg", [P, K2, HG * P]), sb("wo", [P, HG, D])
        na, dtb, rw = sb("na", [P, HV]), sb("dtb", [P, HV]), sb("rw", [P, 1])
        tri, low, lmask = sb("tri", [P, P]), sb("low", [P, P]), sb("lmask", [P, LV, P])
        la_all, be_all = sb("la_all", [P, B * NG, CH * HG]), sb("be_all", [P, B * NG, CH * HG])
        la, be, nb = sb("la", [P, CH * HG]), sb("be", [P, CH * HG]), sb("nb", [P, CH * HG])
        qb = sb("qb", [P, 1])
        xb = sb("xb", [P, K2, S])
        with ExitStack() as c2:
            tb = lambda n, s, t=F32: c2.enter_context(nc.sbuf_tensor("dp_" + n, s, t))
            z, az, w, r = (tb(n, [P, CH, 2 * HV]) for n in ("z", "az", "w", "r"))
            lp = tb("lp", [P, CH, HV])
            ps, xn_fm, s_out, ident, ones = g["ps"], g["xn_fm"], g["s"], g["ident"], g["ones"]
            load(nc, pre, "load", [(wba[:], d["dr_wba"]), (na[:], d["dr_loga"].partition_broadcast(P)),
                                   (dtb[:], d["dr_dtb"].partition_broadcast(P)), (rw[:], d["dr_rms"]),
                                   (tri[:], d["c_tri"]), (low[:], d["c_low"]), (lmask[:], d["c_lmask"]),
                                   (wq[:], d["dr_wq"][0]), (cw[:], d["dr_cw"][0]), (wg[:], d["dr_wg"][0]), (wo[:], d["dr_wo"][0])])
            with nc.Block() as block:
                @block.scalar
                def _(act):
                    act.activation(na[:], na[:], ACT.Exp).then_inc(pre["order"], 1)
                    act.wait_ge(pre["order"], 1)
                    act.mul(na[:], na[:], -1.0)

                @block.vector
                def _(dve):
                    dve.memset(qb[:], float(-0.5 * np.log(128.0)))
            end_of_iteration(nc, pre)
            with nc.Fori(0, B) as b:
                with nc.Block() as block:
                    @block.scalar
                    def _(act):
                        act.activation(xb[:], xn_fm[:, :, ds(b * S, S)], ACT.Copy).then_inc(pre["xb"], 1)
                        act.wait_ge(pre["z"], 1)
                        act.activation(az[:, :, 0:HV], z[:, :, 0:HV], ACT.Exp, scale=-1.0).then_inc(pre["az"], 1)
                        act.activation(az[:, :, HV:], z[:, :, HV:], ACT.Abs).then_inc(pre["az"], 1)
                        act.wait_ge(pre["az"], 2)
                        act.activation(az[:, :, HV:], az[:, :, HV:], ACT.Exp, scale=-1.0).then_inc(pre["ez"], 1)
                        act.wait_ge(pre["w"], 1)
                        act.activation(z[:, :, HV:], w[:, :, HV:], ACT.Ln).then_inc(pre["lz"], 1)

                    @block.tensor
                    def _(pe):
                        pe.wait_ge(pre["xb"], 1)
                        for t in range(CH):
                            for k in range(K2):
                                last = pe.matmul(ps[0][:, t * 2 * HV:(t + 1) * 2 * HV], xb[:, k, t * P:(t + 1) * P], wba[:, k, :],
                                                 start=(k == 0), stop=(k == K2 - 1))
                        last.then_inc(pre["sp"], 1)

                    @block.vector
                    def _(dve):
                        st = Steps(dve, pre["order"])
                        dve.wait_ge(pre["sp"], 1)
                        zp = ps[0][:, 0:CH * 2 * HV].rearrange("p (t f) -> p t f", t=CH)
                        st.mark(dve.tensor_copy(z[:, :, 0:HV], zp[:, :, 0:HV]))
                        dve.tensor_tensor(z[:, :, HV:], zp[:, :, HV:], bc(dtb[:], 1, CH), ALU.add).then_inc(pre["z"], 1)
                        dve.wait_ge(pre["z"], 1)
                        dve.tensor_scalar(r[:, :, HV:], z[:, :, HV:], 0.0, None, ALU.max).then_inc(pre["r"], 1)
                        dve.wait_ge(pre["ez"], 1)
                        dve.tensor_scalar(w[:], az[:], 1.0, None, ALU.add).then_inc(pre["w"], 1)
                        dve.wait_ge(pre["w"], 1)
                        st.mark(dve.reciprocal(r[:, :, 0:HV], w[:, :, 0:HV]))
                        log1p_small(dve, st, az[:, :, HV:], lp[:])
                        dve.wait_ge(pre["lz"], 1)
                        log1p_join(dve, st, az[:, :, HV:], w[:, :, HV:], z[:, :, HV:], lp[:])
                        st.link(dve.tensor_tensor(r[:, :, HV:], r[:, :, HV:], lp[:], ALU.add))
                        for n in range(NG):
                            h0 = n * HG
                            dve.tensor_copy(be_all[:, ds(b * NG + n, 1), :].squeeze(1).rearrange("p (c h) -> p c h", h=HG),
                                            r[:, :, h0:h0 + HG])
                            dve.tensor_tensor(la_all[:, ds(b * NG + n, 1), :].squeeze(1).rearrange("p (c h) -> p c h", h=HG),
                                              r[:, :, HV + h0:HV + h0 + HG], bc(na[:, h0:h0 + HG], 1, CH), ALU.mult)
                end_of_iteration(nc, pre)
        with nc.Block() as block:
            @block.vector
            def _(dve):
                dve.memset(s_out[:], 0.0)
        end_of_iteration(nc, pre)

        qkv, gt = sb("qkv", [P, CT, S]), sb("gt", [P, HG, S])
        sq = sb("sq", [P, 2, S])
        ktok, vtok = sb("ktok", [P, CH, KG, P]), sb("vtok", [P, CH, HG, P])
        lam = sb("lam", [P, 2, HG, P])
        L, A, G = (sb(n, [P, 2, HG, P]) for n in ("L", "A", "G"))
        X, Y, W = (sb(n, [P, 2, HG, P]) for n in ("X", "Y", "W"))
        kg, qg = sb("kg", [P, 2, HG, P]), sb("qg", [P, 2, HG, P])
        dcol = sb("dcol", [P, CH, HG])
        R, U, kd, state = (sb(n, [P, HG, P]) for n in ("R", "U", "kd", "state"))
        o, osq = sb("o", [P, HG, P]), sb("osq", [P, HG * P])
        eps = g["eps6"]
        h4 = lambda ap: ap.rearrange("p (h n) -> p h n", h=HG)
        flat = lambda ap: ap.rearrange("p h n -> p (h n)")
        NQ = 2 * LV

        with nc.Fori(0, B) as b:
            with nc.Fori(0, NG) as gi:
                with nc.Block() as block:
                    @block.sync
                    def _(sp):
                        sp.wait_ge(sig["proj"], CT + HG)
                        sp.dma_start(wq[:], d["dr_wq"][ds(gi + 1, 1)].squeeze(0)).then_inc(sig["wnext"], 16)
                        sp.dma_start(wg[:], d["dr_wg"][ds(gi + 1, 1)].squeeze(0)).then_inc(sig["wnext"], 16)
                        sp.wait_ge(sig["conv"], CT)
                        sp.dma_start(cw[:], d["dr_cw"][ds(gi + 1, 1)].squeeze(0)).then_inc(sig["wnext"], 16)
                        sp.wait_ge(sig["y_ps"], CH)
                        sp.dma_start(wo[:], d["dr_wo"][ds(gi + 1, 1)].squeeze(0)).then_inc(sig["wnext"], 16)
                        sp.wait_ge(sig["wnext"], 64)

                    @block.tensor
                    def _(pe):
                        pe.wait_ge(sig["xb"], 1)
                        for i in range(CT + HG):
                            if i >= 4:
                                if i - 4 < CT:
                                    pe.wait_ge(sig["conv"], i - 3)
                                else:
                                    pe.wait_ge(sig["gate"], i - 3 - CT)
                            for k in range(K2):
                                w_ = wq[:, k, i * P:(i + 1) * P] if i < CT else wg[:, k, (i - CT) * P:(i - CT + 1) * P]
                                last = pe.matmul(ps[i % 4][:], w_, xb[:, k, :], start=(k == 0), stop=(k == K2 - 1))
                            last.then_inc(sig["proj"], 1)
                        for i in range(2 * KG):
                            pe.wait_ge(sig["sq"], i + 1)
                            if i >= 2:
                                pe.wait_ge(sig["norm"], i - 1)
                            pe.matmul(ps[4 + i % 2][:], ones[:], sq[:, i % 2, :], start=True, stop=True).then_inc(sig["ss"], 1)
                        for c in range(CH):
                            pe.wait_ge(sig["silu"], CT)
                            if c >= 2:
                                pe.wait_ge(sig["vt"], c - 1)
                            for h in range(HG):
                                last = pe.transpose(ps[6 + c % 2][:, h * P:(h + 1) * P], qkv[:, 2 * KG + h, c * P:(c + 1) * P], ident[:])
                            last.then_inc(sig["vt_ps"], 1)
                        for c in range(CH):
                            pe.wait_ge(sig["norm"], 2 * KG)
                            if c >= 2:
                                pe.wait_ge(sig["kt"], c - 1)
                            for h in range(KG):
                                last = pe.transpose(ps[4 + c % 2][:, h * P:(h + 1) * P], qkv[:, KG + h, c * P:(c + 1) * P], ident[:])
                            last.then_inc(sig["kt_ps"], 1)

                        def build(c):
                            j = c % 2
                            pe.wait_ge(sig["lam"], c + 1)
                            if c < 2:
                                pe.wait_ge(sig["gate"], HG)
                                pe.wait_ge(sig["kt"], CH)
                                pe.wait_ge(sig["vt"], CH)
                            else:
                                pe.wait_ge(sig["y"], 2)
                            lc = flat(lam[:, j])
                            pe.matmul(ps[j][:], low[:], lc, start=True, stop=True)
                            for h in range(HG):
                                pe.matmul(ps[2 + j][:, h * P:(h + 1) * P], lam[:, j, h, :], low[:], start=True, stop=True)
                            pe.matmul(ps[4 + j][:], ones[:], lc, start=True, stop=True).then_inc(sig["d_ps"], 1)
                            cc = slice(c * P, (c + 1) * P)
                            for h in range(KG):
                                pe.matmul(ps[6 + j][:, h * P:(h + 1) * P], qkv[:, KG + h, cc], qkv[:, KG + h, cc], start=True, stop=True)
                                last = pe.matmul(ps[6 + j][:, (KG + h) * P:(KG + h + 1) * P], qkv[:, KG + h, cc], qkv[:, h, cc],
                                                 start=True, stop=True)
                            last.then_inc(sig["kk_ps"], 1)

                        def inverse(pair):
                            for s in range(LV):
                                for j in range(2):
                                    n = pair * NQ + 2 * s + j
                                    if s == 0:
                                        pe.wait_ge(sig["l"], 2 * pair + j + 1)
                                        pe.wait_ge(sig["e_row"], 2 * pair + j + 1)
                                    else:
                                        pe.wait_ge(sig["xy"], n - 1)
                                    for h in range(HG):
                                        last = pe.matmul(ps[j][:, h * P:(h + 1) * P], L[:, j, h, :],
                                                         ident[:] if s == 0 else Y[:, j, h, :], start=True, stop=True)
                                    last.then_inc(sig["w_ps"], 1)
                                for j in range(2):
                                    n = pair * NQ + 2 * s + j
                                    pe.wait_ge(sig["w"], n + 1)
                                    for h in range(HG):
                                        last = pe.matmul(ps[2 + j][:, h * P:(h + 1) * P], ident[:] if s == 0 else X[:, j, h, :],
                                                         W[:, j, h, :], start=True, stop=True)
                                    if s < LV - 1:
                                        for h in range(HG):
                                            last = pe.matmul(ps[4 + j][:, h * P:(h + 1) * P], W[:, j, h, :],
                                                             ident[:] if s == 0 else X[:, j, h, :], start=True, stop=True)
                                    last.then_inc(sig["xy_ps"], 1)

                        def recur(c):
                            j = c % 2
                            pe.wait_ge(sig["kg"], c + 1)
                            pe.wait_ge(sig["s"], c + 1)
                            if j == 0:
                                pe.wait_ge(sig["a"], c + 2)
                            else:
                                pe.wait_ge(sig["r"], c)
                            for h in range(HG):
                                last = pe.matmul(ps[6][:, h * P:(h + 1) * P], kg[:, j, h, :], state[:, h, :], start=True, stop=True)
                            last.then_inc(sig["ks"], 1)
                            pe.wait_ge(sig["r"], c + 1)
                            pe.wait_ge(sig["xy"], (c // 2) * NQ + NQ - 1 + j)
                            for h in range(HG):
                                last = pe.matmul(ps[7][:, h * P:(h + 1) * P], Y[:, j, h, :], R[:, h, :], start=True, stop=True)
                            last.then_inc(sig["u_ps"], 1)
                            pe.wait_ge(sig["u"], c + 1)
                            if j == 0:
                                pe.wait_ge(sig["xy"], (c // 2 + 1) * NQ)
                            else:
                                pe.wait_ge(sig["osq"], c)
                            for h in range(HG):
                                pe.matmul(ps[0][:, h * P:(h + 1) * P], state[:, h, :], qg[:, j, h, :], start=True, stop=False)
                                last = pe.matmul(ps[0][:, h * P:(h + 1) * P], U[:, h, :], A[:, j, h, :], start=False, stop=True)
                            last.then_inc(sig["o_ps"], 1)
                            pe.wait_ge(sig["kd"], c + 1)
                            for h in range(HG):
                                last = pe.matmul(ps[1][:, h * P:(h + 1) * P], kd[:, h, :], U[:, h, :], start=True, stop=True)
                            last.then_inc(sig["dst"], 1)
                            pe.wait_ge(sig["osq"], c + 1)
                            if j == 1:
                                pe.wait_ge(sig["orn"], c)
                                pe.wait_ge(sig["o3"], c)
                            pe.matmul(ps[2][:], ones[:], osq[:], start=True, stop=True).then_inc(sig["oss"], 1)
                            pe.wait_ge(sig["o3"], c + 1)
                            if j == 1:
                                pe.wait_ge(sig["y"], c)
                            for h in range(HG):
                                last = pe.matmul(ps[3][:, 0:D], o[:, h, :], wo[:, h, :], start=(h == 0), stop=(h == HG - 1))
                            last.then_inc(sig["y_ps"], 1)

                        for pair in range(2):
                            build(2 * pair)
                            build(2 * pair + 1)
                            inverse(pair)
                            recur(2 * pair)
                            recur(2 * pair + 1)

                    @block.scalar
                    def _(act):
                        st = Steps(act, sig["order"])
                        act.activation(xb[:], xn_fm[:, :, ds(b * S, S)], ACT.Copy).then_inc(sig["xb"], 1)

                        def silu(i):
                            act.wait_ge(sig["conv"], i + 1)
                            act.activation(qkv[:, i, :], qkv[:, i, :], ACT.Silu).then_inc(sig["silu"], 1)

                        for i in range(CT):
                            act.wait_ge(sig["proj"], i + 1)
                            act.activation(qkv[:, i, :], ps[i % 4][:], ACT.Copy, scale=cw[:, i, 3:4]).then_inc(sig["tap0"], 1)
                            if i >= 1:
                                silu(i - 1)
                        silu(CT - 1)
                        for h in range(HG):
                            act.wait_ge(sig["proj"], CT + h + 1)
                            act.activation(gt[:, h, :], ps[(CT + h) % 4][:], ACT.Silu).then_inc(sig["gate"], 1)
                        for i in range(2 * KG):
                            act.wait_ge(sig["silu"], i + 1)
                            if i >= 2:
                                act.wait_ge(sig["ss"], i - 1)
                            act.activation(sq[:, i % 2, :], qkv[:, i, :], ACT.Square).then_inc(sig["sq"], 1)
                        for i in range(2 * KG):
                            act.wait_ge(sig["ss"], i + 1)
                            p = ps[4 + i % 2][:]
                            st.link(act.activation(p, p, ACT.Ln, bias=eps[:, 0:1]))
                            act.activation(p, p, ACT.Exp, scale=-0.5, bias=qb[:, 0:1] if i < KG else 0.0).then_inc(sig["rn"], 1)
                        for c in range(CH):
                            act.wait_ge(sig["vt_ps"], c + 1)
                            act.wait_ge(sig["lam"], 1)
                            for h in range(HG):
                                last = act.activation(vtok[:, c, h, :], ps[6 + c % 2][:, h * P:(h + 1) * P], ACT.Copy,
                                                      scale=be[:, c * HG + h:c * HG + h + 1])
                            last.then_inc(sig["vt"], 1)
                        for c in range(CH):
                            act.wait_ge(sig["kt_ps"], c + 1)
                            act.activation(ktok[:, c].rearrange("p h n -> p (h n)"), ps[4 + c % 2][:, 0:KG * P], ACT.Copy
                                           ).then_inc(sig["kt"], 1)

                        def decays(c):
                            j = c % 2
                            act.wait_ge(sig["d_ps"], c + 1)
                            if c >= 2:
                                act.wait_ge(sig["y"], 2)
                            for dst, bank in ((L, 2), (A, 0), (G, 4)):
                                last = act.activation(flat(dst[:, j]), ps[bank + j][:], ACT.Exp)
                            last.then_inc(sig["e_row"], 1)

                        def recur(c):
                            act.wait_ge(sig["dcol"], c + 1)
                            act.wait_ge(sig["kt"], c + 1)
                            if c >= 1:
                                act.wait_ge(sig["dst"], c)
                            for h in range(HG):
                                last = act.activation(kd[:, h, :], ktok[:, c, h // 2, :], ACT.Copy, scale=dcol[:, c, h:h + 1])
                            last.then_inc(sig["kd"], 1)
                            act.wait_ge(sig["u_ps"], c + 1)
                            act.activation(flat(U), ps[7][:], ACT.Copy).then_inc(sig["u"], 1)
                            act.wait_ge(sig["o_ps"], c + 1)
                            if c >= 1:
                                act.wait_ge(sig["y_ps"], c)
                                act.wait_ge(sig["oss"], c)
                            act.activation(flat(o), ps[0][:], ACT.Copy).then_inc(sig["o"], 1)
                            act.activation(osq[:], ps[0][:], ACT.Square).then_inc(sig["osq"], 1)
                            act.wait_ge(sig["oss"], c + 1)
                            st.link(act.activation(ps[2][:], ps[2][:], ACT.Ln, scale=1.0 / P, bias=eps[:, 0:1]))
                            act.activation(ps[2][:], ps[2][:], ACT.Exp, scale=-0.5).then_inc(sig["orn"], 1)

                        for pair in range(2):
                            decays(2 * pair)
                            decays(2 * pair + 1)
                            recur(2 * pair)
                            recur(2 * pair + 1)

                    @block.gpsimd
                    def _(pool):
                        for c in range(CH):
                            j = c % 2
                            pool.wait_ge(sig["l0"], c + 1)
                            pool.affine_select(out=L[:, j], in_=L[:, j], compare_op=ALU.is_ge, fill=0.0, base=-1,
                                               pattern=[[0, HG], [-1, P]], channel_multiplier=1).then_inc(sig["l"], 1)
                            pool.wait_ge(sig["a0"], c + 1)
                            pool.affine_select(out=A[:, j], in_=A[:, j], compare_op=ALU.is_ge, fill=0.0, base=0,
                                               pattern=[[0, HG], [1, P]], channel_multiplier=-1).then_inc(sig["a"], 1)
                            pool.wait_ge(sig["g"], c + 1)
                            pool.wait_ge(sig["norm"], 2 * KG)
                            if c >= 2:
                                pool.wait_ge(sig["o_ps"], c - 1)
                            for dst, base in ((kg, KG), (qg, 0)):
                                for h in range(HG):
                                    last = pool.tensor_tensor(dst[:, j, h, :], G[:, j, h, :],
                                                              qkv[:, base + h // 2, c * P:(c + 1) * P], ALU.mult)
                            last.then_inc(sig["kg"], 1)

                    @block.vector
                    def _(dve):
                        st = Steps(dve, sig["porder"])
                        st.mark(dve.tensor_copy(la[:], la_all[:, ds(b * NG + gi, 1), :].squeeze(1)))
                        st.mark(dve.tensor_copy(be[:], be_all[:, ds(b * NG + gi, 1), :].squeeze(1)))
                        st.wait()
                        st.mark(dve.tensor_scalar(nb[:], be[:], -1.0, None, ALU.mult))
                        dve.memset(state[:], 0.0).then_inc(sig["s"], 1)

                        def lams(c):
                            if c >= 2:
                                dve.wait_ge(sig["d_ps"], c - 1)
                            for h in range(HG):
                                last = dve.tensor_scalar(lam[:, c % 2, h, :], tri[:], la[:, c * HG + h:c * HG + h + 1], None, ALU.mult)
                            last.then_inc(sig["lam"], 1)

                        lams(0)
                        lams(1)
                        for i in range(CT):
                            dve.wait_ge(sig["tap0"], i + 1)
                            for n in (1, 2, 3):
                                ins = dve.scalar_tensor_tensor(out=qkv[:, i, n:], in0=ps[i % 4][:, 0:S - n], scalar=cw[:, i, 3 - n:4 - n],
                                                               in1=qkv[:, i, n:], op0=ALU.mult, op1=ALU.add)
                                if n < 3:
                                    st.link(ins)
                                else:
                                    ins.then_inc(sig["conv"], 1)
                        for i in range(2 * KG):
                            dve.wait_ge(sig["rn"], i + 1)
                            dve.wait_ge(sig["sq"], i + 1)
                            dve.tensor_tensor(qkv[:, i, :], qkv[:, i, :], ps[4 + i % 2][:], ALU.mult).then_inc(sig["norm"], 1)

                        def build(c):
                            j = c % 2
                            dve.wait_ge(sig["e_row"], c + 1)
                            dve.tensor_scalar(flat(G[:, j]), flat(G[:, j]), LEAST, None, ALU.max).then_inc(sig["g"], 1)
                            dve.tensor_scalar(dcol[:, c, :], A[:, j, :, P - 1], LEAST, None, ALU.max).then_inc(sig["dcol"], 1)
                            dve.wait_ge(sig["kk_ps"], c + 1)
                            kk = ps[6 + j][:, 0:KG * P].rearrange("p (k n) -> p k n", k=KG)
                            kq = ps[6 + j][:, KG * P:].rearrange("p (k n) -> p k n", k=KG)
                            for k in range(KG):
                                hh = slice(2 * k, 2 * k + 2)
                                last = dve.scalar_tensor_tensor(out=L[:, j, hh, :], in0=L[:, j, hh, :], scalar=LEAST, in1=bc(kk[:, k, :], 1, 2),
                                                                op0=ALU.max, op1=ALU.mult)
                            st.link(last)
                            for h in range(HG):
                                last = dve.tensor_scalar(L[:, j, h, :], L[:, j, h, :], be[:, c * HG + h:c * HG + h + 1], None, ALU.mult)
                            last.then_inc(sig["l0"], 1)
                            dve.wait_ge(sig["dcol"], c + 1)
                            for k in range(KG):
                                hh = slice(2 * k, 2 * k + 2)
                                last = dve.scalar_tensor_tensor(out=A[:, j, hh, :], in0=A[:, j, hh, :], scalar=LEAST, in1=bc(kq[:, k, :], 1, 2),
                                                                op0=ALU.max, op1=ALU.mult)
                            last.then_inc(sig["a0"], 1)

                        def inverse(pair):
                            for s in range(LV):
                                for j in range(2):
                                    n = pair * NQ + 2 * s + j
                                    dve.wait_ge(sig["w_ps"], n + 1)
                                    if s > 0:
                                        dve.wait_ge(sig["xy_ps"], n - 1)
                                    dve.tensor_tensor(W[:, j], h4(ps[j][:]), bc(lmask[:, s, :], 1, HG), ALU.mult).then_inc(sig["w"], 1)
                                for j in range(2):
                                    n = pair * NQ + 2 * s + j
                                    dve.wait_ge(sig["xy_ps"], n + 1)
                                    if s > 0:
                                        dve.wait_ge(sig["xy"], n - 1)
                                    last = dve.tensor_tensor(Y[:, j], bc(ident[:], 1, HG) if s == 0 else Y[:, j], h4(ps[2 + j][:]), ALU.subtract)
                                    if s < LV - 1:
                                        last = dve.tensor_tensor(X[:, j], bc(ident[:], 1, HG) if s == 0 else X[:, j], h4(ps[4 + j][:]), ALU.subtract)
                                    last.then_inc(sig["xy"], 1)

                        def recur(c):
                            j = c % 2
                            dve.wait_ge(sig["ks"], c + 1)
                            dve.wait_ge(sig["vt"], c + 1)
                            if c >= 1:
                                dve.wait_ge(sig["u_ps"], c)
                            for h in range(HG):
                                last = dve.scalar_tensor_tensor(out=R[:, h, :], in0=ps[6][:, h * P:(h + 1) * P],
                                                                scalar=nb[:, c * HG + h:c * HG + h + 1], in1=vtok[:, c, h, :],
                                                                op0=ALU.mult, op1=ALU.add)
                            last.then_inc(sig["r"], 1)
                            dve.wait_ge(sig["o_ps"], c + 1)
                            dve.wait_ge(sig["dst"], c + 1)
                            dve.wait_ge(sig["s"], c + 1)
                            for h in range(HG):
                                last = dve.scalar_tensor_tensor(out=state[:, h, :], in0=state[:, h, :], scalar=G[:, j, h, P - 1:P],
                                                                in1=ps[1][:, h * P:(h + 1) * P], op0=ALU.mult, op1=ALU.add)
                            last.then_inc(sig["s"], 1)
                            dve.wait_ge(sig["orn"], c + 1)
                            st.link(dve.scalar_tensor_tensor(out=flat(o), in0=flat(o), scalar=rw[:, 0:1], in1=ps[2][:],
                                                             op0=ALU.mult, op1=ALU.mult))
                            dve.tensor_tensor(o[:], o[:], gt[:, :, c * P:(c + 1) * P], ALU.mult).then_inc(sig["o3"], 1)
                            dve.wait_ge(sig["y_ps"], c + 1)
                            so = s_out[:, ds(b * CH + c, 1), :].squeeze(1)
                            dve.tensor_tensor(so, so, ps[3][:, 0:D], ALU.add).then_inc(sig["y"], 1)

                        for pair in range(2):
                            if pair:
                                lams(2)
                                lams(3)
                            build(2 * pair)
                            build(2 * pair + 1)
                            inverse(pair)
                            recur(2 * pair)
                            recur(2 * pair + 1)
                end_of_iteration(nc, sig)


def nvfp4_mlp(nc, g, d):
    N = 2048
    NTL = N // P
    with ExitStack() as ctx:
        sb = lambda n, s, t=F32: ctx.enter_context(nc.sbuf_tensor("nv_" + n, s, t))
        sig = signals(nc, ctx, "nv", "load next code sgn part v1 v2 v3 done xb a b act h down acc")
        wg, wu, wd = (sb(n, [P, 2, N]) for n in ("wg", "wu", "wd"))
        xb = sb("xb", [P, K2, S])
        act_, h = sb("act", [P, 2, S]), sb("h", [P, 2, S])
        acc, gate = sb("acc", [P, CH, D]), sb("gate", [P, CH, D])
        ps, xn_fm = g["ps"], g["xn_fm"]
        NB, CW = 3 * 4, N // 4
        with ExitStack() as c2:
            tb = lambda n, s, t=F32: c2.enter_context(nc.sbuf_tensor("nv_" + n, s, t))
            code, scale = tb("code", [P, 2, CW], I32), tb("scale", [P, 2, CW])
            m, sg = tb("m", [P, 2, CW], I32), tb("sg", [P, 2, CW], I32)
            hi4, hi6, sgn = tb("hi4", [P, 2, CW]), tb("hi6", [P, 2, CW]), tb("sgn", [P, 2, CW])
            m2, m6 = tb("m2", [P, 1]), tb("m6", [P, 1])
            with nc.Block() as block:
                @block.vector
                def _(dve):
                    dve.memset(m2[:], -2.0)
                    dve.memset(m6[:], -6.0)
            end_of_iteration(nc, sig)
            with nc.Block() as block:
                @block.sync
                def _(sp):
                    for i in range(NB):
                        if i >= 2:
                            sp.wait_ge(sig["done"], 2 * (i - 1))
                        name, c0 = ("gate", "up", "down")[i // 4], (i % 4) * CW
                        sp.dma_start(code[:, i % 2, :], d["nv_" + name + "_w"][:, c0:c0 + CW]).then_inc(sig["load"] if i % 2 == 0 else sig["next"], 16)
                        sp.dma_start(scale[:, i % 2, :], d["nv_" + name + "_s"][:, c0:c0 + CW]).then_inc(sig["load"] if i % 2 == 0 else sig["next"], 16)

                @block.scalar
                def _(act):
                    for u in range(2 * NB):
                        act.wait_ge(sig["sgn"], u + 1)
                        if u >= 2:
                            act.wait_ge(sig["done"], u - 1)
                        r = u % 2
                        act.activation(hi4[:, r, :], m[:, r, :], ACT.Relu, scale=0.5, bias=m2[:, 0:1])
                        act.activation(hi6[:, r, :], m[:, r, :], ACT.Relu, bias=m6[:, 0:1])
                        act.activation(sgn[:, r, :], sg[:, r, :], ACT.Copy, scale=-0.25, bias=1.0).then_inc(sig["part"], 1)

                @block.gpsimd
                def _(pool):
                    for u in range(2 * NB):
                        i, r = u // 2, u % 2
                        pool.wait_ge(sig["part"], u + 1)
                        pool.tensor_tensor(sgn[:, r, :], sgn[:, r, :], scale[:, i % 2, :], ALU.mult).then_inc(sig["v2"], 1)

                @block.vector
                def _(dve):
                    def take(u):
                        i, nib, r = u // 2, u % 2, u % 2
                        dve.wait_ge(sig["load"] if i % 2 == 0 else sig["next"], 32 * (i // 2 + 1))
                        if u >= 2:
                            dve.wait_ge(sig["part"], u - 1)
                            dve.wait_ge(sig["done"], u - 1)
                        dve.tensor_scalar(m[:, r, :], code[:, i % 2, :], 4 * nib, 7, ALU.logical_shift_right, ALU.bitwise_and
                                          ).then_inc(sig["code"], 1)
                        dve.tensor_scalar(sg[:, r, :], code[:, i % 2, :], 4 * nib, 8, ALU.logical_shift_right, ALU.bitwise_and
                                          ).then_inc(sig["sgn"], 1)

                    def finish(u):
                        i, nib, r = u // 2, u % 2, u % 2
                        dst = (wg, wu, wd)[i // 4][:, nib, (i % 4) * CW:(i % 4 + 1) * CW]
                        dve.wait_ge(sig["part"], u + 1)
                        dve.scalar_tensor_tensor(out=hi4[:, r, :], in0=m[:, r, :], scalar=0.5, in1=hi4[:, r, :],
                                                 op0=ALU.mult, op1=ALU.add).then_inc(sig["v1"], 1)
                        dve.wait_ge(sig["v1"], u + 1)
                        dve.tensor_tensor(hi4[:, r, :], hi4[:, r, :], hi6[:, r, :], ALU.add).then_inc(sig["v3"], 1)
                        dve.wait_ge(sig["v3"], u + 1)
                        dve.wait_ge(sig["v2"], u + 1)
                        dve.tensor_tensor(dst, hi4[:, r, :], sgn[:, r, :], ALU.mult).then_inc(sig["done"], 1)

                    for u in range(2 * NB):
                        take(u)
                        if u >= 1:
                            finish(u - 1)
                    finish(2 * NB - 1)
            end_of_iteration(nc, sig)
        with nc.Fori(0, B) as b:
            with nc.Block() as block:
                @block.tensor
                def _(pe):
                    pe.wait_ge(sig["xb"], 1)

                    def up(u):
                        if u >= 2:
                            pe.wait_ge(sig["h"], u - 1)
                        for n, (w, what) in enumerate(((wg, "a"), (wu, "b"))):
                            for k in range(K2):
                                last = pe.matmul(ps[2 * (u % 2) + n][:], w[:, k, u * P:(u + 1) * P], xb[:, k, :],
                                                 start=(k == 0), stop=(k == K2 - 1))
                            last.then_inc(sig[what], 1)

                    def down(u):
                        pe.wait_ge(sig["h"], u + 1)
                        q, nib = u // 2, u % 2
                        for t in range(CH):
                            last = pe.matmul(ps[4 + t // 2][:, (t % 2) * D:(t % 2 + 1) * D], h[:, u % 2, t * P:(t + 1) * P],
                                             wd[:, nib, q * D:(q + 1) * D], start=(u == 0 and t % 2 == 0), stop=(u == NTL - 1),
                                             skip_group_check=True)
                        last.then_inc(sig["down"], 1)

                    for u in range(NTL):
                        up(u)
                        if u >= 1:
                            down(u - 1)
                    down(NTL - 1)

                @block.scalar
                def _(act):
                    act.activation(xb[:], xn_fm[:, :, ds(b * S, S)], ACT.Copy).then_inc(sig["xb"], 1)
                    for u in range(NTL):
                        act.wait_ge(sig["a"], u + 1)
                        if u >= 2:
                            act.wait_ge(sig["h"], u - 1)
                        act.activation(act_[:, u % 2, :], ps[2 * (u % 2)][:], ACT.Gelu_apprx_tanh).then_inc(sig["act"], 1)

                @block.vector
                def _(dve):
                    for u in range(NTL):
                        dve.wait_ge(sig["act"], u + 1)
                        dve.wait_ge(sig["b"], u + 1)
                        if u >= 2:
                            dve.wait_ge(sig["down"], u - 1)
                        dve.tensor_tensor(h[:, u % 2, :], act_[:, u % 2, :], ps[2 * (u % 2) + 1][:], ALU.mult).then_inc(sig["h"], 1)
                    dve.wait_ge(sig["down"], NTL)
                    for t in range(2):
                        dve.tensor_copy(acc[:, 2 * t:2 * t + 2, :].rearrange("p t f -> p (t f)"), ps[4 + t][:])
            end_of_iteration(nc, sig)
            gated_update(nc, g, acc, gate, b)


def linear_attention(nc, g, d):
    with ExitStack() as ctx:
        sb = lambda n, s, t=F32: ctx.enter_context(nc.sbuf_tensor("la_" + n, s, t))
        sig = signals(nc, ctx, "la", "load xb q_ps q qd k_ps ka k v_ps v kv_ps kvm nd den lden rden o out_ps out")
        wq, wk, wv, wo = (sb(n, [P, K2, D]) for n in ("wq", "wk", "wv", "wo"))
        bq, bk, bv, bo = sb("bq", [P, K2]), sb("bk", [P, D]), sb("bv", [P, D]), sb("bo", [P, D])
        dec_row, dec_col, blocks = sb("dec_row", [P, S]), sb("dec_col", [P, CH]), sb("blocks", [P, P])
        xb, q = sb("xb", [P, K2, S]), sb("q", [P, K2, S])
        k_, v = sb("k", [P, CH, D]), sb("v", [P, CH, D])
        kv, ksum = sb("kv", [P, K2, P]), sb("ksum", [P, K2, P])
        rd, o = sb("rd", [P, K2, S]), sb("o", [P, K2, S])
        ps, xn_fm, s_out, ones, eps = g["ps"], g["xn_fm"], g["s"], g["ones"], g["eps6"]
        load(nc, sig, "load", [(wq[:], d["la_wq"]), (wk[:], d["la_wk"]), (wv[:], d["la_wv"]), (wo[:], d["la_wo"]), (bq[:], d["la_bq"]),
                               (bk[:], d["la_bk"].partition_broadcast(P)), (bv[:], d["la_bv"].partition_broadcast(P)),
                               (bo[:], d["la_bo"].partition_broadcast(P)), (dec_row[:], d["c_dec"].partition_broadcast(P)),
                               (dec_col[:], d["c_dec_col"]), (blocks[:], d["c_blocks"])])
        with nc.Fori(0, B) as b:
            with nc.Block() as block:
                @block.tensor
                def _(pe):
                    pe.wait_ge(sig["xb"], 1)
                    for m in range(K2):
                        for k in range(K2):
                            last = pe.matmul(ps[m][:], wq[:, k, m * P:(m + 1) * P], xb[:, k, :], start=(k == 0), stop=(k == K2 - 1))
                        last.then_inc(sig["q_ps"], 1)
                    for w, what, bank in ((wk, "k_ps", 2), (wv, "v_ps", 4)):
                        for t in range(CH):
                            for k in range(K2):
                                last = pe.matmul(ps[bank + t // 2][:, (t % 2) * D:(t % 2 + 1) * D], xb[:, k, t * P:(t + 1) * P], w[:, k, :],
                                                 start=(k == 0), stop=(k == K2 - 1))
                        last.then_inc(sig[what], 1)
                    pe.wait_ge(sig["k"], CH)
                    pe.wait_ge(sig["v"], CH)
                    for m in range(K2):
                        ms = slice(m * P, (m + 1) * P)
                        for t in range(CH):
                            pe.matmul(ps[6 + m][:, 0:P], k_[:, t, ms], v[:, t, ms], start=(t == 0), stop=(t == CH - 1))
                        for t in range(CH):
                            last = pe.matmul(ps[6 + m][:, P:2 * P], k_[:, t, ms], ones[:], start=(t == 0), stop=(t == CH - 1))
                        last.then_inc(sig["kv_ps"], 1)
                    for m in range(K2):
                        pe.wait_ge(sig["kvm"], 2 * (m + 1))
                        pe.wait_ge(sig["qd"], m + 1)
                        pe.matmul(ps[2 + m][:], ksum[:, m, :], q[:, m, :], start=True, stop=True).then_inc(sig["den"], 1)
                        pe.matmul(ps[4 + m][:], kv[:, m, :], q[:, m, :], start=True, stop=True).then_inc(sig["nd"], 1)
                    pe.wait_ge(sig["o"], K2)
                    for t in range(CH):
                        for m in range(K2):
                            last = pe.matmul(ps[t // 2][:, (t % 2) * D:(t % 2 + 1) * D], o[:, m, t * P:(t + 1) * P], wo[:, m, :],
                                             start=(m == 0), stop=(m == K2 - 1))
                    last.then_inc(sig["out_ps"], 1)

                @block.scalar
                def _(act):
                    act.activation(xb[:], xn_fm[:, :, ds(b * S, S)], ACT.Copy).then_inc(sig["xb"], 1)
                    for m in range(K2):
                        act.wait_ge(sig["q_ps"], m + 1)
                        act.activation(q[:, m, :], ps[m][:], ACT.Relu, bias=bq[:, m:m + 1]).then_inc(sig["q"], 1)
                    for t in range(CH):
                        act.wait_ge(sig["ka"], t + 1)
                        act.activation(k_[:, t, :], k_[:, t, :], ACT.Relu, scale=dec_col[:, t:t + 1]).then_inc(sig["k"], 1)
                    for m in range(K2):
                        act.wait_ge(sig["den"], m + 1)
                        act.activation(rd[:, m, :], ps[2 + m][:], ACT.Ln, bias=eps[:, 0:1]).then_inc(sig["lden"], 1)
                        act.wait_ge(sig["lden"], m + 1)
                        act.activation(rd[:, m, :], rd[:, m, :], ACT.Exp, scale=-1.0).then_inc(sig["rden"], 1)

                @block.vector
                def _(dve):
                    dve.wait_ge(sig["k_ps"], 1)
                    for t in range(CH):
                        dve.tensor_tensor(k_[:, t, :], ps[2 + t // 2][:, (t % 2) * D:(t % 2 + 1) * D], bk[:], ALU.add).then_inc(sig["ka"], 1)
                    dve.wait_ge(sig["v_ps"], 1)
                    for t in range(CH):
                        dve.tensor_tensor(v[:, t, :], ps[4 + t // 2][:, (t % 2) * D:(t % 2 + 1) * D], bv[:], ALU.add).then_inc(sig["v"], 1)
                    for m in range(K2):
                        dve.wait_ge(sig["q"], m + 1)
                        dve.tensor_tensor(q[:, m, :], q[:, m, :], dec_row[:], ALU.mult).then_inc(sig["qd"], 1)
                    for m in range(K2):
                        dve.wait_ge(sig["kv_ps"], m + 1)
                        dve.tensor_tensor(kv[:, m, :], ps[6 + m][:, 0:P], blocks[:], ALU.mult).then_inc(sig["kvm"], 1)
                        dve.tensor_tensor(ksum[:, m, :], ps[6 + m][:, P:2 * P], blocks[:], ALU.mult).then_inc(sig["kvm"], 1)
                    for m in range(K2):
                        dve.wait_ge(sig["rden"], m + 1)
                        dve.wait_ge(sig["nd"], m + 1)
                        dve.tensor_tensor(o[:, m, :], rd[:, m, :], ps[4 + m][:], ALU.mult).then_inc(sig["o"], 1)
                    dve.wait_ge(sig["out_ps"], 1)
                    for t in range(CH):
                        dve.tensor_tensor(s_out[:, ds(b * CH + t, 1), :].squeeze(1), ps[t // 2][:, (t % 2) * D:(t % 2 + 1) * D], bo[:], ALU.add)
            end_of_iteration(nc, sig)


def latent_attention(nc, g, d):
    NH, DN, DR, DV, QL, KL = 16, 128, 64, 128, 192, 64
    QM = QL // 2
    HG, NG = 4, NH // 4
    SCALE = float((DN + DR) ** -0.5)
    with ExitStack() as ctx:
        sb = lambda n, s, t=F32: ctx.enter_context(nc.sbuf_tensor("mla_" + n, s, t))
        pre = signals(nc, ctx, "mp", "load xb lat_ps lat sq ss l1 rn out pe_ps t1 t2 order")
        sig = signals(nc, ctx, "mla", "wnext kvb v_ps v qn_ps qp_ps kn_ps qn qp kn s_ps m0 m1 nm e rs p pt_ps pt o_ps o y_ps y order")
        qn_all, kvn_all, kr_all = sb("qn_all", [QM, 2, B * S]), sb("kvn_all", [KL, B * S]), sb("kr_all", [P, B * S])
        ps, xn_fm, s_out, ident, ones, eps = g["ps"], g["xn_fm"], g["s"], g["ident"], g["ones"], g["eps6"]
        table = sb("table", [P, S])
        with ExitStack() as c2:
            tb = lambda n, s, t=F32: c2.enter_context(nc.sbuf_tensor("mp_" + n, s, t))
            wa = tb("wa", [P, K2, QL + KL + 4 * DR])
            qg, kg_ = tb("qg", [QM, 2]), tb("kg", [KL, 1])
            cos2, sin2 = tb("cos2", [P, S]), tb("sin2", [P, S])
            xb, lat, sq = tb("xb", [P, K2, S]), tb("lat", [P, 3, S]), tb("sq", [P, 3, S])
            t1 = tb("t1", [P, S])
            load(nc, pre, "load", [(wa[:], d["mla_wa"]), (qg[:], d["mla_qg"]), (kg_[:], d["mla_kg"]), (cos2[:], d["c_cos2"]),
                                   (sin2[:], d["c_sin2"]), (table[0:DR, :], d["c_cos2"][0:DR]), (table[DR:, :], d["c_sin2"][0:DR])])
            sizes = [QM, QM, KL]
            with nc.Fori(0, B) as b:
                with nc.Block() as block:
                    @block.tensor
                    def _(pe):
                        pe.wait_ge(pre["xb"], 1)
                        c0 = 0
                        for i, n in enumerate(sizes + [2 * DR, 2 * DR]):
                            for k in range(K2):
                                last = pe.matmul(ps[i][0:n, :], wa[:, k, c0:c0 + n], xb[:, k, :], start=(k == 0), stop=(k == K2 - 1))
                            last.then_inc(pre["lat_ps"], 1)
                            c0 += n
                        pe.wait_ge(pre["sq"], 3)
                        pe.matmul(ps[5][:], ones[0:QM, :], sq[0:QM, 0, :], start=True, stop=False)
                        pe.matmul(ps[5][:], ones[0:QM, :], sq[0:QM, 1, :], start=False, stop=True)
                        pe.matmul(ps[6][:], ones[0:KL, :], sq[0:KL, 2, :], start=True, stop=True).then_inc(pre["ss"], 1)

                    @block.scalar
                    def _(act):
                        st = Steps(act, pre["order"])
                        act.activation(xb[:], xn_fm[:, :, ds(b * S, S)], ACT.Copy).then_inc(pre["xb"], 1)
                        for i, n in enumerate(sizes):
                            act.wait_ge(pre["lat_ps"], i + 1)
                            act.activation(lat[0:n, i, :], ps[i][0:n, :], ACT.Copy).then_inc(pre["lat"], 1)
                            act.activation(sq[0:n, i, :], ps[i][0:n, :], ACT.Square).then_inc(pre["sq"], 1)
                        act.wait_ge(pre["ss"], 1)
                        for bank, n in ((5, QL), (6, KL)):
                            st.link(act.activation(ps[bank][:], ps[bank][:], ACT.Ln, scale=1.0 / n, bias=eps[:, 0:1]))
                            act.activation(ps[bank][:], ps[bank][:], ACT.Exp, scale=-0.5).then_inc(pre["rn"], 1)

                    @block.vector
                    def _(dve):
                        dve.wait_ge(pre["lat_ps"], 5)
                        dve.tensor_tensor(t1[:], cos2[:], ps[3][:], ALU.mult).then_inc(pre["t1"], 1)
                        kr = kr_all[:, ds(b * S, S)]
                        dve.tensor_tensor(kr, sin2[:], ps[4][:], ALU.mult).then_inc(pre["t2"], 1)
                        dve.wait_ge(pre["t1"], 1)
                        dve.wait_ge(pre["t2"], 1)
                        dve.tensor_tensor(kr, kr, t1[:], ALU.add)
                        dve.wait_ge(pre["lat"], 3)
                        for i, n in enumerate(sizes):
                            dve.wait_ge(pre["rn"], 1 if i < 2 else 2)
                            out = qn_all[:, i, ds(b * S, S)] if i < 2 else kvn_all[:, ds(b * S, S)]
                            gamma = qg[:, i:i + 1] if i < 2 else kg_[:, 0:1]
                            dve.scalar_tensor_tensor(out=out, in0=lat[0:n, i, :], scalar=gamma, in1=ps[5 if i < 2 else 6][0:n, :],
                                                     op0=ALU.mult, op1=ALU.mult)
                end_of_iteration(nc, pre)
        with nc.Block() as block:
            @block.vector
            def _(dve):
                dve.memset(s_out[:], 0.0)
        end_of_iteration(nc, pre)

        wq = sb("wq", [QM, 2, HG, 2 * P])
        wk, wv, wo = sb("wk", [KL, HG, DN]), sb("wv", [KL, HG * DV]), sb("wo", [P, HG, D])
        later = sb("later", [P, P])
        kvb, V = sb("kvb", [KL, S]), sb("V", [P, CH, HG * DV])
        qn, qp, kn = sb("qn", [P, 2, S]), sb("qp", [P, 2, S]), sb("kn", [P, 2, S])
        pr, PT, o = sb("pr", [P, 2, S]), sb("PT", [P, 2, CH, S]), sb("o", [P, 2, S])
        mx, nm, rs = sb("mx", [P, 4 * CH]), sb("nm", [P, 4 * CH]), sb("rs", [P, 4 * CH])
        load(nc, sig, "wnext", [(later[:], d["c_later"]), (wq[:], d["mla_wq"][0]), (wk[:], d["mla_wk"][0]), (wv[:], d["mla_wv"][0]),
                                (wo[:], d["mla_wo"][0])])
        NU = HG * CH
        with nc.Fori(0, B) as b:
            with nc.Fori(0, NG) as gi:
                with nc.Block() as block:
                    @block.sync
                    def _(sp):
                        sp.wait_ge(sig["v_ps"], CH)
                        sp.dma_start(wv[:], d["mla_wv"][ds(gi + 1, 1)].squeeze(0)).then_inc(sig["wnext"], 16)
                        sp.wait_ge(sig["kn_ps"], HG)
                        sp.dma_start(wq[:], d["mla_wq"][ds(gi + 1, 1)].squeeze(0)).then_inc(sig["wnext"], 16)
                        sp.dma_start(wk[:], d["mla_wk"][ds(gi + 1, 1)].squeeze(0)).then_inc(sig["wnext"], 16)
                        sp.wait_ge(sig["y_ps"], HG)
                        sp.dma_start(wo[:], d["mla_wo"][ds(gi + 1, 1)].squeeze(0)).then_inc(sig["wnext"], 16)
                        sp.wait_ge(sig["wnext"], 64)

                    @block.tensor
                    def _(pe):
                        pe.wait_ge(sig["kvb"], 1)
                        for t in range(CH):
                            pe.matmul(ps[2 + t][:], kvb[:, t * P:(t + 1) * P], wv[:], start=True, stop=True).then_inc(sig["v_ps"], 1)

                        def project(h):
                            if h >= 1:
                                pe.wait_ge(sig["kn"], h)
                            for i in range(2):
                                last = pe.matmul(ps[0][:], wq[:, i, h, 0:P], qn_all[:, i, ds(b * S, S)], start=(i == 0), stop=(i == 1))
                            last.then_inc(sig["qn_ps"], 1)
                            if h >= 1:
                                pe.wait_ge(sig["qp"], h)
                            for i in range(2):
                                last = pe.matmul(ps[1][:], wq[:, i, h, P:2 * P], qn_all[:, i, ds(b * S, S)], start=(i == 0), stop=(i == 1))
                            last.then_inc(sig["qp_ps"], 1)
                            pe.wait_ge(sig["qn"], h + 1)
                            pe.matmul(ps[0][:], wk[:, h, :], kvb[:], start=True, stop=True).then_inc(sig["kn_ps"], 1)

                        def scores(u):
                            h, t = u // CH, u % CH
                            pe.wait_ge(sig["kn"], h + 1)
                            pe.wait_ge(sig["qp"], h + 1)
                            if u < 2:
                                pe.wait_ge(sig["v"], CH)
                            else:
                                pe.wait_ge(sig["e"], u - 1)
                            n, tt = (t + 1) * P, slice(t * P, (t + 1) * P)
                            pe.matmul(ps[2 + u % 2][:, 0:n], qn[:, h % 2, tt], kn[:, h % 2, 0:n], start=True, stop=False)
                            pe.matmul(ps[2 + u % 2][:, 0:n], qp[:, h % 2, tt], kr_all[:, ds(b * S, n)], start=False, stop=True
                                      ).then_inc(sig["s_ps"], 1)

                        def turn(u):
                            t = u % CH
                            pe.wait_ge(sig["p"], u + 1)
                            if u >= 1:
                                pe.wait_ge(sig["pt"], u)
                            for j in range(t + 1):
                                last = pe.transpose(ps[4][:, j * P:(j + 1) * P], pr[:, u % 2, j * P:(j + 1) * P], ident[:])
                            last.then_inc(sig["pt_ps"], 1)

                        def attend(h):
                            pe.wait_ge(sig["pt"], CH * (h + 1))
                            if h >= 1:
                                pe.wait_ge(sig["o"], h)
                            for j in range(CH):
                                last = pe.matmul(ps[5][:, j * P:], V[:, j, h * DV:(h + 1) * DV], PT[:, h % 2, j, j * P:],
                                                 start=(j == 0), stop=(j == CH - 1))
                            last.then_inc(sig["o_ps"], 1)

                        def out(h):
                            pe.wait_ge(sig["o"], h + 1)
                            for t in range(CH):
                                last = pe.matmul(ps[6 + t // 2][:, (t % 2) * D:(t % 2 + 1) * D], o[:, h % 2, t * P:(t + 1) * P], wo[:, h, :],
                                                 start=(h == 0 and t % 2 == 0), stop=(h == HG - 1), skip_group_check=True)
                            last.then_inc(sig["y_ps"], 1)

                        project(0)
                        for h in range(HG):
                            for t in range(CH):
                                u = h * CH + t
                                scores(u)
                                if t == 1 and h + 1 < HG:
                                    project(h + 1)
                                if u >= 1:
                                    turn(u - 1)
                                if t == 0 and h >= 1:
                                    attend(h - 1)
                                if t == 1 and h >= 1:
                                    out(h - 1)
                        turn(NU - 1)
                        attend(HG - 1)
                        out(HG - 1)

                    @block.scalar
                    def _(act):
                        act.activation(kvb[:], kvn_all[:, ds(b * S, S)], ACT.Copy).then_inc(sig["kvb"], 1)

                        def copies(h):
                            if h >= 2:
                                act.wait_ge(sig["s_ps"], CH * (h - 1))
                            act.wait_ge(sig["qn_ps"], h + 1)
                            act.activation(qn[:, h % 2, :], ps[0][:], ACT.Copy).then_inc(sig["qn"], 1)
                            act.wait_ge(sig["kn_ps"], h + 1)
                            act.activation(kn[:, h % 2, :], ps[0][:], ACT.Copy).then_inc(sig["kn"], 1)

                        def exps(u):
                            n = (u % CH + 1) * P
                            act.wait_ge(sig["nm"], u + 1)
                            if u >= 2:
                                act.wait_ge(sig["pt_ps"], u - 1)
                            act.activation(pr[:, u % 2, 0:n], ps[2 + u % 2][:, 0:n], ACT.Exp, scale=SCALE, bias=nm[:, u:u + 1],
                                           accum_out=rs[:, u:u + 1]).then_inc(sig["e"], 1)

                        def turned(u):
                            h, t = u // CH, u % CH
                            act.wait_ge(sig["pt_ps"], u + 1)
                            if h >= 2:
                                act.wait_ge(sig["o_ps"], h - 1)
                            act.activation(PT[:, h % 2, 0:t + 1, t * P:(t + 1) * P],
                                           ps[4][:, 0:(t + 1) * P].rearrange("p (j n) -> p j n", n=P), ACT.Copy).then_inc(sig["pt"], 1)

                        copies(0)
                        for u in range(NU):
                            exps(u)
                            if u % CH == 1 and u // CH + 1 < HG:
                                copies(u // CH + 1)
                            if u >= 1:
                                turned(u - 1)
                        turned(NU - 1)

                    @block.vector
                    def _(dve):
                        for t in range(CH):
                            dve.wait_ge(sig["v_ps"], t + 1)
                            dve.tensor_copy(V[:, t, :], ps[2 + t][:]).then_inc(sig["v"], 1)

                        def rotate(h):
                            dve.wait_ge(sig["qp_ps"], h + 1)
                            if h >= 2:
                                dve.wait_ge(sig["s_ps"], CH * (h - 1))
                            dve.tensor_tensor(qp[:, h % 2, :], table[:], ps[1][:], ALU.mult).then_inc(sig["qp"], 1)

                        def maxima(u):
                            t = u % CH
                            dve.wait_ge(sig["s_ps"], u + 1)
                            diag = ps[2 + u % 2][:, t * P:(t + 1) * P]
                            dve.tensor_tensor(diag, diag, later[:], ALU.add).then_inc(sig["m0"], 1)
                            dve.wait_ge(sig["m0"], u + 1)
                            dve.reduce_max(mx[:, u:u + 1], ps[2 + u % 2][:, 0:(t + 1) * P], AX_X).then_inc(sig["m1"], 1)
                            dve.wait_ge(sig["m1"], u + 1)
                            dve.tensor_scalar(nm[:, u:u + 1], mx[:, u:u + 1], -SCALE, None, ALU.mult).then_inc(sig["nm"], 1)

                        def normalise(u):
                            n = (u % CH + 1) * P
                            dve.wait_ge(sig["e"], u + 1)
                            dve.reciprocal(rs[:, u:u + 1], rs[:, u:u + 1]).then_inc(sig["rs"], 1)
                            dve.wait_ge(sig["rs"], u + 1)
                            dve.tensor_scalar(pr[:, u % 2, 0:n], pr[:, u % 2, 0:n], rs[:, u:u + 1], None, ALU.mult).then_inc(sig["p"], 1)

                        def attended(h):
                            dve.wait_ge(sig["o_ps"], h + 1)
                            if h >= 2:
                                dve.wait_ge(sig["y_ps"], h - 1)
                            dve.tensor_copy(o[:, h % 2, :], ps[5][:]).then_inc(sig["o"], 1)

                        rotate(0)
                        for u in range(NU):
                            maxima(u)
                            if u % CH == 1 and u // CH + 1 < HG:
                                rotate(u // CH + 1)
                            if u >= 1:
                                normalise(u - 1)
                            if u % CH == 1 and u // CH >= 1:
                                attended(u // CH - 1)
                        normalise(NU - 1)
                        attended(HG - 1)
                        dve.wait_ge(sig["y_ps"], HG)
                        for t in range(CH // 2):
                            so = s_out[:, ds(b * CH + 2 * t, 2), :]
                            dve.tensor_tensor(so, so, ps[6 + t][:].rearrange("p (t f) -> p t f", t=2), ALU.add)
                end_of_iteration(nc, sig)


def two_experts(nc, g, d):
    F = 2 * D
    FT = F // P
    with ExitStack() as ctx:
        sb = lambda n, s, t=F32: ctx.enter_context(nc.sbuf_tensor("te_" + n, s, t))
        sig = signals(nc, ctx, "te", "load xb lg lc m m1 up h down y z acc")
        wg = sb("wg", [P, K2, 2])
        wa, wb = sb("wa", [P, 2, K2, F]), sb("wb", [P, 2, FT, D])
        ba, bb = sb("ba", [P, 2, FT]), sb("bb", [P, 2, D])
        xb, h = sb("xb", [P, K2, S]), sb("h", [P, 2, FT, S])
        lc, m = sb("lc", [P, CH, 2]), sb("m", [P, 2, CH])
        y = sb("y", [P, 2, CH, D])
        acc, gate = sb("acc", [P, CH, D]), sb("gate", [P, CH, D])
        ps, xn_fm = g["ps"], g["xn_fm"]
        load(nc, sig, "load", [(wg[:], d["te_wg"]), (wa[:], d["te_wa"]), (wb[:], d["te_wb"]), (ba[:], d["te_ba"]),
                               (bb[:], d["te_bb"].partition_broadcast(P))])
        with nc.Fori(0, B) as b:
            with nc.Block() as block:
                @block.tensor
                def _(pe):
                    pe.wait_ge(sig["xb"], 1)
                    for t in range(CH):
                        for k in range(K2):
                            last = pe.matmul(ps[7][:, 2 * t:2 * t + 2], xb[:, k, t * P:(t + 1) * P], wg[:, k, :], start=(k == 0), stop=(k == K2 - 1))
                    last.then_inc(sig["lg"], 1)
                    for e in range(2):
                        for f in range(FT):
                            u = e * FT + f
                            if u >= 3:
                                pe.wait_ge(sig["h"], u - 2)
                            for k in range(K2):
                                last = pe.matmul(ps[u % 3][:], wa[:, e, k, f * P:(f + 1) * P], xb[:, k, :], start=(k == 0), stop=(k == K2 - 1))
                            last.then_inc(sig["up"], 1)
                    for e in range(2):
                        pe.wait_ge(sig["h"], FT * (e + 1))
                        for t in range(CH):
                            for f in range(FT):
                                last = pe.matmul(ps[3 + 2 * e + t // 2][:, (t % 2) * D:(t % 2 + 1) * D], h[:, e, f, t * P:(t + 1) * P], wb[:, e, f, :],
                                                 start=(f == 0), stop=(f == FT - 1))
                        last.then_inc(sig["down"], 1)

                @block.scalar
                def _(act):
                    act.activation(xb[:], xn_fm[:, :, ds(b * S, S)], ACT.Copy).then_inc(sig["xb"], 1)
                    for e in range(2):
                        for f in range(FT):
                            u = e * FT + f
                            act.wait_ge(sig["up"], u + 1)
                            act.activation(h[:, e, f, :], ps[u % 3][:], (ACT.Gelu, ACT.Relu)[e], bias=ba[:, e, f:f + 1]).then_inc(sig["h"], 1)

                @block.vector
                def _(dve):
                    dve.wait_ge(sig["lg"], 1)
                    dve.tensor_copy(lc[:].rearrange("p t e -> p (t e)"), ps[7][:, 0:2 * CH]).then_inc(sig["lc"], 1)
                    dve.wait_ge(sig["lc"], 1)
                    dve.tensor_tensor(m[:, 0, :], lc[:, :, 0], lc[:, :, 1], ALU.is_ge).then_inc(sig["m"], 1)
                    dve.wait_ge(sig["m"], 1)
                    dve.tensor_scalar(m[:, 1, :], m[:, 0, :], -1.0, 1.0, ALU.mult, ALU.add).then_inc(sig["m1"], 1)
                    for e in range(2):
                        dve.wait_ge(sig["down"], e + 1)
                        for t in range(CH):
                            dve.tensor_tensor(y[:, e, t, :], ps[3 + 2 * e + t // 2][:, (t % 2) * D:(t % 2 + 1) * D], bb[:, e, :], ALU.add
                                              ).then_inc(sig["y"], 1)
                    dve.wait_ge(sig["m1"], 1)
                    dve.wait_ge(sig["y"], 2 * CH)
                    for t in range(CH):
                        dve.tensor_scalar(y[:, 1, t, :], y[:, 1, t, :], m[:, 1, t:t + 1], None, ALU.mult).then_inc(sig["z"], 1)
                    for t in range(CH):
                        dve.wait_ge(sig["z"], t + 1)
                        dve.scalar_tensor_tensor(out=acc[:, t, :], in0=y[:, 0, t, :], scalar=m[:, 0, t:t + 1], in1=y[:, 1, t, :],
                                                 op0=ALU.mult, op1=ALU.add)
            end_of_iteration(nc, sig)
            gated_update(nc, g, acc, gate, b)


def program(nc, d, layers=(0, 1, 2, 3), dump=None):
    with ExitStack() as ctx:
        sb = lambda n, s, t=F32: ctx.enter_context(nc.sbuf_tensor(n, s, t))
        g = {"x": sb("x_res", [P, NT, D]), "xn_fm": sb("xn_fm", [P, K2, B * S]), "s": sb("s_mix", [P, NT, D]),
             "ident": sb("ident", [P, P]), "ones": sb("ones", [P, P]), "eps": sb("eps", [P, 1]),
             "eps6": sb("eps6", [P, 1])}
        g["ps"] = [ctx.enter_context(nc.psum_tensor("bank%d" % i, [P, 512], F32)) for i in range(8)]
        main = signals(nc, ctx, "main", "load store")
        g["ln_sig"] = signals(nc, ctx, "ln", "stats meanvar std rstd xn turned")
        g["up_sig"] = signals(nc, ctx, "up", "silu sg")
        with nc.Block() as block:
            @block.sync
            def _(sp):
                sp.dma_start(g["x"][:], d["x"]).then_inc(main["load"], 16)
                sp.dma_start(g["ident"][:], d["c_ident"]).then_inc(main["load"], 16)
                sp.wait_ge(main["load"], 32)

            @block.vector
            def _(dve):
                dve.memset(g["ones"][:], 1.0)
                dve.memset(g["eps"][:], LN_EPS)
                dve.memset(g["eps6"][:], 1e-6)
        end_of_iteration(nc, main)
        if 0 in layers:
            g["layer"] = 0
            layer_norm(nc, g)
            mamba(nc, g, d)
            if not dump: experts(nc, g, d, "e0", 8, 1, 128, 0, False)
        if 1 in layers:
            g["layer"] = 1
            layer_norm(nc, g)
            delta_rule(nc, g, d)
            if not dump: nvfp4_mlp(nc, g, d)
        if 2 in layers:
            g["layer"] = 2
            layer_norm(nc, g)
            linear_attention(nc, g, d)
            if not dump: experts(nc, g, d, "e2", 16, 2, 88, 2, True)
        if 3 in layers:
            g["layer"] = 3
            layer_norm(nc, g)
            latent_attention(nc, g, d)
            if not dump: two_experts(nc, g, d)
        with nc.Block() as block:
            @block.sync
            def _(sp):
                sp.dma_start(d["out"], g[dump or "x"][:]).then_inc(main["store"], 16)
                sp.wait_ge(main["store"], 16)


def fm(w):
    o, i = w.shape
    return w.T.reshape(i // K2, K2, o)


def layouts(a):
    r = {}
    r["x"] = a["L0_attn_x"].reshape(NT, P, D).transpose(1, 0, 2)
    r["c_ident"] = np.eye(P, dtype=np.float32)
    r["ma_wx"] = fm(a["L0_attn_W_x"])
    r["ma_wdt"] = a["L0_attn_W_dt"].reshape(P, K2, 64).transpose(2, 1, 0)
    r["ma_bdt"] = a["L0_attn_b_dt"].reshape(P, K2)
    r["ma_alog"] = a["L0_attn_A_log"].reshape(P, K2, 16)
    r["ma_d"] = a["L0_attn_D"].reshape(P, K2)
    r["e0_router"] = fm(a["L0_ffn_router_gate"])
    gu = a["L0_ffn_expert_gate_up"].reshape(8, P, K2, 128, 2)
    r["e0_w13"] = gu.transpose(1, 0, 2, 4, 3)
    r["e0_w2"] = a["L0_ffn_expert_down"].transpose(1, 0, 2)
    r["e2_router"] = fm(a["L2_ffn_gate_w"])
    w1 = np.concatenate([a["L2_ffn_w1"], a["L2_ffn_sw1"].reshape(2, 176, D)])
    w3 = np.concatenate([a["L2_ffn_w3"], a["L2_ffn_sw3"].reshape(2, 176, D)])
    r["e2_w13"] = np.stack([w1, w3], 1).reshape(18, 2, 176, P, K2).transpose(3, 0, 4, 1, 2)
    w2 = np.concatenate([a["L2_ffn_w2"], a["L2_ffn_sw2"].reshape(D, 2, 176).transpose(1, 0, 2)])
    r["e2_w2"] = w2.reshape(18, D, 2, 88).transpose(3, 0, 2, 1).reshape(88, 36, D)
    r["dr_wba"] = fm(np.concatenate([a["L1_attn_w_beta"], a["L1_attn_w_alpha"]]))
    r["dr_loga"], r["dr_dtb"], r["dr_rms"] = a["L1_attn_log_A"], a["L1_attn_dt_bias"], a["L1_attn_rms_w"].reshape(P, 1)
    i = np.arange(P)
    r["c_tri"] = (i[:, None] <= i[None, :]).astype(np.float32)
    r["c_low"] = (i[:, None] > i[None, :]).astype(np.float32)
    lm = []
    for s in (1, 2, 4, 8, 16, 32, 64):
        same = i[:, None] // (2 * s) == i[None, :] // (2 * s)
        lm.append(same & (i[:, None] % (2 * s) < s) & (i[None, :] % (2 * s) >= s))
    r["c_lmask"] = np.stack(lm, 1).astype(np.float32)
    slots = [0, 1, 2, 3, 0]
    w, cw = a["L1_attn_w_qkv"], a["L1_attn_conv_w"].reshape(4096, 4)
    rows = [np.concatenate([np.arange(256) + 256 * n, 1024 + np.arange(256) + 256 * n, 2048 + np.arange(512) + 512 * n]) for n in slots]
    r["dr_wq"] = np.stack([fm(w[q]) for q in rows])
    r["dr_cw"] = np.stack([cw[q].reshape(8, P, 4).transpose(1, 0, 2) for q in rows])
    r["dr_wg"] = np.stack([fm(a["L1_attn_w_gate"][512 * n:512 * n + 512]) for n in slots])
    r["dr_wo"] = np.stack([a["L1_attn_w_out"][:, 512 * n:512 * n + 512].T.reshape(4, P, D).transpose(1, 0, 2) for n in slots])
    order = np.arange(2048).reshape(8, P, 2).transpose(0, 2, 1).ravel()
    for n in ("gate", "up"):
        r["nv_" + n + "_w"] = a["L1_ffn_" + n + "_W_packed"].T[:, order]
        r["nv_" + n + "_s"] = np.repeat(a["L1_ffn_" + n + "_scales"].T[:, order], 16, axis=0)
    r["nv_down_w"] = a["L1_ffn_down_W_packed"].reshape(D, 8, P).transpose(2, 1, 0).reshape(P, 8 * D)
    r["nv_down_s"] = np.repeat(a["L1_ffn_down_scales"].reshape(D, 8, 8).transpose(2, 1, 0), 16, axis=0).reshape(P, 8 * D)
    for n in "qkv":
        r["la_w" + n] = fm(a["L2_attn_W" + n])
    r["la_wo"] = a["L2_attn_Wo"].T.reshape(K2, P, D).transpose(1, 0, 2)
    r["la_bq"] = a["L2_attn_bq"].reshape(K2, P).T
    r["la_bk"], r["la_bv"], r["la_bo"] = a["L2_attn_bk"], a["L2_attn_bv"], a["L2_attn_bo"]
    r["c_dec"] = np.exp(-np.arange(S, dtype=np.float32) / np.float32(S))
    r["c_dec_col"] = r["c_dec"].reshape(CH, P).T
    r["c_blocks"] = (i[:, None] // 16 == i[None, :] // 16).astype(np.float32)
    rot = (np.arange(64) + 32) % 64
    wa = a["L3_attn_w_kv_a"]
    pe = wa[:, 256:]
    cat = np.concatenate([wa[:, :256], pe, pe, pe[:, rot], pe[:, rot]], 1)
    r["mla_wa"] = fm(cat.T)
    r["mla_qg"] = a["L3_attn_q_a_gamma"].reshape(2, 96).T
    r["mla_kg"] = a["L3_attn_kv_a_gamma"].reshape(64, 1)
    inv = np.float32(1.0) / np.float32(10000.0) ** (np.arange(0, 64, 2, dtype=np.float32) / np.float32(64))
    ang = np.concatenate([np.arange(S, dtype=np.float32)[:, None] * inv] * 2, 1).T
    sign = np.where(np.arange(64) < 32, -1, 1).astype(np.float32)[:, None]
    r["c_cos2"] = np.concatenate([np.cos(ang)] * 2)
    r["c_sin2"] = np.concatenate([np.sin(ang) * sign] * 2)
    wq = a["L3_attn_w_qb"].reshape(2, 96, 16, 192)
    wq = np.concatenate([wq, wq[..., 128 + rot]], -1).reshape(2, 96, 4, 4, 256).transpose(2, 1, 0, 3, 4)
    r["mla_wq"] = wq[slots]
    wkv = a["L3_attn_w_kvb"].reshape(64, 4, 4, 256).transpose(1, 0, 2, 3)[slots]
    r["mla_wk"] = wkv[..., :128]
    r["mla_wv"] = wkv[..., 128:].reshape(5, 64, 512)
    r["mla_wo"] = a["L3_attn_w_o"].reshape(4, 4, P, D).transpose(0, 2, 1, 3)[slots]
    r["c_later"] = np.where(i[None, :] > i[:, None], np.float32(-1e30), np.float32(0))
    r["te_wg"] = fm(a["L3_ffn_Wg"])
    r["te_wa"] = np.stack([fm(a["L3_ffn_W0a"]), fm(a["L3_ffn_W1a"])], 1)
    r["te_wb"] = np.stack([a["L3_ffn_W0b"].T.reshape(4, P, D), a["L3_ffn_W1b"].T.reshape(4, P, D)]).transpose(2, 0, 1, 3)
    r["te_ba"] = np.stack([a["L3_ffn_b0a"].reshape(4, P), a["L3_ffn_b1a"].reshape(4, P)]).transpose(2, 0, 1)
    r["te_bb"] = np.stack([a["L3_ffn_b0b"], a["L3_ffn_b1b"]])
    return r


def kernel(**inputs):
    import concourse.bacc as _bacc
    from concourse.bass_utils import run_bass_kernel_spmd as _run

    nc = _bacc.Bacc("TRN2", target_bir_lowering=False, num_devices=1)
    arrays = {"in_" + k: np.ascontiguousarray(v) for k, v in layouts({k: np.asarray(v) for k, v in inputs.items()}).items()}
    d = {k[3:]: nc.dram_tensor(k, v.shape, mybir.dt.from_np(v.dtype), kind="ExternalInput").ap() for k, v in arrays.items()}
    d["out"] = nc.dram_tensor("out", (P, NT, D), F32, kind="ExternalOutput").ap()
    program(nc, d)
    r = _run(nc, [arrays], core_ids=[0])
    return np.asarray(r.results[0]["out"]).transpose(1, 0, 2).reshape(B, S, D)
```

```python
from contextlib import ExitStack

import concourse.bass as bass
from concourse import mybir
import numpy as np

F32 = mybir.dt.float32
BF16 = mybir.dt.bfloat16
I32 = mybir.dt.int32
ALU = mybir.AluOpType
ACT = mybir.ActivationFunctionType
AX_X = mybir.AxisListType.X

P = 128
B, S, D = 4, 512, 256
CH = S // P
NT = B * CH
K2 = D // P
LN_EPS = 1e-5


def ds(i, n):
    return bass.ds(i, n)


def signals(nc, ctx, prefix, names):
    return {n: ctx.enter_context(nc.semaphore(prefix + "_" + n)) for n in names.split()}


def end_of_iteration(nc, sig):
    nums = sorted(x.num for x in sig.values())
    while nums:
        n = 1
        while n < len(nums) and nums[n] == nums[0] + n:
            n += 1
        nc.gpsimd.sem_clear(range(nums[0], nums[0] + n))
        nums = nums[n:]
    nc.all_engine_barrier()


class Steps:

    def __init__(self, eng, sem):
        self.eng, self.sem, self.n = eng, sem, 0

    def mark(self, ins):
        ins.then_inc(self.sem, 1)
        self.n += 1
        return self.n

    def wait(self):
        self.eng.wait_ge(self.sem, self.n)

    def link(self, ins):
        self.mark(ins)
        self.wait()


def log1p_small(dve, st, e, h):
    st.link(dve.tensor_scalar(h, e, -0.25, None, ALU.mult))
    for c in (1.0 / 3.0, -0.5, 1.0):
        st.link(dve.scalar_tensor_tensor(out=h, in0=h, scalar=c, in1=e, op0=ALU.add, op1=ALU.mult))


def log1p_join(dve, st, e, w, ln_w, h):
    st.link(dve.scalar_tensor_tensor(out=w, in0=w, scalar=1.0, in1=e, op0=ALU.subtract, op1=ALU.subtract))
    st.link(dve.tensor_tensor(w, ln_w, w, ALU.subtract))
    st.link(dve.tensor_tensor(w, w, h, ALU.subtract))
    st.link(dve.scalar_tensor_tensor(out=w, in0=e, scalar=1.0 / 64.0, in1=w, op0=ALU.is_ge, op1=ALU.mult))
    st.link(dve.tensor_tensor(h, h, w, ALU.add))


def fetch(nc, sig, name, pairs):
    with nc.Block() as block:
        @block.sync
        def _(sp):
            for dst, src in pairs:
                sp.dma_start(dst, src).then_inc(sig[name], 16)
    return 16 * len(pairs)


def arrive(nc, sig, name, total):
    with nc.Block() as block:
        @block.sync
        def _(sp):
            sp.wait_ge(sig[name], total)
    end_of_iteration(nc, sig)


def load(nc, sig, name, pairs, meanwhile=None):
    total = fetch(nc, sig, name, pairs)
    if meanwhile:
        meanwhile()
    arrive(nc, sig, name, total)


def bc(ap, dim, n):
    shape = list(ap.shape)
    return ap.unsqueeze(dim).to_broadcast(shape[:dim] + [n] + shape[dim:])


def layer_norm(nc, g):
    with ExitStack() as ctx:
        sb = lambda n, s, t=F32: ctx.enter_context(nc.sbuf_tensor("ln%d_" % g["layer"] + n, s, t))
        st, mv = sb("st", [P, NT, 6]), sb("mv", [P, NT, 2])
        std, rstd, r2, xn = sb("std", [P, NT]), sb("rstd", [P, NT]), sb("r2", [P, NT]), sb("xn", [P, NT, D])
        sig = g["ln_sig"]
        x, xn_fm, ident, ps, eps = g["x"], g["xn_fm"], g["ident"], g["ps"], g["eps"]
        with nc.Block() as block:
            @block.vector
            def _(dve):
                for t in range(NT):
                    dve.bn_stats(st[:, t, :], x[:, t, :]).then_inc(sig["stats"], 1)
                    if t >= 1:
                        dve.wait_ge(sig["stats"], t)
                        dve.bn_aggr(mv[:, t - 1, :], st[:, t - 1, :]).then_inc(sig["meanvar"], 1)
                dve.wait_ge(sig["stats"], NT)
                dve.bn_aggr(mv[:, NT - 1, :], st[:, NT - 1, :]).then_inc(sig["meanvar"], 1)
                dve.wait_ge(sig["std"], 1)
                so = Steps(dve, sig["rstd"])
                so.link(dve.reciprocal(rstd[:], std[:]))
                so.link(dve.tensor_tensor(r2[:], rstd[:], rstd[:], ALU.mult))
                so.link(dve.scalar_tensor_tensor(out=r2[:], in0=mv[:, :, 1], scalar=LN_EPS, in1=r2[:], op0=ALU.add, op1=ALU.mult))
                so.link(dve.tensor_scalar(r2[:], r2[:], -0.5, 1.5, ALU.mult, ALU.add))
                so.link(dve.tensor_tensor(rstd[:], rstd[:], r2[:], ALU.mult))
                for t in range(NT):
                    dve.tensor_scalar(xn[:, t, :], x[:, t, :], mv[:, t, 0:1], rstd[:, t:t + 1], ALU.subtract, ALU.mult
                                      ).then_inc(sig["xn"], 1)

            @block.tensor
            def _(pe):
                for t in range(NT):
                    b, c = t // CH, t % CH
                    pe.wait_ge(sig["xn"], t + 1)
                    for k in range(K2):
                        last = pe.transpose(ps[2 * b + k][:, c * P:(c + 1) * P], xn[:, t, k::2], ident[:])
                    if c == CH - 1:
                        last.then_inc(sig["turned"], 1)

            @block.scalar
            def _(act):
                act.wait_ge(sig["meanvar"], NT)
                act.activation(std[:], mv[:, :, 1], ACT.Sqrt, bias=eps[:, 0:1]).then_inc(sig["std"], 1)
                for b in range(B):
                    act.wait_ge(sig["turned"], b + 1)
                    for k in range(K2):
                        act.activation(xn_fm[:, k, b * S:(b + 1) * S], ps[2 * b + k][:], ACT.Copy)
        end_of_iteration(nc, sig)


def gates_of_row(act, sig, gate, tile, ready):
    for t in range(CH):
        ready(t)
        act.activation(gate[:, t, :], tile(t), ACT.Silu).then_inc(sig["up_silu"], 1)


def update_of_row(dve, g, sig, gate, b):
    x, s = g["x"], g["s"]
    for t in range(CH):
        dve.wait_ge(sig["up_silu"], t + 1)
        dve.tensor_tensor(gate[:, t, :], gate[:, t, :], s[:, ds(b * CH + t, 1), :].squeeze(1), ALU.mult).then_inc(sig["up_sg"], 1)
    for t in range(CH):
        xt = x[:, ds(b * CH + t, 1), :].squeeze(1)
        dve.wait_ge(sig["up_sg"], t + 1)
        dve.tensor_tensor(xt, xt, gate[:, t, :], ALU.add)


def mamba(nc, g, d):
    NS, R = 16, 64
    M = R + 2 * NS
    with ExitStack() as ctx:
        sb = lambda n, s, t=F32: ctx.enter_context(nc.sbuf_tensor("ma_" + n, s, t))
        sig = signals(nc, ctx, "ma", "load xb xp_ps xp dt_ps az ez w lz rz dt u b_bc c_bc da dbx h hc y_used y yd turned order")
        wx, wdt = sb("wx", [P, K2, M]), sb("wdt", [R, K2, P])
        bdt, na, dp = sb("bdt", [P, K2]), sb("na", [P, K2, NS]), sb("dp", [P, K2])
        xb, xp, az, rz = sb("xb", [P, K2, S]), sb("xp", [M, S]), sb("az", [P, K2, S]), sb("rz", [P, K2, S])
        dt, u = sb("dt", [P, K2, S]), sb("u", [P, K2, S])
        da, dbx, h, hc = sb("da", [P, 4, S]), sb("dbx", [P, 2, S]), sb("h", [P, 2, S]), sb("hc", [P, 4, S])
        yd, wz, lz = sb("yd", [P, K2, S]), sb("wz", [P, K2, S]), sb("lz", [P, K2, S])
        ps, ident, xn_fm, s_out = g["ps"], g["ident"], g["xn_fm"], g["s"]
        load(nc, sig, "load", [(wx[:], d["ma_wx"]), (wdt[:], d["ma_wdt"]), (bdt[:], d["ma_bdt"]),
                               (na[:], d["ma_alog"]), (dp[:], d["ma_d"])], lambda: layer_norm(nc, g))
        with nc.Block() as block:
            @block.scalar
            def _(act):
                act.activation(na[:], na[:], ACT.Exp).then_inc(sig["order"], 1)
                act.wait_ge(sig["order"], 1)
                act.mul(na[:], na[:], -1.0)
        end_of_iteration(nc, sig)
        y_ps = [ps[1], ps[2]]
        with nc.Fori(0, B) as b:
            with nc.Block() as block:
                @block.tensor
                def _(pe):
                    pe.wait_ge(sig["xb"], 1)
                    for k in range(K2):
                        last = pe.matmul(ps[0][0:M, :], wx[:, k, :], xb[:, k, :], start=(k == 0), stop=(k == K2 - 1))
                    last.then_inc(sig["xp_ps"], 1)
                    pe.wait_ge(sig["xp"], 1)
                    for k in range(K2):
                        pe.matmul(y_ps[k][:], wdt[:, k, :], xp[0:R, :], start=True, stop=True).then_inc(sig["dt_ps"], 1)

                    def reduce(n):
                        for k in range(K2):
                            i = K2 * n + k
                            pe.wait_ge(sig["hc"], i + 1)
                            if n == 0:
                                pe.wait_ge(sig["rz"], k + 1)
                            pe.matmul(y_ps[k][:], ident[:], hc[:, i % 4, :], start=(n == 0), stop=(n == NS - 1)
                                      ).then_inc(sig["y_used"], 1)

                    for n in range(NS):
                        if n >= 2:
                            pe.wait_ge(sig["hc"], K2 * (n - 1))
                        for what, row, bank in (("b_bc", R, 3), ("c_bc", R + NS, 5)):
                            pe.matmul(ps[bank + n % 2][:], ident[0:M, row + n:row + n + 1].to_broadcast([M, P]), xp[:],
                                      start=True, stop=True).then_inc(sig[what], 1)
                        if n >= 1:
                            reduce(n - 1)
                    reduce(NS - 1)
                    for k in range(K2):
                        pe.wait_ge(sig["yd"], k + 1)
                        for t in range(CH):
                            last = pe.transpose(ps[3 + k][:, t * P:(t + 1) * P], yd[:, k, t * P:(t + 1) * P], ident[:])
                        last.then_inc(sig["turned"], 1)

                @block.scalar
                def _(act):
                    act.preload_act_table_set("natural_log_exp_and_others")
                    act.activation(xb[:], xn_fm[:, :, ds(b * S, S)], ACT.Copy).then_inc(sig["xb"], 1)
                    act.wait_ge(sig["xp_ps"], 1)
                    act.activation(xp[:], ps[0][0:M, :], ACT.Copy).then_inc(sig["xp"], 1)
                    for k in range(K2):
                        act.wait_ge(sig["dt_ps"], k + 1)
                        act.activation(az[:, k, :], y_ps[k][:], ACT.Abs, bias=bdt[:, k:k + 1]).then_inc(sig["az"], 1)
                        act.wait_ge(sig["az"], k + 1)
                        act.activation(az[:, k, :], az[:, k, :], ACT.Exp, scale=-1.0).then_inc(sig["ez"], 1)
                        act.wait_ge(sig["w"], k + 1)
                        act.activation(lz[:, k, :], wz[:, k, :], ACT.Ln).then_inc(sig["lz"], 1)
                    for i in range(K2 * NS):
                        n, k = i // K2, i % K2
                        if n == 0:
                            act.wait_ge(sig["dt"], k + 1)
                        if i >= 4:
                            act.wait_ge(sig["h"], i - 3)
                        act.activation(da[:, i % 4, :], dt[:, k, :], ACT.Exp, scale=na[:, k, n:n + 1]).then_inc(sig["da"], 1)
                    for k in range(K2):
                        act.wait_ge(sig["turned"], k + 1)
                        act.activation(s_out[:, ds(b * CH, CH), k::2],
                                       ps[3 + k][:].rearrange("p (t f) -> p t f", t=CH), ACT.Copy)

                @block.vector
                def _(dve):
                    st = Steps(dve, sig["order"])
                    for k in range(K2):
                        dve.wait_ge(sig["az"], k + 1)
                        dve.tensor_scalar(rz[:, k, :], y_ps[k][:], bdt[:, k:k + 1], 0.0, ALU.add, ALU.max).then_inc(sig["rz"], 1)
                        dve.wait_ge(sig["ez"], k + 1)
                        dve.tensor_scalar(wz[:, k, :], az[:, k, :], 1.0, None, ALU.add).then_inc(sig["w"], 1)
                        dve.wait_ge(sig["w"], k + 1)
                        log1p_small(dve, st, az[:, k, :], dt[:, k, :])
                    for k in range(K2):
                        dve.wait_ge(sig["lz"], k + 1)
                        log1p_join(dve, st, az[:, k, :], wz[:, k, :], lz[:, k, :], dt[:, k, :])
                        dve.tensor_tensor(dt[:, k, :], dt[:, k, :], rz[:, k, :], ALU.add).then_inc(sig["dt"], 1)
                    dve.wait_ge(sig["xb"], 1)
                    for k in range(K2):
                        dve.wait_ge(sig["dt"], k + 1)
                        dve.tensor_tensor(u[:, k, :], dt[:, k, :], xb[:, k, :], ALU.mult).then_inc(sig["u"], 1)

                    def drive(i):
                        n, k = i // K2, i % K2
                        dve.wait_ge(sig["b_bc"], n + 1)
                        if n == 0:
                            dve.wait_ge(sig["u"], k + 1)
                        if i >= 2:
                            dve.wait_ge(sig["h"], i - 1)
                        dve.tensor_tensor(dbx[:, i % 2, :], u[:, k, :], ps[3 + n % 2][:], ALU.mult).then_inc(sig["dbx"], 1)

                    def read_out(i):
                        n = i // K2
                        dve.wait_ge(sig["c_bc"], n + 1)
                        dve.wait_ge(sig["h"], i + 1)
                        if i >= 4:
                            dve.wait_ge(sig["y_used"], i - 3)
                        dve.tensor_tensor(hc[:, i % 4, :], h[:, i % 2, :], ps[5 + n % 2][:], ALU.mult).then_inc(sig["hc"], 1)

                    for i in range(K2 * NS):
                        drive(i)
                        if i >= 1:
                            read_out(i - 1)
                        dve.wait_ge(sig["da"], i + 1)
                        dve.wait_ge(sig["dbx"], i + 1)
                        if i >= 2:
                            dve.wait_ge(sig["hc"], i - 1)
                        dve.tensor_tensor_scan(h[:, i % 2, :], da[:, i % 4, :], dbx[:, i % 2, :], 0.0, ALU.mult, ALU.add
                                               ).then_inc(sig["h"], 1)
                    read_out(K2 * NS - 1)
                    for k in range(K2):
                        dve.wait_ge(sig["y_used"], K2 * (NS - 1) + k + 1)
                        dve.scalar_tensor_tensor(out=yd[:, k, :], in0=xb[:, k, :], scalar=dp[:, k:k + 1], in1=y_ps[k][:],
                                                 op0=ALU.mult, op1=ALU.add).then_inc(sig["yd"], 1)
            end_of_iteration(nc, sig)


def expert_weights(nc, ctx, d, name, E, M, shared, packed):
    NE = E + shared
    sb = lambda n, s, t=F32: ctx.enter_context(nc.sbuf_tensor(name + "_" + n, s, t))
    sem = {"weights": ctx.enter_context(nc.semaphore(name + "_weights"))}
    router = sb("router", [P, K2, E])
    NU, LAST = -(-NE * M // P), (NE * M - 1) % P + 1
    w13 = sb("w13", [P, K2, 2, NE * M], BF16 if packed else F32)
    w2 = sb("w2", [P, NU, D], BF16 if packed else F32)
    pairs = [(router[:], d[name + "_router"]), (w13[:], d[name + "_w13"])]
    if not packed:
        total = fetch(nc, sem, "weights", pairs + [(w2[:], d[name + "_w2"])])
        return sem, total, router, w13, w2, None
    owner = sb("owner", [3 * 32, NE * M])
    total = fetch(nc, sem, "weights", pairs + [(w2[:, 0:NU - 1, :], d[name + "_w2"]), (w2[0:LAST, NU - 1, :], d[name + "_w2_last"]),
                                               (owner[:], d["c_owner"])])
    return sem, total, router, w13, w2, owner


def experts(nc, g, d, name, E, M, shared, packed, weights):
    NE = E + shared
    W = 16 if E == 8 else 24
    with ExitStack() as ctx:
        sb = lambda n, s, t=F32: ctx.enter_context(nc.sbuf_tensor(name + "_" + n, s, t))
        sig = signals(nc, ctx, name, "xb part lg top neg score w a b act h down acc wt_ps wt_rest wt wb hm high r1 mid r2 parts up_silu up_sg order")
        sem, total, router, w13, w2, owner = weights
        xb = sb("xb", [P, K2, S])
        part = sb("part", [P, 3, K2, S], BF16) if packed else None
        rest = sb("rest", [P, K2, S]) if packed else None
        if packed:
            NE_P = 32
            wt, wt3 = sb("wt", [NE, S]), sb("wt3", [3 * NE_P, S], BF16)
            ownerb = sb("ownerb", [3 * NE_P, NE * M], BF16)
            hp = sb("hp", [P, 3, 3, S], BF16)
        vals, rep, mr = sb("vals", [P, CH, W]), sb("rep", [P, CH, 8]), sb("mr", [P, CH, W])
        m8, nm, ssum = sb("m8", [P, CH, 8]), sb("nm", [P, CH]), sb("ssum", [P, CH])
        w = sb("w", [P, CH, NE])
        sg, h = sb("sg", [P, 2, S]), sb("h", [P, 2, S])
        acc, gate = sb("acc", [P, CH, D]), sb("gate", [P, CH, D])
        ps, xn_fm, ident = g["ps"], g["xn_fm"], g["ident"]
        NU, LAST = -(-NE * M // P), (NE * M - 1) % P + 1
        LAG = 2 if packed else 1
        rows = lambda u: LAST if u == NU - 1 else P
        arrive(nc, sem, "weights", total)
        with nc.Block() as block:
            @block.vector
            def _(dve):
                dve.memset(vals[:], -1.0)
                dve.memset(rep[:], -1.0)
                dve.memset(w[:], 1.0)
                if packed:
                    dve.memset(wt3[:], 0.0)
                    dve.tensor_copy(ownerb[:], owner[:])
        end_of_iteration(nc, sig)
        with nc.Fori(0, B) as b:
            with nc.Block() as block:
                @block.tensor
                def _(pe):
                    def scores():
                        pe.wait_ge(sig["xb"], 1)
                        for t in range(CH):
                            for k in range(K2):
                                last = pe.matmul(ps[7][:, t * E:(t + 1) * E], xb[:, k, t * P:(t + 1) * P], router[:, k, :],
                                                 start=(k == 0), stop=(k == K2 - 1))
                        last.then_inc(sig["lg"], 1)

                    def up(u):
                        if u >= 2:
                            pe.wait_ge(sig["h"], u - 1)
                        for n, what in ((0, "a"), (1, "b")):
                            out = ps[2 * (u % 2) + n][0:rows(u), :]
                            cols = slice(u * P, u * P + rows(u))
                            if packed:
                                if u == 0 and n == 0:
                                    pe.wait_ge(sig["part"], 3)
                                terms = [(w13[:, k, n, cols], part[:, q, k, :]) for q in (2, 1, 0) for k in range(K2)]
                            else:
                                terms = [(w13[:, k, n, cols], xn_fm[:, k, ds(b * S, S)]) for k in range(K2)]
                            for q, (l, r) in enumerate(terms):
                                last = pe.matmul(out, l, r, start=(q == 0), stop=(q == len(terms) - 1))
                            last.then_inc(sig[what], 1)

                    def turn_gates():
                        pe.wait_ge(sig["w"], CH)
                        for t in range(CH):
                            last = pe.transpose(ps[7][0:NE, t * P:(t + 1) * P], w[:, t, :], ident[:])
                        last.then_inc(sig["wt_ps"], 1)

                    def spread(u):
                        if u < 2:
                            pe.wait_ge(sig["wt"], 1)
                        else:
                            pe.wait_ge(sig["h"], u - 1)
                        pe.matmul(ps[6 + u % 2][0:rows(u), :], ownerb[:, u * P:u * P + rows(u)], wt3[:], start=True, stop=True
                                  ).then_inc(sig["wb"], 1)

                    def down(u):
                        pe.wait_ge(sig["parts" if packed else "h"], u + 1)
                        if not packed:
                            if u >= 2:
                                pe.wait_ge(sig["acc"], CH * (u - 1))
                            if u == 1:
                                pe.wait_ge(sig["w"], CH)
                        for t in range(CH):
                            bank = 4 + t // 2 if packed else 4 + 2 * (u % 2) + t // 2
                            tt = slice(t * P, (t + 1) * P)
                            parts = [hp[0:rows(u), u % 3, q, tt] for q in (2, 1, 0)] if packed else [h[0:rows(u), u % 2, tt]]
                            for n, part_ in enumerate(parts):
                                last = pe.matmul(ps[bank][:, (t % 2) * D:(t % 2 + 1) * D], part_, w2[0:rows(u), u, :],
                                                 start=((u == 0 or not packed) and t % 2 == 0 and n == 0),
                                                 stop=((u == NU - 1 or not packed) and n == len(parts) - 1), skip_group_check=True)
                        last.then_inc(sig["down"], 1)

                    if packed:
                        scores()
                    for u in range(NU):
                        up(u)
                        if not packed and u == 0:
                            scores()
                        if packed and u == 1:
                            turn_gates()
                            spread(0)
                        if packed and u >= 1:
                            spread(u)
                        if u >= LAG:
                            down(u - LAG)
                    for u in range(NU - LAG, NU):
                        down(u)

                @block.scalar
                def _(act):
                    act.activation(xb[:], xn_fm[:, :, ds(b * S, S)], ACT.Copy).then_inc(sig["xb"], 1)
                    if shared:
                        act.wait_ge(sig["lg"], 1)
                        act.activation(vals[:, :, 0:E], ps[7][:, 0:CH * E].rearrange("p (t e) -> p t e", t=CH), ACT.Sigmoid
                                       ).then_inc(sig["score"], 1)
                    else:
                        act.wait_ge(sig["neg"], 1)
                        for t in range(CH):
                            act.activation(vals[:, t, 0:E], ps[7][:, t * E:(t + 1) * E], ACT.Exp, bias=nm[:, t:t + 1]
                                           ).then_inc(sig["score"], 1)

                    def to_part(u, q):
                        act.wait_ge(sig[("h", "r1", "r2")[q]], u + 1)
                        if q == 0 and u >= 3:
                            act.wait_ge(sig["down"], u - 2)
                        act.activation(hp[0:rows(u), u % 3, q, :], h[0:rows(u), u % 2, :], ACT.Copy
                                       ).then_inc(sig[("high", "mid", "parts")[q]], 1)

                    for u in range(NU):
                        if packed and u == 0:
                            act.wait_ge(sig["wt_ps"], 1)
                            act.activation(wt[:], ps[7][0:NE, :], ACT.Copy).then_inc(sig["wt_rest"], 1)
                        act.wait_ge(sig["a"], u + 1)
                        if u >= 2:
                            act.wait_ge(sig["h"], u - 1)
                        act.activation(sg[0:rows(u), u % 2, :], ps[2 * (u % 2)][0:rows(u), :], ACT.Silu).then_inc(sig["act"], 1)
                        if packed:
                            if u >= 1:
                                to_part(u - 1, 1)
                            to_part(u, 0)
                            if u >= 1:
                                to_part(u - 1, 2)
                    if packed:
                        to_part(NU - 1, 1)
                        to_part(NU - 1, 2)
                    if packed:
                        gates_of_row(act, sig, gate, lambda t: ps[4 + t // 2][:, (t % 2) * D:(t % 2 + 1) * D],
                                     lambda t: act.wait_ge(sig["down"], NU))
                    else:
                        gates_of_row(act, sig, gate, lambda t: acc[:, t, :], lambda t: act.wait_ge(sig["acc"], CH * (NE - 1) + t + 1))

                @block.vector
                def _(dve):
                    st = Steps(dve, sig["order"])
                    if packed:
                        for q in range(3):
                            src = xn_fm[:, :, ds(b * S, S)] if q == 0 else rest[:]
                            dve.tensor_copy(part[:, q, :, :], src).then_inc(sig["part"], 1)
                            if q < 2:
                                dve.wait_ge(sig["part"], q + 1)
                                st.link(dve.tensor_tensor(rest[:], src, part[:, q, :, :], ALU.subtract))
                    else:
                        dve.wait_ge(sig["lg"], 1)
                        for t in range(CH):
                            dve.max(m8[:, t, :], ps[7][:, t * E:(t + 1) * E]).then_inc(sig["top"], 1)
                        dve.wait_ge(sig["top"], CH)
                        dve.tensor_scalar(nm[:], m8[:, :, 0], -1.0, None, ALU.mult).then_inc(sig["neg"], 1)
                    dve.wait_ge(sig["score"], 1 if shared else CH)
                    if not shared:
                        dve.wait_ge(sig["neg"], 1)
                    for t in range(CH):
                        last = dve.max(m8[:, t, :], vals[:, t, 0:E])
                    st.link(last)
                    st.mark(dve.tensor_copy(rep[:, :, 0:2], m8[:, :, 0:2]))
                    st.link(dve.tensor_tensor(ssum[:], m8[:, :, 0], m8[:, :, 1], ALU.add))
                    st.link(dve.reciprocal(ssum[:], ssum[:]))
                    for t in range(CH):
                        last = dve.match_replace(out=mr[:, t, :], in_to_replace=rep[:, t, :], in_values=vals[:, t, :], imm_value=-2.0)
                    st.link(last)
                    for t in range(CH):
                        st.mark(dve.scalar_tensor_tensor(out=mr[:, t, 0:E], in0=mr[:, t, 0:E], scalar=-1.5, in1=vals[:, t, 0:E],
                                                         op0=ALU.is_lt, op1=ALU.mult))
                    st.wait()
                    for t in range(CH):
                        dve.tensor_scalar(w[:, t, 0:E], mr[:, t, 0:E], ssum[:, t:t + 1], None, ALU.mult).then_inc(sig["w"], 1)
                    dve.wait_ge(sig["w"], CH)

                    def add(e):
                        dve.wait_ge(sig["down"], e + 1)
                        for t in range(CH):
                            y = ps[4 + 2 * (e % 2) + t // 2][:, (t % 2) * D:(t % 2 + 1) * D]
                            if e == 0:
                                dve.tensor_scalar(acc[:, t, :], y, w[:, t, 0:1], None, ALU.mult).then_inc(sig["acc"], 1)
                            else:
                                dve.wait_ge(sig["acc"], CH * (e - 1) + t + 1)
                                dve.scalar_tensor_tensor(out=acc[:, t, :], in0=y, scalar=w[:, t, e:e + 1], in1=acc[:, t, :],
                                                         op0=ALU.mult, op1=ALU.add).then_inc(sig["acc"], 1)

                    def leave(u, q):
                        hu = h[0:rows(u), u % 2, :]
                        dve.wait_ge(sig[("high", "mid")[q]], u + 1)
                        dve.tensor_tensor(hu, hu, hp[0:rows(u), u % 3, q, :], ALU.subtract).then_inc(sig[("r1", "r2")[q]], 1)

                    if packed:
                        dve.wait_ge(sig["wt_rest"], 1)
                        for q in range(3):
                            p3 = wt3[q * NE_P:q * NE_P + NE, :]
                            if q < 2:
                                st.link(dve.tensor_copy(p3, wt[:]))
                                st.link(dve.tensor_tensor(wt[:], wt[:], p3, ALU.subtract))
                            else:
                                dve.tensor_copy(p3, wt[:]).then_inc(sig["wt"], 1)
                    for u in range(NU):
                        dve.wait_ge(sig["act"], u + 1)
                        dve.wait_ge(sig["b"], u + 1)
                        if u >= 2:
                            dve.wait_ge(sig["parts" if packed else "down"], u - 1)
                        hu = h[0:rows(u), u % 2, :]
                        ins = dve.tensor_tensor(hu, sg[0:rows(u), u % 2, :], ps[2 * (u % 2) + 1][0:rows(u), :], ALU.mult)
                        if packed:
                            ins.then_inc(sig["hm"], 1)
                            dve.wait_ge(sig["hm"], u + 1)
                            dve.wait_ge(sig["wb"], u + 1)
                            ins = dve.tensor_tensor(hu, hu, ps[6 + u % 2][0:rows(u), :], ALU.mult)
                        ins.then_inc(sig["h"], 1)
                        if packed:
                            if u >= 1:
                                leave(u - 1, 1)
                            leave(u, 0)
                        if not packed and u >= 1:
                            add(u - 1)
                    if packed:
                        leave(NU - 1, 1)
                    else:
                        add(NE - 1)
                    update_of_row(dve, g, sig, gate, b)
            end_of_iteration(nc, sig)


def delta_rule(nc, g, d):
    HV, HG, KG = 16, 4, 2
    NG = HV // HG
    CT = 2 * KG + HG
    LEAST = float(np.exp(-30.0))
    LV = 7
    HC = P // 2
    with ExitStack() as ctx:
        sb = lambda n, s, t=F32: ctx.enter_context(nc.sbuf_tensor("dr_" + n, s, t))
        pre = signals(nc, ctx, "dp", "load xb z az ez w lz r sp be order")
        sig = signals(nc, ctx, "dr", "wnext proj tap0 conv silu gate sq ss rn norm kt_ps kt vt_ps vt lam d_ps kk_ps kq_ps e_row g l0 a0 "
                                     "dcol l a kg eye w_ps w dy_ps xt_ps xt xy ks r u_ps u qs o_ps o1 osq oss orn o3 kd dst s y_ps y order porder")
        wba, wq, cw = sb("wba", [P, K2, 2 * HV]), sb("wq", [P, K2, CT * P]), sb("cw", [P, CT, 4])
        wg, wo = sb("wg", [P, K2, HG * P]), sb("wo", [P, HG, D])
        na, dtb, rw = sb("na", [P, HV]), sb("dtb", [P, HV]), sb("rw", [P, 1])
        tri, low, lmask = sb("tri", [P, P]), sb("low", [P, P]), sb("lmask", [P, LV, HC])
        la_all, be_all = sb("la_all", [P, B * NG, CH * HG]), sb("be_all", [P, B * NG, CH * HG])
        la, be, nb = sb("la", [P, CH * HG]), sb("be", [P, CH * HG]), sb("nb", [P, CH * HG])
        qb = sb("qb", [P, 1])
        with ExitStack() as c2:
            tb = lambda n, s, t=F32: c2.enter_context(nc.sbuf_tensor("dp_" + n, s, t))
            z, az, w, r = (tb(n, [P, NT, 2 * HV]) for n in ("z", "az", "w", "r"))
            lp = tb("lp", [P, NT, HV])
            ps, xn_fm, s_out, ident, ones = g["ps"], g["xn_fm"], g["s"], g["ident"], g["ones"]
            load(nc, pre, "load", [(wba[:], d["dr_wba"]), (na[:], d["dr_loga"].partition_broadcast(P)),
                                   (dtb[:], d["dr_dtb"].partition_broadcast(P)), (rw[:], d["dr_rms"]),
                                   (tri[:], d["c_tri"]), (low[:], d["c_low"]), (lmask[:], d["c_lmask"]),
                                   (wq[:], d["dr_wq"][0]), (cw[:], d["dr_cw"][0]), (wg[:], d["dr_wg"][0]), (wo[:], d["dr_wo"][0])],
                 lambda: layer_norm(nc, g))
            with nc.Block() as block:
                @block.scalar
                def _(act):
                    act.activation(na[:], na[:], ACT.Exp).then_inc(pre["order"], 1)
                    act.wait_ge(pre["order"], 1)
                    act.mul(na[:], na[:], -1.0)

                @block.vector
                def _(dve):
                    dve.memset(qb[:], float(-0.5 * np.log(128.0)))
            end_of_iteration(nc, pre)
            with nc.Block() as block:
                @block.scalar
                def _(act):
                    act.preload_act_table_set("natural_log_exp_and_others")
                    act.wait_ge(pre["z"], 1)
                    act.activation(az[:, :, 0:HV], z[:, :, 0:HV], ACT.Exp, scale=-1.0).then_inc(pre["az"], 1)
                    act.activation(az[:, :, HV:], z[:, :, HV:], ACT.Abs).then_inc(pre["az"], 1)
                    act.wait_ge(pre["az"], 2)
                    act.activation(az[:, :, HV:], az[:, :, HV:], ACT.Exp, scale=-1.0).then_inc(pre["ez"], 1)
                    act.wait_ge(pre["w"], 1)
                    act.activation(z[:, :, HV:], w[:, :, HV:], ACT.Ln).then_inc(pre["lz"], 1)

                @block.tensor
                def _(pe):
                    for t in range(NT):
                        for k in range(K2):
                            last = pe.matmul(ps[0][:, t * 2 * HV:(t + 1) * 2 * HV], xn_fm[:, k, t * P:(t + 1) * P], wba[:, k, :],
                                             start=(k == 0), stop=(k == K2 - 1))
                    last.then_inc(pre["sp"], 1)

                @block.vector
                def _(dve):
                    st = Steps(dve, pre["order"])
                    dve.wait_ge(pre["sp"], 1)
                    zp = ps[0][:, 0:NT * 2 * HV].rearrange("p (t f) -> p t f", t=NT)
                    st.mark(dve.tensor_copy(z[:, :, 0:HV], zp[:, :, 0:HV]))
                    dve.tensor_tensor(z[:, :, HV:], zp[:, :, HV:], bc(dtb[:], 1, NT), ALU.add).then_inc(pre["z"], 1)
                    dve.wait_ge(pre["z"], 1)
                    dve.tensor_scalar(r[:, :, HV:], z[:, :, HV:], 0.0, None, ALU.max).then_inc(pre["r"], 1)
                    dve.wait_ge(pre["ez"], 1)
                    dve.tensor_scalar(w[:], az[:], 1.0, None, ALU.add).then_inc(pre["w"], 1)
                    dve.wait_ge(pre["w"], 1)
                    st.mark(dve.reciprocal(r[:, :, 0:HV], w[:, :, 0:HV]))
                    log1p_small(dve, st, az[:, :, HV:], lp[:])
                    dve.wait_ge(pre["lz"], 1)
                    log1p_join(dve, st, az[:, :, HV:], w[:, :, HV:], z[:, :, HV:], lp[:])
                    st.link(dve.tensor_tensor(r[:, :, HV:], r[:, :, HV:], lp[:], ALU.add))
                    for b in range(B):
                        for n in range(NG):
                            h0, tt = n * HG, slice(b * CH, (b + 1) * CH)
                            dve.tensor_copy(be_all[:, b * NG + n, :].rearrange("p (c h) -> p c h", h=HG), r[:, tt, h0:h0 + HG])
                            dve.tensor_tensor(la_all[:, b * NG + n, :].rearrange("p (c h) -> p c h", h=HG),
                                              r[:, tt, HV + h0:HV + h0 + HG], bc(na[:, h0:h0 + HG], 1, CH), ALU.mult)
            end_of_iteration(nc, pre)
        with nc.Block() as block:
            @block.vector
            def _(dve):
                dve.memset(s_out[:], 0.0)
        end_of_iteration(nc, pre)

        qkv, gt = sb("qkv", [P, CT, S]), sb("gt", [P, HG, S])
        sq = sb("sq", [P, 2, S])
        ktok, vtok = sb("ktok", [P, CH, KG, P]), sb("vtok", [P, CH, HG, P])
        lam = sb("lam", [P, 2, HG, P])
        A, G, Y, kg, qg = (sb(n, [P, CH, HG, P]) for n in ("A", "G", "Y", "kg", "qg"))
        L, X = sb("L", [P, CH, HG, P]), sb("X", [P, 2, HG, P])
        W = sb("W", [P, 2, HG, HC])
        dcol = sb("dcol", [P, CH, HG])
        R, U, kd, state = (sb(n, [P, HG, P]) for n in ("R", "U", "kd", "state"))
        o, osq = sb("o", [P, HG, P]), sb("osq", [P, HG * P])
        eps = g["eps6"]
        h4 = lambda ap: ap.rearrange("p (h n) -> p h n", h=HG)
        flat = lambda ap: ap.rearrange("p h n -> p (h n)")
        NQ = 2 * LV
        NX = 2 * (LV - 1)

        def second(ap, s):
            ap = ap.rearrange("p (b two n) -> p b two n", two=2, n=1 << s) if len(ap.shape) == 2 else \
                ap.rearrange("p h (b two n) -> p h b two n", two=2, n=1 << s)
            return ap[:, :, 1, :] if len(ap.shape) == 4 else ap[:, :, :, 1, :]

        def blocks(ap, s):
            return ap.rearrange("p (b n) -> p b n", n=1 << s) if len(ap.shape) == 2 else ap.rearrange("p h (b n) -> p h b n", n=1 << s)

        part_rows = lambda s: P if s < LV - 1 else HC
        half = lambda bank: bank[:, 0:HG * HC].rearrange("p (h n) -> p h n", h=HG)
        QK = 2 * KG
        build_banks = lambda c: ps[4:8] if c else ps[0:4]
        oss_bank = lambda c: 7 if c < 2 else 0
        y_bank = lambda c: 6 if c < 2 else 1
        bank_v, bank_kt, bank_vt = (lambda n: 4 + n), (lambda n: 4 + n), (lambda c: 4 + (c + 2) % 4)

        with nc.Fori(0, B) as b:
            with nc.Fori(0, NG) as gi:
                with nc.Block() as block:
                    @block.sync
                    def _(sp):
                        sp.wait_ge(sig["proj"], CT + HG)
                        sp.dma_start(wq[:], d["dr_wq"][ds(gi + 1, 1)].squeeze(0)).then_inc(sig["wnext"], 16)
                        sp.dma_start(wg[:], d["dr_wg"][ds(gi + 1, 1)].squeeze(0)).then_inc(sig["wnext"], 16)
                        sp.wait_ge(sig["conv"], CT)
                        sp.dma_start(cw[:], d["dr_cw"][ds(gi + 1, 1)].squeeze(0)).then_inc(sig["wnext"], 16)
                        sp.wait_ge(sig["y_ps"], CH)
                        sp.dma_start(wo[:], d["dr_wo"][ds(gi + 1, 1)].squeeze(0)).then_inc(sig["wnext"], 16)
                        sp.wait_ge(sig["wnext"], 64)

                    @block.tensor
                    def _(pe):
                        def project(i, bank):
                            for k in range(K2):
                                w_ = wq[:, k, i * P:(i + 1) * P] if i < CT else wg[:, k, (i - CT) * P:(i - CT + 1) * P]
                                last = pe.matmul(ps[bank][:], w_, xn_fm[:, k, ds(b * S, S)], start=(k == 0), stop=(k == K2 - 1))
                            last.then_inc(sig["proj"], 1)

                        def decay_sums(c):
                            j, bk = c % 2, build_banks(c)
                            if c == 0:
                                pe.wait_ge(sig["gate"], HG)
                            elif c == 2:
                                pe.wait_ge(sig["vt"], CH)
                            elif c == 3:
                                pe.wait_ge(sig["e_row"], c)
                            pe.wait_ge(sig["lam"], c + 1)
                            lc = flat(lam[:, j])
                            if c == 1:
                                pe.wait_ge(sig["norm"], KG)
                            pe.matmul(bk[0][:], low[:], lc, start=True, stop=True)
                            for h in range(HG):
                                pe.matmul(bk[1][:, h * P:(h + 1) * P], lam[:, j, h, :], low[:], start=True, stop=True)
                            if c == 1:
                                pe.wait_ge(sig["norm"], QK)
                            pe.matmul(bk[2][:], ones[:], lc, start=True, stop=True).then_inc(sig["d_ps"], 1)

                        def gram(c, queries):
                            cc, base = slice(c * P, (c + 1) * P), KG if queries else 0
                            for h in range(KG):
                                last = pe.matmul(build_banks(c)[3][:, (base + h) * P:(base + h + 1) * P], qkv[:, h, cc], qkv[:, base + h, cc],
                                                 start=True, stop=True)
                            return last

                        def build(c):
                            decay_sums(c)
                            if c == 3:
                                pe.wait_ge(sig["a0"], c)
                            gram(c, False)
                            gram(c, True).then_inc(sig["kk_ps"], 1)

                        def inverse(pair, beside):
                            for s in range(LV):
                                for j in range(2):
                                    n, c, rows = pair * NQ + 2 * s + j, 2 * pair + j, part_rows(s)
                                    if s == 0:
                                        pe.wait_ge(sig["l"], c + 1)
                                        if pair == 0:
                                            pe.wait_ge(sig["e_row"], 1)
                                        else:
                                            pe.wait_ge(sig["xy"], n - 1)
                                        for h in range(HG):
                                            last = pe.transpose(ps[j][:, h * P:(h + 1) * P], L[:, c, h, :], ident[:])
                                    else:
                                        pe.wait_ge(sig["xy"], n - 1)
                                        if pair == 0 and s == 1 and j == 1:
                                            pe.wait_ge(sig["a0"], 1)
                                        if pair or s >= 2:
                                            pe.wait_ge(sig["xt"], pair * NX + 2 * (s - 2) + j + 1)
                                        for h in range(HG):
                                            last = pe.transpose(ps[2 + j][0:rows, h * P:(h + 1) * P], Y[:, c, h, 0:rows], ident[:])
                                        last.then_inc(sig["xt_ps"], 1)
                                        for h in range(HG):
                                            last = pe.matmul(blocks(ps[j][0:rows, h * HC:(h + 1) * HC], s), L[:, c, h, 0:rows], second(Y[:, c, h, :], s),
                                                             start=True, stop=True)
                                    last.then_inc(sig["w_ps"], 1)
                                if s > 0:
                                    for j in range(2):
                                        n = pair * NQ + 2 * s + j
                                        pe.wait_ge(sig["w"], n + 1)
                                        pe.wait_ge(sig["xt"], pair * NX + 2 * (s - 1) + j + 1)
                                        for h in range(HG):
                                            last = pe.matmul(ps[j][0:rows, h * HC:(h + 1) * HC], X[0:rows, j, h, 0:rows], W[0:rows, j, h, :], start=True, stop=True)
                                        last.then_inc(sig["dy_ps"], 1)
                                beside(s)

                        def k_tok(n):
                            pe.wait_ge(sig["conv"], QK + n + 1)
                            for c in (2 * n, 2 * n + 1):
                                for h in range(KG):
                                    q = (c % 2) * KG + h
                                    last = pe.transpose(ps[bank_kt(n)][:, q * P:(q + 1) * P], qkv[:, h, c * P:(c + 1) * P], ident[:])
                            last.then_inc(sig["kt_ps"], 1)

                        def v_tok(c):
                            pe.wait_ge(sig["silu"], CT)
                            if c >= 2:
                                pe.wait_ge(sig["kt"], c - 1)
                            for h in range(HG):
                                last = pe.transpose(ps[bank_vt(c)][:, h * P:(h + 1) * P], qkv[:, QK + h, c * P:(c + 1) * P], ident[:])
                            last.then_inc(sig["vt_ps"], 1)

                        def squares(i):
                            pe.wait_ge(sig["sq"], i + 1)
                            pe.matmul(ps[4 + i][:], ones[:], sq[:, i % 2, :], start=True, stop=True).then_inc(sig["ss"], 1)

                        def beside_first(s):
                            if s < 2:
                                for n in (2 * s, 2 * s + 1):
                                    pe.wait_ge(sig["e_row"], 2)
                                    if n == 3:
                                        pe.wait_ge(sig["a0"], 2)
                                    project(QK + n, bank_v(n))
                            elif s == 2:
                                k_tok(0)
                                k_tok(1)
                            elif s == 3:
                                for c in range(CH):
                                    v_tok(c)
                            elif s == 4:
                                build(2)
                            elif s == 6:
                                build(3)

                        def key_state(c):
                            pe.wait_ge(sig["kg"], c + 1)
                            pe.wait_ge(sig["s"], c + 1)
                            if c == 0:
                                pe.wait_ge(sig["e_row"], CH)
                                pe.wait_ge(sig["a0"], CH)
                            for h in range(HG):
                                last = pe.matmul(ps[4][:, h * P:(h + 1) * P], kg[:, c, h, :], state[:, h, :], start=True, stop=True)
                            last.then_inc(sig["ks"], 1)

                        def query_state(c):
                            if c >= 1:
                                pe.wait_ge(sig["o1"], c)
                            if 1 <= c <= 2:
                                pe.wait_ge(sig["y"], c)
                            for h in range(HG):
                                last = pe.matmul(ps[6][:, h * P:(h + 1) * P], state[:, h, :], qg[:, c, h, :], start=(h == 0), stop=False,
                                                 skip_group_check=True)
                            last.then_inc(sig["qs"], 1)

                        def solve(c):
                            pe.wait_ge(sig["r"], c + 1)
                            pe.wait_ge(sig["xy"], (c // 2) * NQ + NQ - 1 + c % 2)
                            for h in range(HG):
                                last = pe.matmul(ps[5][:, h * P:(h + 1) * P], Y[:, c, h, :], R[:, h, :], start=True, stop=True)
                            last.then_inc(sig["u_ps"], 1)

                        def read_and_grow(c):
                            pe.wait_ge(sig["u"], c + 1)
                            if c < CH - 1:
                                pe.wait_ge(sig["kd"], c + 1)
                                if 1 <= c <= 2:
                                    pe.wait_ge(sig["o3"], c)
                                for h in range(HG):
                                    last = pe.matmul(ps[7][:, h * P:(h + 1) * P], kd[:, h, :], U[:, h, :], start=True, stop=True)
                                last.then_inc(sig["dst"], 1)
                            pe.wait_ge(sig["a"], c + 1)
                            for h in range(HG):
                                last = pe.matmul(ps[6][:, h * P:(h + 1) * P], U[:, h, :], A[:, c, h, :], start=False, stop=(h == HG - 1),
                                                 skip_group_check=True)
                            last.then_inc(sig["o_ps"], 1)

                        def out_norm(c):
                            pe.wait_ge(sig["osq"], c + 1)
                            if c < 2:
                                pe.wait_ge(sig["s"], c + 2)
                            elif c == 2:
                                pe.wait_ge(sig["xy"], 2 * NQ)
                            else:
                                pe.wait_ge(sig["o3"], c)
                            pe.matmul(ps[oss_bank(c)][:], ones[:], osq[:], start=True, stop=True).then_inc(sig["oss"], 1)

                        def out(c):
                            pe.wait_ge(sig["o3"], c + 1)
                            if c == 3:
                                pe.wait_ge(sig["y"], c)
                            for h in range(HG):
                                last = pe.matmul(ps[y_bank(c)][:, 0:D], o[:, h, :], wo[:, h, :], start=(h == 0), stop=(h == HG - 1))
                            last.then_inc(sig["y_ps"], 1)

                        def beside_second(s):
                            if s == 0:
                                key_state(0)
                                query_state(0)
                            elif s == 1:
                                solve(0)
                            elif s == 2:
                                read_and_grow(0)
                            elif s == 3:
                                out_norm(0)
                                key_state(1)
                            elif s == 4:
                                out(0)
                                query_state(1)
                                solve(1)
                            elif s == 5:
                                read_and_grow(1)
                            else:
                                out_norm(1)

                        for i in range(QK):
                            project(i, 4 + i)
                        for i in range(HG):
                            project(CT + i, i)
                            if i >= 1:
                                squares(i - 1)
                        squares(QK - 1)
                        decay_sums(0)
                        pe.wait_ge(sig["norm"], KG)
                        gram(0, False).then_inc(sig["kk_ps"], 1)
                        build(1)
                        pe.wait_ge(sig["l0"], 1)
                        gram(0, True).then_inc(sig["kq_ps"], 1)
                        inverse(0, beside_first)
                        inverse(1, beside_second)
                        key_state(2)
                        out(1)
                        query_state(2)
                        solve(2)
                        read_and_grow(2)
                        key_state(3)
                        query_state(3)
                        solve(3)
                        out_norm(2)
                        read_and_grow(3)
                        out(2)
                        out_norm(3)
                        out(3)

                    @block.scalar
                    def _(act):
                        st = Steps(act, sig["order"])

                        def tap(i):
                            act.wait_ge(sig["proj"], i + 1 + (HG if i >= QK else 0))
                            act.activation(qkv[:, i, :], ps[4 + i % 4][:], ACT.Copy, scale=cw[:, i, 3:4]).then_inc(sig["tap0"], 1)

                        def silu(i):
                            act.wait_ge(sig["conv"], i + 1)
                            act.activation(qkv[:, i, :], qkv[:, i, :], ACT.Silu).then_inc(sig["silu"], 1)

                        def square(i):
                            act.wait_ge(sig["silu"], i + 1)
                            if i >= 2:
                                act.wait_ge(sig["ss"], i - 1)
                            act.activation(sq[:, i % 2, :], qkv[:, i, :], ACT.Square).then_inc(sig["sq"], 1)

                        def k_tok(n):
                            act.wait_ge(sig["kt_ps"], n + 1)
                            act.activation(ktok[:, 2 * n:2 * n + 2].rearrange("p c h n -> p (c h n)"), ps[bank_kt(n)][:], ACT.Copy
                                           ).then_inc(sig["kt"], 1)

                        def gate(n):
                            act.wait_ge(sig["proj"], QK + n + 1)
                            act.activation(gt[:, n, :], ps[n][:], ACT.Silu).then_inc(sig["gate"], 1)

                        def v_tok(c):
                            act.wait_ge(sig["vt_ps"], c + 1)
                            act.wait_ge(sig["lam"], 1)
                            for h in range(HG):
                                last = act.activation(vtok[:, c, h, :], ps[bank_vt(c)][:, h * P:(h + 1) * P], ACT.Copy,
                                                      scale=be[:, c * HG + h:c * HG + h + 1])
                            last.then_inc(sig["vt"], 1)

                        def decays(c):
                            act.wait_ge(sig["d_ps"], c + 1)
                            for dst, bank in ((L[:, c], 1), (A[:, c], 0), (G[:, c], 2)):
                                last = act.activation(flat(dst), build_banks(c)[bank][:], ACT.Exp)
                            last.then_inc(sig["e_row"], 1)

                        def inverse(pair, beside):
                            for s in range(1, LV):
                                for j in range(2):
                                    act.wait_ge(sig["xt_ps"], pair * NX + 2 * (s - 1) + j + 1)
                                    act.activation(flat(X[0:part_rows(s), j]), ps[2 + j][0:part_rows(s), :], ACT.Copy).then_inc(sig["xt"], 1)
                                beside(s)

                        def decayed_keys(c):
                            act.wait_ge(sig["dcol"], c + 1)
                            act.wait_ge(sig["kt"], 2)
                            if c >= 1:
                                act.wait_ge(sig["dst"], c)
                            for h in range(HG):
                                last = act.activation(kd[:, h, :], ktok[:, c, h // 2, :], ACT.Copy, scale=dcol[:, c, h:h + 1])
                            last.then_inc(sig["kd"], 1)

                        def solved(c):
                            act.wait_ge(sig["u_ps"], c + 1)
                            if c >= 1:
                                act.wait_ge(sig["o_ps"], c)
                            act.activation(flat(U), ps[5][:], ACT.Copy).then_inc(sig["u"], 1)

                        def read(c):
                            act.wait_ge(sig["o_ps"], c + 1)
                            if c >= 1:
                                act.wait_ge(sig["oss"], c)
                            act.activation(osq[:], ps[6][:], ACT.Square).then_inc(sig["osq"], 1)

                        def out_norm(c):
                            p = ps[oss_bank(c)][:]
                            act.wait_ge(sig["oss"], c + 1)
                            st.link(act.activation(p, p, ACT.Ln, scale=1.0 / P, bias=eps[:, 0:1]))
                            act.activation(p, p, ACT.Exp, scale=-0.5).then_inc(sig["orn"], 1)

                        for i in range(QK):
                            tap(i)
                        for i in range(QK):
                            silu(i)
                            square(i)
                            gate(i)
                        act.preload_act_table_set("natural_log_exp_and_others")

                        def norms(tiles):
                            for i in tiles:
                                act.wait_ge(sig["ss"], i + 1)
                                st.mark(act.activation(ps[4 + i][:], ps[4 + i][:], ACT.Ln, bias=eps[:, 0:1]))
                            st.wait()
                            for i in tiles:
                                act.activation(ps[4 + i][:], ps[4 + i][:], ACT.Exp, scale=-0.5, bias=0.0 if i < KG else qb[:, 0:1]
                                               ).then_inc(sig["rn"], 1)

                        norms(range(KG))
                        decays(0)
                        norms(range(KG, QK))
                        decays(1)
                        tap(4)
                        tap(5)

                        def beside_first(s):
                            if s == 1:
                                silu(4)
                                silu(5)
                                tap(6)
                                tap(7)
                            elif s == 2:
                                silu(6)
                                silu(7)
                                k_tok(0)
                                k_tok(1)
                            elif s == 3:
                                v_tok(0)
                                v_tok(1)
                            elif s == 4:
                                v_tok(2)
                                v_tok(3)
                                act.preload_act_table_set("natural_log_exp_and_others")
                            elif s == 5:
                                decays(2)
                            elif s == 6:
                                decays(3)
                                decayed_keys(0)

                        def beside_second(s):
                            if s == 1:
                                solved(0)
                            elif s == 2:
                                read(0)
                            elif s == 3:
                                out_norm(0)
                            elif s == 4:
                                decayed_keys(1)
                                solved(1)
                            elif s == 5:
                                read(1)

                        inverse(0, beside_first)
                        inverse(1, beside_second)
                        out_norm(1)
                        decayed_keys(2)
                        solved(2)
                        read(2)
                        solved(3)
                        out_norm(2)
                        read(3)
                        out_norm(3)

                    @block.gpsimd
                    def _(pool):
                        for c in range(CH):
                            pool.tensor_copy(Y[:, c], bc(ident[:], 1, HG)).then_inc(sig["eye"], 1)
                        for pair in range(CH // 2):
                            both = (2 * pair, 2 * pair + 1)
                            for c in both:
                                pool.wait_ge(sig["l0"], c + 1)
                                pool.affine_select(out=L[:, c], in_=L[:, c], compare_op=ALU.is_ge, fill=0.0, base=-1,
                                                   pattern=[[0, HG], [-1, P]], channel_multiplier=1).then_inc(sig["l"], 1)
                            for c in both:
                                pool.wait_ge(sig["a0"], c + 1)
                                pool.affine_select(out=A[:, c], in_=A[:, c], compare_op=ALU.is_ge, fill=0.0, base=0,
                                                   pattern=[[0, HG], [1, P]], channel_multiplier=-1).then_inc(sig["a"], 1)
                            pool.wait_ge(sig["g"], both[1] + 1)
                            pool.wait_ge(sig["norm"], QK)
                            for c in both:
                                for dst, base in ((kg, 0), (qg, KG)):
                                    for h in range(HG):
                                        last = pool.tensor_tensor(dst[:, c, h, :], G[:, c, h, :],
                                                                  qkv[:, base + h // 2, c * P:(c + 1) * P], ALU.mult)
                                last.then_inc(sig["kg"], 1)

                    @block.vector
                    def _(dve):
                        st = Steps(dve, sig["porder"])
                        st.mark(dve.tensor_copy(la[:], la_all[:, ds(b * NG + gi, 1), :].squeeze(1)))
                        st.mark(dve.tensor_copy(be[:], be_all[:, ds(b * NG + gi, 1), :].squeeze(1)))
                        st.wait()
                        st.mark(dve.tensor_scalar(nb[:], be[:], -1.0, None, ALU.mult))
                        dve.memset(state[:], 0.0).then_inc(sig["s"], 1)

                        def lams(c):
                            if c >= 2:
                                dve.wait_ge(sig["d_ps"], c - 1)
                            for h in range(HG):
                                last = dve.tensor_scalar(lam[:, c % 2, h, :], tri[:], la[:, c * HG + h:c * HG + h + 1], None, ALU.mult)
                            last.then_inc(sig["lam"], 1)

                        def conv(i):
                            dve.wait_ge(sig["tap0"], i + 1)
                            for n in (1, 2, 3):
                                ins = dve.scalar_tensor_tensor(out=qkv[:, i, n:], in0=ps[4 + i % 4][:, 0:S - n], scalar=cw[:, i, 3 - n:4 - n],
                                                               in1=qkv[:, i, n:], op0=ALU.mult, op1=ALU.add)
                                if n < 3:
                                    st.link(ins)
                                else:
                                    ins.then_inc(sig["conv"], 1)

                        def build_l(c):
                            dve.wait_ge(sig["e_row"], c + 1)
                            dve.wait_ge(sig["kk_ps"], c + 1)
                            kk = build_banks(c)[3][:, 0:KG * P].rearrange("p (k n) -> p k n", k=KG)
                            for k in range(KG):
                                hh = slice(2 * k, 2 * k + 2)
                                last = dve.scalar_tensor_tensor(out=L[:, c, hh, :], in0=L[:, c, hh, :], scalar=LEAST, in1=bc(kk[:, k, :], 1, 2),
                                                                op0=ALU.max, op1=ALU.mult)
                            st.link(last)
                            for h in range(HG):
                                last = dve.tensor_scalar(L[:, c, h, :], L[:, c, h, :], be[:, c * HG + h:c * HG + h + 1], None, ALU.mult)
                            last.then_inc(sig["l0"], 1)

                        def build_a(c):
                            if c == 0:
                                dve.wait_ge(sig["kq_ps"], 1)
                            kq = build_banks(c)[3][:, KG * P:].rearrange("p (k n) -> p k n", k=KG)
                            dve.tensor_scalar(dcol[:, c, :], A[:, c, :, P - 1], LEAST, None, ALU.max).then_inc(sig["dcol"], 1)
                            dve.wait_ge(sig["dcol"], c + 1)
                            for k in range(KG):
                                hh = slice(2 * k, 2 * k + 2)
                                last = dve.scalar_tensor_tensor(out=A[:, c, hh, :], in0=A[:, c, hh, :], scalar=LEAST, in1=bc(kq[:, k, :], 1, 2),
                                                                op0=ALU.max, op1=ALU.mult)
                            last.then_inc(sig["a0"], 1)
                            dve.tensor_scalar(flat(G[:, c]), flat(G[:, c]), LEAST, None, ALU.max).then_inc(sig["g"], 1)

                        def inverse(pair, beside):
                            for s in range(LV):
                                for j in range(2):
                                    n = pair * NQ + 2 * s + j
                                    dve.wait_ge(sig["w_ps"], n + 1)
                                    if s > 0:
                                        dve.wait_ge(sig["xy"], n - 1)
                                    rows = part_rows(s)
                                    src = second(h4(ps[j][:]), s) if s == 0 else blocks(half(ps[j])[0:rows], s)
                                    dve.tensor_tensor(blocks(W[0:rows, j], s), src, bc(blocks(lmask[0:rows, s, :], s), 1, HG), ALU.mult
                                                      ).then_inc(sig["w"], 1)
                                for j in range(2):
                                    n, c = pair * NQ + 2 * s + j, 2 * pair + j
                                    y = second(Y[0:part_rows(s), c], s)
                                    if s == 0:
                                        dve.wait_ge(sig["w"], n + 1)
                                        dve.wait_ge(sig["eye"], c + 1)
                                        dy = blocks(W[:, j], s)
                                    else:
                                        dve.wait_ge(sig["dy_ps"], pair * NX + 2 * (s - 1) + j + 1)
                                        dve.wait_ge(sig["xt_ps"], pair * NX + 2 * (s - 1) + j + 1)
                                        dy = blocks(half(ps[j])[0:part_rows(s)], s)
                                    dve.tensor_tensor(y, y, dy, ALU.subtract).then_inc(sig["xy"], 1)
                                beside(s)

                        def beside_first(s):
                            if s < 2:
                                conv(4 + 2 * s)
                                conv(5 + 2 * s)
                            elif s < 4:
                                lams(s)
                            elif s == 5:
                                build_l(2)
                                build_a(2)
                            elif s == 6:
                                build_l(3)
                                build_a(3)

                        def residue(c):
                            dve.wait_ge(sig["ks"], c + 1)
                            dve.wait_ge(sig["vt"], c + 1)
                            if c >= 1:
                                dve.wait_ge(sig["u_ps"], c)
                            for h in range(HG):
                                last = dve.scalar_tensor_tensor(out=R[:, h, :], in0=ps[4][:, h * P:(h + 1) * P],
                                                                scalar=nb[:, c * HG + h:c * HG + h + 1], in1=vtok[:, c, h, :],
                                                                op0=ALU.mult, op1=ALU.add)
                            last.then_inc(sig["r"], 1)

                        def grow(c):
                            dve.wait_ge(sig["qs"], c + 1)
                            dve.wait_ge(sig["dst"], c + 1)
                            dve.wait_ge(sig["s"], c + 1)
                            dve.wait_ge(sig["g"], c + 1)
                            for h in range(HG):
                                last = dve.scalar_tensor_tensor(out=state[:, h, :], in0=state[:, h, :], scalar=G[:, c, h, P - 1:P],
                                                                in1=ps[7][:, h * P:(h + 1) * P], op0=ALU.mult, op1=ALU.add)
                            last.then_inc(sig["s"], 1)

                        def gate(c):
                            dve.wait_ge(sig["osq"], c + 1)
                            if c >= 1:
                                dve.wait_ge(sig["y_ps"], c)
                            dve.tensor_tensor(o[:], h4(ps[6][:]), gt[:, :, c * P:(c + 1) * P], ALU.mult).then_inc(sig["o1"], 1)

                        def gated(c):
                            dve.wait_ge(sig["orn"], c + 1)
                            dve.wait_ge(sig["o1"], c + 1)
                            dve.scalar_tensor_tensor(out=flat(o), in0=flat(o), scalar=rw[:, 0:1], in1=ps[oss_bank(c)][:],
                                                     op0=ALU.mult, op1=ALU.mult).then_inc(sig["o3"], 1)

                        def add(c):
                            dve.wait_ge(sig["y_ps"], c + 1)
                            so = s_out[:, ds(b * CH + c, 1), :].squeeze(1)
                            dve.tensor_tensor(so, so, ps[y_bank(c)][:, 0:D], ALU.add).then_inc(sig["y"], 1)

                        def beside_second(s):
                            if s == 0:
                                residue(0)
                            elif s == 2:
                                grow(0)
                                gate(0)
                            elif s == 3:
                                residue(1)
                                gated(0)
                            elif s == 4:
                                add(0)
                            elif s == 5:
                                grow(1)
                                gate(1)

                        lams(0)
                        lams(1)
                        for i in range(QK):
                            conv(i)

                        def norm(i):
                            dve.wait_ge(sig["rn"], i + 1)
                            dve.wait_ge(sig["sq"], i + 1)
                            dve.tensor_tensor(qkv[:, i, :], qkv[:, i, :], ps[4 + i][:], ALU.mult).then_inc(sig["norm"], 1)

                        norm(0)
                        norm(1)
                        build_l(0)
                        norm(2)
                        norm(3)
                        build_l(1)
                        build_a(0)
                        build_a(1)
                        inverse(0, beside_first)
                        inverse(1, beside_second)
                        residue(2)
                        gated(1)
                        add(1)
                        grow(2)
                        gate(2)
                        residue(3)
                        gated(2)
                        gate(3)
                        add(2)
                        gated(3)
                        add(3)
                end_of_iteration(nc, sig)


def nvfp4_mlp(nc, g, d):
    N = 2048
    NTL = N // P
    with ExitStack() as ctx:
        sb = lambda n, s, t=F32: ctx.enter_context(nc.sbuf_tensor("nv_" + n, s, t))
        sig = signals(nc, ctx, "nv", "load next code sgn part v1 v2 v3 done a b act h down up_silu up_sg")
        wg, wu, wd = (sb(n, [P, 2, N]) for n in ("wg", "wu", "wd"))
        act_, h = sb("act", [P, 2, S]), sb("h", [P, 2, S])
        gate = sb("gate", [P, CH, D])
        ps, xn_fm = g["ps"], g["xn_fm"]
        NK = 3
        NB, CW = NK * 4, N // 4
        TB = CW // P

        def row_products(pe, b, unpacking):
            def up(u):
                if unpacking:
                    pe.wait_ge(sig["done"], 2 * (NK * (u // TB) + 2))
                if u >= 2:
                    pe.wait_ge(sig["h"], u - 1)
                for n, (w, what) in enumerate(((wg, "a"), (wu, "b"))):
                    for k in range(K2):
                        last = pe.matmul(ps[2 * (u % 2) + n][:], w[:, k, u * P:(u + 1) * P], xn_fm[:, k, ds(b * S, S)],
                                         start=(k == 0), stop=(k == K2 - 1))
                    last.then_inc(sig[what], 1)

            def down(u):
                if unpacking:
                    pe.wait_ge(sig["done"], 2 * (NK * (u // TB) + 3))
                pe.wait_ge(sig["h"], u + 1)
                q, nib = u // 2, u % 2
                for t in range(CH):
                    last = pe.matmul(ps[4 + t // 2][:, (t % 2) * D:(t % 2 + 1) * D], h[:, u % 2, t * P:(t + 1) * P],
                                     wd[:, nib, q * D:(q + 1) * D], start=(u == 0 and t % 2 == 0), stop=(u == NTL - 1),
                                     skip_group_check=True)
                last.then_inc(sig["down"], 1)

            for u in range(NTL):
                up(u)
                if u >= 1:
                    down(u - 1)
            down(NTL - 1)

        def gelu(act, u):
            act.wait_ge(sig["a"], u + 1)
            if u >= 2:
                act.wait_ge(sig["h"], u - 1)
            act.activation(act_[:, u % 2, :], ps[2 * (u % 2)][:], ACT.Gelu_apprx_tanh).then_inc(sig["act"], 1)

        def gates(act):
            gates_of_row(act, sig, gate, lambda t: ps[4 + t // 2][:, (t % 2) * D:(t % 2 + 1) * D],
                         lambda t: act.wait_ge(sig["down"], NTL))

        def gated_hidden(dve, u):
            dve.wait_ge(sig["act"], u + 1)
            dve.wait_ge(sig["b"], u + 1)
            if u >= 2:
                dve.wait_ge(sig["down"], u - 1)
            dve.tensor_tensor(h[:, u % 2, :], act_[:, u % 2, :], ps[2 * (u % 2) + 1][:], ALU.mult).then_inc(sig["h"], 1)

        def tiles_beside(u):
            c, k = divmod(u, 2 * NK)
            return [TB * (c - 1) + k] if c and k < TB else []

        with ExitStack() as c2:
            tb = lambda n, s, t=F32: c2.enter_context(nc.sbuf_tensor("nv_" + n, s, t))
            code, scale = tb("code", [P, 2, CW], I32), tb("scale", [P, 2, CW])
            m, sg = tb("m", [P, 2, CW], I32), tb("sg", [P, 2, CW], I32)
            hi4, hi6, sgn = tb("hi4", [P, 2, CW]), tb("hi6", [P, 2, CW]), tb("sgn", [P, 2, CW])
            m2, m6 = tb("m2", [P, 1]), tb("m6", [P, 1])
            with nc.Block() as block:
                @block.vector
                def _(dve):
                    dve.memset(m2[:], -2.0)
                    dve.memset(m6[:], -6.0)
            end_of_iteration(nc, sig)
            with nc.Block() as block:
                @block.sync
                def _(sp):
                    for i in range(NB):
                        if i >= 2:
                            sp.wait_ge(sig["done"], 2 * (i - 1))
                        name, c0 = ("gate", "up", "down")[i % NK], (i // NK) * CW
                        sp.dma_start(code[:, i % 2, :], d["nv_" + name + "_w"][:, c0:c0 + CW]).then_inc(sig["load"] if i % 2 == 0 else sig["next"], 16)
                        sp.dma_start(scale[:, i % 2, :], d["nv_" + name + "_s"][:, c0:c0 + CW]).then_inc(sig["load"] if i % 2 == 0 else sig["next"], 16)

                @block.scalar
                def _(act):
                    for u in range(2 * NB):
                        act.wait_ge(sig["sgn"], u + 1)
                        if u >= 2:
                            act.wait_ge(sig["done"], u - 1)
                        r = u % 2
                        act.activation(hi4[:, r, :], m[:, r, :], ACT.Relu, scale=0.5, bias=m2[:, 0:1])
                        act.activation(hi6[:, r, :], m[:, r, :], ACT.Relu, bias=m6[:, 0:1])
                        act.activation(sgn[:, r, :], sg[:, r, :], ACT.Copy, scale=-0.25, bias=1.0).then_inc(sig["part"], 1)
                        for tile in tiles_beside(u):
                            gelu(act, tile)
                    for tile in range(NTL - TB, NTL):
                        gelu(act, tile)
                    gates(act)

                @block.tensor
                def _(pe):
                    row_products(pe, 0, True)

                @block.gpsimd
                def _(pool):
                    for u in range(2 * NB):
                        i, r = u // 2, u % 2
                        pool.wait_ge(sig["part"], u + 1)
                        pool.tensor_tensor(sgn[:, r, :], sgn[:, r, :], scale[:, i % 2, :], ALU.mult).then_inc(sig["v2"], 1)

                @block.vector
                def _(dve):
                    def take(u):
                        i, nib, r = u // 2, u % 2, u % 2
                        dve.wait_ge(sig["load"] if i % 2 == 0 else sig["next"], 32 * (i // 2 + 1))
                        if u >= 2:
                            dve.wait_ge(sig["part"], u - 1)
                            dve.wait_ge(sig["done"], u - 1)
                        dve.tensor_scalar(m[:, r, :], code[:, i % 2, :], 4 * nib, 7, ALU.logical_shift_right, ALU.bitwise_and
                                          ).then_inc(sig["code"], 1)
                        dve.tensor_scalar(sg[:, r, :], code[:, i % 2, :], 4 * nib, 8, ALU.logical_shift_right, ALU.bitwise_and
                                          ).then_inc(sig["sgn"], 1)

                    def finish(u):
                        i, nib, r = u // 2, u % 2, u % 2
                        dst = (wg, wu, wd)[i % NK][:, nib, (i // NK) * CW:(i // NK + 1) * CW]
                        dve.wait_ge(sig["part"], u + 1)
                        dve.scalar_tensor_tensor(out=hi4[:, r, :], in0=m[:, r, :], scalar=0.5, in1=hi4[:, r, :],
                                                 op0=ALU.mult, op1=ALU.add).then_inc(sig["v1"], 1)
                        dve.wait_ge(sig["v1"], u + 1)
                        dve.tensor_tensor(hi4[:, r, :], hi4[:, r, :], hi6[:, r, :], ALU.add).then_inc(sig["v3"], 1)
                        dve.wait_ge(sig["v3"], u + 1)
                        dve.wait_ge(sig["v2"], u + 1)
                        dve.tensor_tensor(dst, hi4[:, r, :], sgn[:, r, :], ALU.mult).then_inc(sig["done"], 1)

                    for u in range(2 * NB):
                        take(u)
                        if u >= 1:
                            finish(u - 1)
                        for tile in tiles_beside(u):
                            gated_hidden(dve, tile)
                    finish(2 * NB - 1)
                    for tile in range(NTL - TB, NTL):
                        gated_hidden(dve, tile)
                    update_of_row(dve, g, sig, gate, 0)
            end_of_iteration(nc, sig)
        with nc.Fori(1, B) as b:
            with nc.Block() as block:
                @block.tensor
                def _(pe):
                    row_products(pe, b, False)

                @block.scalar
                def _(act):
                    for u in range(NTL):
                        gelu(act, u)
                    gates(act)

                @block.vector
                def _(dve):
                    for u in range(NTL):
                        gated_hidden(dve, u)
                    update_of_row(dve, g, sig, gate, b)
            end_of_iteration(nc, sig)


def linear_attention(nc, g, d):
    with ExitStack() as ctx:
        sb = lambda n, s, t=F32: ctx.enter_context(nc.sbuf_tensor("la_" + n, s, t))
        sig = signals(nc, ctx, "la", "load xb q_ps q qd k_ps ka k v_ps v kv_ps kvm nd den lden rden o out_ps out")
        wq, wk, wv, wo = (sb(n, [P, K2, D]) for n in ("wq", "wk", "wv", "wo"))
        bq, bk, bv, bo = sb("bq", [P, K2]), sb("bk", [P, D]), sb("bv", [P, D]), sb("bo", [P, D])
        dec_row, dec_col, blocks = sb("dec_row", [P, S]), sb("dec_col", [P, CH]), sb("blocks", [P, P])
        xb, q = sb("xb", [P, K2, S]), sb("q", [P, K2, S])
        k_, v = sb("k", [P, CH, D]), sb("v", [P, CH, D])
        kv, ksum = sb("kv", [P, K2, P]), sb("ksum", [P, K2, P])
        rd, o = sb("rd", [P, K2, S]), sb("o", [P, K2, S])
        ps, xn_fm, s_out, ones, eps = g["ps"], g["xn_fm"], g["s"], g["ones"], g["eps6"]
        load(nc, sig, "load", [(wq[:], d["la_wq"]), (wk[:], d["la_wk"]), (wv[:], d["la_wv"]), (wo[:], d["la_wo"]), (bq[:], d["la_bq"]),
                               (bk[:], d["la_bk"].partition_broadcast(P)), (bv[:], d["la_bv"].partition_broadcast(P)),
                               (bo[:], d["la_bo"].partition_broadcast(P)), (dec_row[:], d["c_dec"].partition_broadcast(P)),
                               (dec_col[:], d["c_dec_col"]), (blocks[:], d["c_blocks"])], lambda: layer_norm(nc, g))
        with nc.Fori(0, B) as b:
            with nc.Block() as block:
                @block.tensor
                def _(pe):
                    pe.wait_ge(sig["xb"], 1)
                    for m in range(K2):
                        for k in range(K2):
                            last = pe.matmul(ps[m][:], wq[:, k, m * P:(m + 1) * P], xb[:, k, :], start=(k == 0), stop=(k == K2 - 1))
                        last.then_inc(sig["q_ps"], 1)
                    for w, what, bank in ((wk, "k_ps", 2), (wv, "v_ps", 4)):
                        for t in range(CH):
                            for k in range(K2):
                                last = pe.matmul(ps[bank + t // 2][:, (t % 2) * D:(t % 2 + 1) * D], xb[:, k, t * P:(t + 1) * P], w[:, k, :],
                                                 start=(k == 0), stop=(k == K2 - 1))
                        last.then_inc(sig[what], 1)
                    pe.wait_ge(sig["k"], CH)
                    pe.wait_ge(sig["v"], CH)
                    for m in range(K2):
                        ms = slice(m * P, (m + 1) * P)
                        for t in range(CH):
                            pe.matmul(ps[6 + m][:, 0:P], k_[:, t, ms], v[:, t, ms], start=(t == 0), stop=(t == CH - 1))
                        for t in range(CH):
                            last = pe.matmul(ps[6 + m][:, P:2 * P], k_[:, t, ms], ones[:], start=(t == 0), stop=(t == CH - 1))
                        last.then_inc(sig["kv_ps"], 1)
                    for m in range(K2):
                        pe.wait_ge(sig["kvm"], 2 * (m + 1))
                        pe.wait_ge(sig["qd"], m + 1)
                        pe.matmul(ps[2 + m][:], ksum[:, m, :], q[:, m, :], start=True, stop=True).then_inc(sig["den"], 1)
                        pe.matmul(ps[4 + m][:], kv[:, m, :], q[:, m, :], start=True, stop=True).then_inc(sig["nd"], 1)
                    pe.wait_ge(sig["o"], K2)
                    for t in range(CH):
                        for m in range(K2):
                            last = pe.matmul(ps[t // 2][:, (t % 2) * D:(t % 2 + 1) * D], o[:, m, t * P:(t + 1) * P], wo[:, m, :],
                                             start=(m == 0), stop=(m == K2 - 1))
                    last.then_inc(sig["out_ps"], 1)

                @block.scalar
                def _(act):
                    act.preload_act_table_set("natural_log_exp_and_others")
                    act.activation(xb[:], xn_fm[:, :, ds(b * S, S)], ACT.Copy).then_inc(sig["xb"], 1)
                    for m in range(K2):
                        act.wait_ge(sig["q_ps"], m + 1)
                        act.activation(q[:, m, :], ps[m][:], ACT.Relu, bias=bq[:, m:m + 1]).then_inc(sig["q"], 1)
                    for t in range(CH):
                        act.wait_ge(sig["ka"], t + 1)
                        act.activation(k_[:, t, :], k_[:, t, :], ACT.Relu, scale=dec_col[:, t:t + 1]).then_inc(sig["k"], 1)
                    for m in range(K2):
                        act.wait_ge(sig["den"], m + 1)
                        act.activation(rd[:, m, :], ps[2 + m][:], ACT.Ln, bias=eps[:, 0:1]).then_inc(sig["lden"], 1)
                        act.wait_ge(sig["lden"], m + 1)
                        act.activation(rd[:, m, :], rd[:, m, :], ACT.Exp, scale=-1.0).then_inc(sig["rden"], 1)

                @block.vector
                def _(dve):
                    dve.wait_ge(sig["k_ps"], 1)
                    for t in range(CH):
                        dve.tensor_tensor(k_[:, t, :], ps[2 + t // 2][:, (t % 2) * D:(t % 2 + 1) * D], bk[:], ALU.add).then_inc(sig["ka"], 1)
                    dve.wait_ge(sig["v_ps"], 1)
                    for t in range(CH):
                        dve.tensor_tensor(v[:, t, :], ps[4 + t // 2][:, (t % 2) * D:(t % 2 + 1) * D], bv[:], ALU.add).then_inc(sig["v"], 1)
                    for m in range(K2):
                        dve.wait_ge(sig["q"], m + 1)
                        dve.tensor_tensor(q[:, m, :], q[:, m, :], dec_row[:], ALU.mult).then_inc(sig["qd"], 1)
                    for m in range(K2):
                        dve.wait_ge(sig["kv_ps"], m + 1)
                        dve.tensor_tensor(kv[:, m, :], ps[6 + m][:, 0:P], blocks[:], ALU.mult).then_inc(sig["kvm"], 1)
                        dve.tensor_tensor(ksum[:, m, :], ps[6 + m][:, P:2 * P], blocks[:], ALU.mult).then_inc(sig["kvm"], 1)
                    for m in range(K2):
                        dve.wait_ge(sig["rden"], m + 1)
                        dve.wait_ge(sig["nd"], m + 1)
                        dve.tensor_tensor(o[:, m, :], rd[:, m, :], ps[4 + m][:], ALU.mult).then_inc(sig["o"], 1)
                    dve.wait_ge(sig["out_ps"], 1)
                    for t in range(CH):
                        dve.tensor_tensor(s_out[:, ds(b * CH + t, 1), :].squeeze(1), ps[t // 2][:, (t % 2) * D:(t % 2 + 1) * D], bo[:], ALU.add)
            end_of_iteration(nc, sig)


def latent_attention(nc, g, d):
    NH, DN, DR, DV, QL, KL = 16, 128, 64, 128, 192, 64
    QM = QL // 2
    SCALE = float((DN + DR) ** -0.5)
    with ExitStack() as ctx:
        sb = lambda n, s, t=F32: ctx.enter_context(nc.sbuf_tensor("mla_" + n, s, t))
        pre = signals(nc, ctx, "mp", "load lat_ps lat sq ss rn out t1 t2 kr order")
        sig = signals(nc, ctx, "mla", "load wab_ps wab wvo_ps wvo kvb kvt_ps kvt q_ps qa q s_ps nm e pt_ps pt pv o_ps o y_ps order")
        qn_all, kf_all = sb("qn_all", [QM, 2, B * S]), sb("kf_all", [P, B * S])
        ps, xn_fm, s_out, ident, ones, eps = g["ps"], g["xn_fm"], g["s"], g["ident"], g["ones"], g["eps6"]
        qcos, qsin = sb("qcos", [P, S]), sb("qsin", [P, S])
        wq = sb("wq", [QM, 2, NH, KL + DR])
        wvo = sb("wvo", [P, NH // 2, D])
        identb, laterb = sb("identb", [P, P], BF16), sb("laterb", [P, P], BF16)
        weights = ExitStack()
        tw = lambda n, s, t=F32: weights.enter_context(nc.sbuf_tensor("mw_" + n, s, t))
        wqn, wk = tw("wqn", [DN, NH, QL]), tw("wk", [DN, NH, KL])
        wv, wo, later = tw("wv", [DV, NH, 2 * KL]), tw("wo", [DV, NH, D]), tw("later", [P, P])
        with ExitStack() as c2:
            tb = lambda n, s, t=F32: c2.enter_context(nc.sbuf_tensor("mp_" + n, s, t))
            wa = tb("wa", [P, K2, QL + KL + 4 * DR])
            qg, kg_ = tb("qg", [QM, 2]), tb("kg", [KL, 1])
            cos2, sin2 = tb("cos2", [P, S]), tb("sin2", [P, S])
            t1 = tb("t1", [P, S])
            load(nc, pre, "load", [(wa[:], d["mla_wa"]), (qg[:], d["mla_qg"]), (kg_[:], d["mla_kg"]), (cos2[:], d["c_cos2"]),
                                   (sin2[:], d["c_sin2"]), (qcos[:], d["c_qcos"]), (qsin[:], d["c_qsin"])],
                 lambda: layer_norm(nc, g))
            fetched = fetch(nc, sig, "load", [(wqn[:], d["mla_wqn"]), (wk[:], d["mla_wk"]), (wq[:, :, :, KL:], d["mla_wqp"]),
                                              (wv[:], d["mla_wv"]), (wo[:], d["mla_wo"]), (later[:], d["c_later"])])
            lat, sq = tb("lat", [P, 2, 3, S]), tb("sq", [P, 2, 3, S])
            sizes = [QM, QM, KL]
            NL = len(sizes)
            with nc.Block() as block:
                @block.tensor
                def _(pe):
                    def latents(b):
                        c0 = 0
                        for i, n in enumerate(sizes + [2 * DR, 2 * DR]):
                            if b and i < NL:
                                pe.wait_ge(pre["sq"], NL * (b - 1) + i + 1)
                            elif b:
                                pe.wait_ge(pre["t1"] if i == NL else pre["t2"], b)
                            for k in range(K2):
                                last = pe.matmul(ps[i][0:n, :], wa[:, k, c0:c0 + n], xn_fm[:, k, b * S:(b + 1) * S],
                                                 start=(k == 0), stop=(k == K2 - 1))
                            last.then_inc(pre["lat_ps"], 1)
                            c0 += n

                    def squares(b):
                        pe.wait_ge(pre["sq"], NL * (b + 1))
                        if b:
                            pe.wait_ge(pre["out"], NL * b)
                        r_ = b % 2
                        pe.matmul(ps[5][:], ones[0:QM, :], sq[0:QM, r_, 0, :], start=True, stop=False)
                        pe.matmul(ps[5][:], ones[0:QM, :], sq[0:QM, r_, 1, :], start=False, stop=True)
                        pe.matmul(ps[6][:], ones[0:KL, :], sq[0:KL, r_, 2, :], start=True, stop=True).then_inc(pre["ss"], 1)

                    for b in range(B):
                        latents(b)
                        if b:
                            squares(b - 1)
                    squares(B - 1)

                @block.scalar
                def _(act):
                    st = Steps(act, pre["order"])
                    act.preload_act_table_set("natural_log_exp_and_others")

                    def norms(b):
                        act.wait_ge(pre["ss"], b + 1)
                        for bank, n in ((5, QL), (6, KL)):
                            st.link(act.activation(ps[bank][:], ps[bank][:], ACT.Ln, scale=1.0 / n, bias=eps[:, 0:1]))
                            act.activation(ps[bank][:], ps[bank][:], ACT.Exp, scale=-0.5).then_inc(pre["rn"], 1)

                    for b in range(B):
                        for i, n in enumerate(sizes):
                            act.wait_ge(pre["lat_ps"], (NL + 2) * b + i + 1)
                            if b >= 2:
                                act.wait_ge(pre["out"], NL * (b - 2) + i + 1)
                                act.wait_ge(pre["ss"], b - 1)
                            act.activation(lat[0:n, b % 2, i, :], ps[i][0:n, :], ACT.Copy).then_inc(pre["lat"], 1)
                            act.activation(sq[0:n, b % 2, i, :], ps[i][0:n, :], ACT.Square).then_inc(pre["sq"], 1)
                        if b:
                            norms(b - 1)
                    norms(B - 1)

                @block.vector
                def _(dve):
                    def position(b):
                        kr = kf_all[DR:, b * S:(b + 1) * S]
                        dve.wait_ge(pre["lat_ps"], (NL + 2) * (b + 1))
                        if b:
                            dve.wait_ge(pre["kr"], b)
                        dve.tensor_tensor(t1[DR:, :], cos2[DR:, :], ps[3][DR:, :], ALU.mult).then_inc(pre["t1"], 1)
                        dve.tensor_tensor(kr, sin2[DR:, :], ps[4][DR:, :], ALU.mult).then_inc(pre["t2"], 1)
                        dve.wait_ge(pre["t1"], b + 1)
                        dve.wait_ge(pre["t2"], b + 1)
                        dve.tensor_tensor(kr, kr, t1[DR:, :], ALU.add).then_inc(pre["kr"], 1)

                    def normalise(b):
                        cols = slice(b * S, (b + 1) * S)
                        dve.wait_ge(pre["lat"], NL * (b + 1))
                        for i, n in enumerate(sizes):
                            dve.wait_ge(pre["rn"], 2 * b + (1 if i < 2 else 2))
                            out = qn_all[:, i, cols] if i < 2 else kf_all[0:KL, cols]
                            gamma = qg[:, i:i + 1] if i < 2 else kg_[:, 0:1]
                            dve.scalar_tensor_tensor(out=out, in0=lat[0:n, b % 2, i, :], scalar=gamma, in1=ps[5 if i < 2 else 6][0:n, :],
                                                     op0=ALU.mult, op1=ALU.mult).then_inc(pre["out"], 1)

                    for b in range(B):
                        position(b)
                        if b:
                            normalise(b - 1)
                    normalise(B - 1)
            end_of_iteration(nc, pre)
        with weights:
            arrive(nc, sig, "load", fetched)
            HB = 8
            with nc.Block() as block:
                @block.tensor
                def _(pe):
                    for c in range(NH // HB):
                        for i in range(2):
                            for h in range(HB):
                                last = pe.matmul(ps[2 * c + i][0:QM, h * KL:(h + 1) * KL], wqn[:, c * HB + h, i * QM:(i + 1) * QM],
                                                 wk[:, c * HB + h, :], start=True, stop=True)
                            last.then_inc(sig["wab_ps"], 1)
                    for h in range(NH):
                        if h >= 4:
                            pe.wait_ge(sig["wvo"], h - 3)
                        pe.matmul(ps[4 + h % 4][:, 0:D], wv[:, h, :], wo[:, h, :], start=True, stop=True).then_inc(sig["wvo_ps"], 1)

                @block.scalar
                def _(act):
                    for c in range(NH // HB):
                        for i in range(2):
                            act.wait_ge(sig["wab_ps"], 2 * c + i + 1)
                            act.activation(wq[:, i, c * HB:(c + 1) * HB, 0:KL],
                                           ps[2 * c + i][0:QM, :].rearrange("p (h c) -> p h c", c=KL), ACT.Copy)

                @block.vector
                def _(dve):
                    dve.tensor_copy(identb[:], ident[:])
                    dve.tensor_copy(laterb[:], later[:])
                    for h in range(NH):
                        half = slice(0, KL) if h % 2 == 0 else slice(KL, 2 * KL)
                        dve.wait_ge(sig["wvo_ps"], h + 1)
                        dve.tensor_copy(wvo[half, h // 2, :], ps[4 + h % 4][half, 0:D]).then_inc(sig["wvo"], 1)
            end_of_iteration(nc, sig)

        kvb, kvt = sb("kvb", [KL, S]), sb("kvt", [P, CH, KL])
        q, t2 = sb("q", [P, 3, S]), sb("t2", [P, S])
        pr, PT = sb("pr", [P, 3, S]), sb("PT", [P, 3, CH, P])
        o, oT = sb("o", [P, CH, 2, KL]), sb("oT", [P, NH // 2, S])
        NU = NH * CH
        nm, rs = sb("nm", [P, NU]), sb("rs", [P, NU])

        def turn_of_unit(u):
            return u + max(0, (u - 3) // 8)

        def turn_of_pair(p):
            return 8 * p + 11 + p if p < NH // 2 - 1 else NU + NH // 2 - 1

        turn_bank = lambda v: ps[(1, 5)[v % 2]]
        y_bank = [ps[0], ps[2], ps[3], ps[4]]
        with nc.Fori(0, B) as b:
            with nc.Block() as block:
                @block.tensor
                def _(pe):
                    def project(h, i):
                        if i == 0 and h >= 1:
                            pe.wait_ge(sig["q"], h)
                        last = pe.matmul(ps[0][:], wq[:, i, h, :], qn_all[:, i, ds(b * S, S)], start=(i == 0), stop=(i == 1))
                        if i == 1:
                            last.then_inc(sig["q_ps"], 1)

                    def scores(u):
                        h, t = u // CH, u % CH
                        pe.wait_ge(sig["q"], h + 1)
                        if u < 3:
                            pe.wait_ge(sig["kvt"], 1)
                        else:
                            pe.wait_ge(sig["e"], u - 2)
                        n, tt = (t + 1) * P, slice(t * P, (t + 1) * P)
                        pe.matmul(ps[2 + u % 3][:, 0:n], q[:, h % 3, tt], kf_all[:, ds(b * S, n)], start=True, stop=False)
                        pe.matmul(ps[2 + u % 3][:, tt], identb[:], laterb[:], start=False, stop=True).then_inc(sig["s_ps"], 1)

                    def turn(u):
                        v = turn_of_unit(u)
                        pe.wait_ge(sig["e"], u + 1)
                        if v >= 2:
                            pe.wait_ge(sig["pt"], v - 1)
                        for j in range(u % CH + 1):
                            last = pe.transpose(turn_bank(v)[:, j * P:(j + 1) * P], pr[:, u % 3, j * P:(j + 1) * P], ident[:])
                        last.then_inc(sig["pt_ps"], 1)

                    def turn_pair(p):
                        v = turn_of_pair(p)
                        pe.wait_ge(sig["o"], 2 * p + 2)
                        pe.wait_ge(sig["pt"], v - 1)
                        for t in range(CH):
                            last = pe.transpose(turn_bank(v)[:, t * P:(t + 1) * P], o[:, t, :, :].rearrange("p h c -> p (h c)"), ident[:])
                        last.then_inc(sig["pt_ps"], 1)

                    def attend(u):
                        h, t = u // CH, u % CH
                        pe.wait_ge(sig["pt"], turn_of_unit(u) + 1)
                        if t == 0 and h >= 2:
                            pe.wait_ge(sig["o"], h - 1)
                        for j in range(t + 1):
                            last = pe.matmul(ps[6 + h % 2][:, t * KL:(t + 1) * KL], PT[:, u % 3, j, :], kvt[:, j, :],
                                             start=(j == 0), stop=(j == t))
                        last.then_inc(sig["pv"], 1)

                    def out(t, pairs):
                        for p in pairs:
                            last = pe.matmul(y_bank[t][:, 0:D], oT[:, p, t * P:(t + 1) * P], wvo[:, p, :],
                                             start=(p == 0), stop=(p == NH // 2 - 1))
                        if p == NH // 2 - 1:
                            last.then_inc(sig["y_ps"], 1)

                    project(0, 0)
                    project(0, 1)
                    pe.wait_ge(sig["kvb"], 1)
                    for t in range(CH):
                        last = pe.transpose(ps[2][:, t * KL:(t + 1) * KL], kvb[:, t * P:(t + 1) * P], ident[0:KL, 0:KL])
                    last.then_inc(sig["kvt_ps"], 1)
                    project(1, 0)
                    project(1, 1)
                    for u in range(NU):
                        h, t = u // CH, u % CH
                        scores(u)
                        if u >= 2:
                            turn(u - 2)
                        if u >= 12 and (u - 12) % 8 == 0:
                            turn_pair((u - 12) // 8)
                        if u >= 3:
                            attend(u - 3)
                        if 1 <= t <= 2 and h + 2 < NH:
                            project(h + 2, t - 1)
                    turn(NU - 2)
                    attend(NU - 3)
                    turn(NU - 1)
                    pe.wait_ge(sig["e"], NU)
                    most = range(NH // 2 - 1)
                    out(0, most)
                    attend(NU - 2)
                    attend(NU - 1)
                    for t in range(1, CH):
                        out(t, most)
                    turn_pair(NH // 2 - 1)
                    pe.wait_ge(sig["pt"], NU + NH // 2)
                    for t in range(CH):
                        out(t, [NH // 2 - 1])

                @block.scalar
                def _(act):
                    def position_free(h):
                        act.wait_ge(sig["q_ps"], h + 1)
                        if h >= 3:
                            act.wait_ge(sig["s_ps"], CH * (h - 2))
                        act.activation(q[0:KL, h % 3, :], ps[0][0:KL, :], ACT.Copy, scale=SCALE).then_inc(sig["qa"], 1)

                    def exps(u):
                        n = (u % CH + 1) * P
                        act.wait_ge(sig["nm"], u + 1)
                        if u >= 3:
                            act.wait_ge(sig["pt_ps"], turn_of_unit(u - 3) + 1)
                        act.activation(pr[:, u % 3, 0:n], ps[2 + u % 3][:, 0:n], ACT.Exp, bias=nm[:, u:u + 1],
                                       accum_out=rs[:, u:u + 1]).then_inc(sig["e"], 1)

                    def turned(u):
                        t, v = u % CH, turn_of_unit(u)
                        act.wait_ge(sig["pt_ps"], v + 1)
                        if u >= 3:
                            act.wait_ge(sig["pv"], u - 2)
                        act.activation(PT[:, u % 3, 0:t + 1, :], turn_bank(v)[:, 0:(t + 1) * P].rearrange("p (j n) -> p j n", n=P),
                                       ACT.Copy).then_inc(sig["pt"], 1)

                    def turned_pair(p):
                        v = turn_of_pair(p)
                        act.wait_ge(sig["pt_ps"], v + 1)
                        act.activation(oT[:, p, :], turn_bank(v)[:], ACT.Copy).then_inc(sig["pt"], 1)

                    act.activation(kvb[:], kf_all[0:KL, ds(b * S, S)], ACT.Copy).then_inc(sig["kvb"], 1)
                    position_free(0)
                    act.wait_ge(sig["kvt_ps"], 1)
                    act.activation(kvt[:], ps[2][:, 0:CH * KL].rearrange("p (t c) -> p t c", c=KL), ACT.Copy).then_inc(sig["kvt"], 1)
                    position_free(1)
                    for u in range(NU):
                        h, t = u // CH, u % CH
                        if u >= 2:
                            turned(u - 2)
                        if u >= 12 and (u - 12) % 8 == 0:
                            turned_pair((u - 12) // 8)
                        exps(u)
                        if t == 2 and h + 2 < NH:
                            position_free(h + 2)
                    turned(NU - 2)
                    turned(NU - 1)
                    turned_pair(NH // 2 - 1)
                    for t in range(CH):
                        act.wait_ge(sig["y_ps"], t + 1)
                        act.activation(s_out[:, ds(b * CH + t, 1), :].squeeze(1), y_bank[t][:, 0:D], ACT.Copy)

                @block.vector
                def _(dve):
                    st = Steps(dve, sig["order"])
                    HALF = DR // 2
                    lo, hi, up = slice(KL, KL + HALF), slice(KL + HALF, KL + DR), slice(KL, KL + DR)

                    def rotate_a(h):
                        dve.wait_ge(sig["qa"], h + 1)
                        if h >= 1:
                            dve.wait_ge(sig["q"], h)
                        st.mark(dve.tensor_tensor(t2[lo, :], qsin[hi, :], ps[0][hi, :], ALU.mult))
                        st.mark(dve.tensor_tensor(t2[hi, :], qsin[lo, :], ps[0][lo, :], ALU.mult))
                        st.wait()

                    def rotate_b(h):
                        st.link(dve.tensor_tensor(ps[0][up, :], qcos[up, :], ps[0][up, :], ALU.mult))
                        dve.tensor_tensor(q[up, h % 3, :], t2[up, :], ps[0][up, :], ALU.add).then_inc(sig["q"], 1)

                    def maxima(u):
                        dve.wait_ge(sig["s_ps"], u + 1)
                        dve.reduce_max(nm[:, u:u + 1], ps[2 + u % 3][:, 0:(u % CH + 1) * P], AX_X, negate=True).then_inc(sig["nm"], 1)

                    def normalise(h):
                        dve.wait_ge(sig["pv"], CH * (h + 1))
                        hs = rs[:, CH * h:CH * (h + 1)]
                        st.link(dve.reciprocal(hs, hs))
                        if h >= 2 and h % 2 == 0:
                            dve.wait_ge(sig["pt_ps"], turn_of_pair(h // 2 - 1) + 1)
                        dve.tensor_tensor(o[:, :, h % 2, :], ps[6 + h % 2][:, 0:CH * KL].rearrange("p (t c) -> p t c", c=KL),
                                          bc(hs, 2, KL), ALU.mult).then_inc(sig["o"], 1)

                    for h in range(2):
                        rotate_a(h)
                        rotate_b(h)
                    for u in range(NU):
                        h, t = u // CH, u % CH
                        maxima(u)
                        if t == 3 and h + 2 < NH:
                            rotate_a(h + 2)
                        if t == 0 and 2 <= h + 1 < NH:
                            rotate_b(h + 1)
                        if t == 2 and h >= 1:
                            normalise(h - 1)
                    normalise(NH - 1)
            end_of_iteration(nc, sig)


def two_expert_weights(nc, ctx, d):
    F = 2 * D
    FT = F // P
    sb = lambda n, s, t=F32: ctx.enter_context(nc.sbuf_tensor("te_" + n, s, t))
    sem = {"weights": ctx.enter_context(nc.semaphore("te_weights"))}
    wg = sb("wg", [P, K2, 2])
    wa, wb = sb("wa", [P, 2, K2, F]), sb("wb", [P, 2, FT, D])
    ba, bb = sb("ba", [P, 2, FT]), sb("bb", [P, 2, D])
    total = fetch(nc, sem, "weights", [(wg[:], d["te_wg"]), (wa[:], d["te_wa"]), (wb[:], d["te_wb"]), (ba[:], d["te_ba"]),
                                       (bb[:], d["te_bb"].partition_broadcast(P))])
    return sem, total, wg, wa, wb, ba, bb


def two_experts(nc, g, d, weights):
    F = 2 * D
    FT = F // P
    with ExitStack() as ctx:
        sb = lambda n, s, t=F32: ctx.enter_context(nc.sbuf_tensor("te_" + n, s, t))
        sig = signals(nc, ctx, "te", "xb lg lc m m1 up h down y z acc up_silu up_sg")
        sem, total, wg, wa, wb, ba, bb = weights
        xb, h = sb("xb", [P, K2, S]), sb("h", [P, 2, FT, S])
        lc, m = sb("lc", [P, CH, 2]), sb("m", [P, 2, CH])
        y = sb("y", [P, 2, CH, D])
        acc, gate = sb("acc", [P, CH, D]), sb("gate", [P, CH, D])
        ps, xn_fm = g["ps"], g["xn_fm"]
        arrive(nc, sem, "weights", total)
        with nc.Fori(0, B) as b:
            with nc.Block() as block:
                @block.tensor
                def _(pe):
                    def scores():
                        pe.wait_ge(sig["xb"], 1)
                        for t in range(CH):
                            for k in range(K2):
                                last = pe.matmul(ps[7][:, 2 * t:2 * t + 2], xb[:, k, t * P:(t + 1) * P], wg[:, k, :],
                                                 start=(k == 0), stop=(k == K2 - 1))
                        last.then_inc(sig["lg"], 1)

                    for e in range(2):
                        for f in range(FT):
                            u = e * FT + f
                            if u >= 3:
                                pe.wait_ge(sig["h"], u - 2)
                            for k in range(K2):
                                last = pe.matmul(ps[u % 3][:], wa[:, e, k, f * P:(f + 1) * P], xn_fm[:, k, ds(b * S, S)], start=(k == 0),
                                                 stop=(k == K2 - 1))
                            last.then_inc(sig["up"], 1)
                            if u == 0:
                                scores()
                    for e in range(2):
                        pe.wait_ge(sig["h"], FT * (e + 1))
                        for t in range(CH):
                            for f in range(FT):
                                last = pe.matmul(ps[3 + 2 * e + t // 2][:, (t % 2) * D:(t % 2 + 1) * D], h[:, e, f, t * P:(t + 1) * P], wb[:, e, f, :],
                                                 start=(f == 0), stop=(f == FT - 1))
                        last.then_inc(sig["down"], 1)

                @block.scalar
                def _(act):
                    act.activation(xb[:], xn_fm[:, :, ds(b * S, S)], ACT.Copy).then_inc(sig["xb"], 1)
                    for e in range(2):
                        for f in range(FT):
                            u = e * FT + f
                            act.wait_ge(sig["up"], u + 1)
                            act.activation(h[:, e, f, :], ps[u % 3][:], (ACT.Gelu, ACT.Relu)[e], bias=ba[:, e, f:f + 1]).then_inc(sig["h"], 1)
                    gates_of_row(act, sig, gate, lambda t: acc[:, t, :], lambda t: act.wait_ge(sig["acc"], t + 1))

                @block.vector
                def _(dve):
                    dve.wait_ge(sig["lg"], 1)
                    dve.tensor_copy(lc[:].rearrange("p t e -> p (t e)"), ps[7][:, 0:2 * CH]).then_inc(sig["lc"], 1)
                    dve.wait_ge(sig["lc"], 1)
                    dve.tensor_tensor(m[:, 0, :], lc[:, :, 0], lc[:, :, 1], ALU.is_ge).then_inc(sig["m"], 1)
                    dve.wait_ge(sig["m"], 1)
                    dve.tensor_scalar(m[:, 1, :], m[:, 0, :], -1.0, 1.0, ALU.mult, ALU.add).then_inc(sig["m1"], 1)
                    for e in range(2):
                        dve.wait_ge(sig["down"], e + 1)
                        for t in range(CH):
                            dve.tensor_tensor(y[:, e, t, :], ps[3 + 2 * e + t // 2][:, (t % 2) * D:(t % 2 + 1) * D], bb[:, e, :], ALU.add
                                              ).then_inc(sig["y"], 1)
                    dve.wait_ge(sig["m1"], 1)
                    dve.wait_ge(sig["y"], 2 * CH)
                    for t in range(CH):
                        dve.tensor_scalar(y[:, 1, t, :], y[:, 1, t, :], m[:, 1, t:t + 1], None, ALU.mult).then_inc(sig["z"], 1)
                    for t in range(CH):
                        dve.wait_ge(sig["z"], t + 1)
                        dve.scalar_tensor_tensor(out=acc[:, t, :], in0=y[:, 0, t, :], scalar=m[:, 0, t:t + 1], in1=y[:, 1, t, :],
                                                 op0=ALU.mult, op1=ALU.add).then_inc(sig["acc"], 1)
                    update_of_row(dve, g, sig, gate, b)
            end_of_iteration(nc, sig)


def program(nc, d, layers=(0, 1, 2, 3), dump=None):
    with ExitStack() as ctx:
        sb = lambda n, s, t=F32: ctx.enter_context(nc.sbuf_tensor(n, s, t))
        g = {"x": sb("x_res", [P, NT, D]), "xn_fm": sb("xn_fm", [P, K2, B * S]), "s": sb("s_mix", [P, NT, D]),
             "ident": sb("ident", [P, P]), "ones": sb("ones", [P, P]), "eps": sb("eps", [P, 1]),
             "eps6": sb("eps6", [P, 1])}
        g["ps"] = [ctx.enter_context(nc.psum_tensor("bank%d" % i, [P, 512], F32)) for i in range(8)]
        main = signals(nc, ctx, "main", "load store")
        g["ln_sig"] = signals(nc, ctx, "ln", "stats meanvar std rstd xn turned")
        with nc.Block() as block:
            @block.sync
            def _(sp):
                sp.dma_start(g["x"][:], d["x"]).then_inc(main["load"], 16)
                sp.dma_start(g["ident"][:], d["c_ident"]).then_inc(main["load"], 16)
                sp.wait_ge(main["load"], 32)

            @block.vector
            def _(dve):
                dve.memset(g["ones"][:], 1.0)
                dve.memset(g["eps"][:], LN_EPS)
                dve.memset(g["eps6"][:], 1e-6)
        end_of_iteration(nc, main)
        if 0 in layers:
            g["layer"] = 0
            with ExitStack() as layer:
                kind = ("e0", 8, 128, 0, False)
                weights = expert_weights(nc, layer, d, *kind)
                mamba(nc, g, d)
                if not dump: experts(nc, g, d, *kind, weights)
        if 1 in layers:
            g["layer"] = 1
            delta_rule(nc, g, d)
            if not dump: nvfp4_mlp(nc, g, d)
        if 2 in layers:
            g["layer"] = 2
            with ExitStack() as layer:
                kind = ("e2", 16, 176, 2, True)
                weights = expert_weights(nc, layer, d, *kind)
                linear_attention(nc, g, d)
                if not dump: experts(nc, g, d, *kind, weights)
        if 3 in layers:
            g["layer"] = 3
            with ExitStack() as layer:
                weights = two_expert_weights(nc, layer, d)
                latent_attention(nc, g, d)
                if not dump: two_experts(nc, g, d, weights)
        with nc.Block() as block:
            @block.sync
            def _(sp):
                sp.dma_start(d["out"], g[dump or "x"][:]).then_inc(main["store"], 16)
                sp.wait_ge(main["store"], 16)


def fm(w):
    o, i = w.shape
    return w.T.reshape(i // K2, K2, o)


def layouts(a):
    r = {}
    r["x"] = a["L0_attn_x"].reshape(NT, P, D).transpose(1, 0, 2)
    r["c_ident"] = np.eye(P, dtype=np.float32)
    r["ma_wx"] = fm(a["L0_attn_W_x"])
    r["ma_wdt"] = a["L0_attn_W_dt"].reshape(P, K2, 64).transpose(2, 1, 0)
    r["ma_bdt"] = a["L0_attn_b_dt"].reshape(P, K2)
    r["ma_alog"] = a["L0_attn_A_log"].reshape(P, K2, 16)
    r["ma_d"] = a["L0_attn_D"].reshape(P, K2)
    r["e0_router"] = fm(a["L0_ffn_router_gate"])
    gu = a["L0_ffn_expert_gate_up"].reshape(8, P, K2, 128, 2)
    r["e0_w13"] = gu.transpose(1, 2, 4, 0, 3).reshape(P, K2, 2, 1024)
    r["e0_w2"] = a["L0_ffn_expert_down"].transpose(1, 0, 2)
    r["e2_router"] = fm(a["L2_ffn_gate_w"])
    w1 = np.concatenate([a["L2_ffn_w1"], a["L2_ffn_sw1"].reshape(2, 176, D)])
    w3 = np.concatenate([a["L2_ffn_w3"], a["L2_ffn_sw3"].reshape(2, 176, D)])
    r["e2_w13"] = np.stack([w1, w3]).reshape(2, 18 * 176, P, K2).transpose(2, 3, 0, 1)
    w2 = np.concatenate([a["L2_ffn_w2"], a["L2_ffn_sw2"].reshape(D, 2, 176).transpose(1, 0, 2)]).transpose(0, 2, 1).reshape(18 * 176, D)
    r["e2_w2"], r["e2_w2_last"] = w2[:24 * P].reshape(24, P, D).transpose(1, 0, 2), w2[24 * P:]
    r["c_owner"] = ((np.arange(96) % 32)[:, None] == np.arange(18 * 176)[None, :] // 176).astype(np.float32)
    r["dr_wba"] = fm(np.concatenate([a["L1_attn_w_beta"], a["L1_attn_w_alpha"]]))
    r["dr_loga"], r["dr_dtb"], r["dr_rms"] = a["L1_attn_log_A"], a["L1_attn_dt_bias"], a["L1_attn_rms_w"].reshape(P, 1)
    i = np.arange(P)
    r["c_tri"] = (i[:, None] <= i[None, :]).astype(np.float32)
    r["c_low"] = (i[:, None] > i[None, :]).astype(np.float32)
    lm, half = [], np.arange(64)[None, :]
    for s in (1, 2, 4, 8, 16, 32, 64):
        lm.append((i[:, None] // (2 * s) == half // s) & (i[:, None] % (2 * s) < s))
    r["c_lmask"] = np.stack(lm, 1).astype(np.float32)
    slots = [0, 1, 2, 3, 0]
    w, cw = a["L1_attn_w_qkv"], a["L1_attn_conv_w"].reshape(4096, 4)
    rows = [np.concatenate([1024 + np.arange(256) + 256 * n, np.arange(256) + 256 * n, 2048 + np.arange(512) + 512 * n]) for n in slots]
    r["dr_wq"] = np.stack([fm(w[q]) for q in rows])
    r["dr_cw"] = np.stack([cw[q].reshape(8, P, 4).transpose(1, 0, 2) for q in rows])
    r["dr_wg"] = np.stack([fm(a["L1_attn_w_gate"][512 * n:512 * n + 512]) for n in slots])
    r["dr_wo"] = np.stack([a["L1_attn_w_out"][:, 512 * n:512 * n + 512].T.reshape(4, P, D).transpose(1, 0, 2) for n in slots])
    order = np.arange(2048).reshape(8, P, 2).transpose(0, 2, 1).ravel()
    for n in ("gate", "up"):
        r["nv_" + n + "_w"] = a["L1_ffn_" + n + "_W_packed"].T[:, order]
        r["nv_" + n + "_s"] = np.repeat(a["L1_ffn_" + n + "_scales"].T[:, order], 16, axis=0)
    r["nv_down_w"] = a["L1_ffn_down_W_packed"].reshape(D, 8, P).transpose(2, 1, 0).reshape(P, 8 * D)
    r["nv_down_s"] = np.repeat(a["L1_ffn_down_scales"].reshape(D, 8, 8).transpose(2, 1, 0), 16, axis=0).reshape(P, 8 * D)
    for n in "qkv":
        r["la_w" + n] = fm(a["L2_attn_W" + n])
    r["la_wo"] = a["L2_attn_Wo"].T.reshape(K2, P, D).transpose(1, 0, 2)
    r["la_bq"] = a["L2_attn_bq"].reshape(K2, P).T
    r["la_bk"], r["la_bv"], r["la_bo"] = a["L2_attn_bk"], a["L2_attn_bv"], a["L2_attn_bo"]
    r["c_dec"] = np.exp(-np.arange(S, dtype=np.float32) / np.float32(S))
    r["c_dec_col"] = r["c_dec"].reshape(CH, P).T
    r["c_blocks"] = (i[:, None] // 16 == i[None, :] // 16).astype(np.float32)
    rot = (np.arange(64) + 32) % 64
    wa = a["L3_attn_w_kv_a"]
    pe = wa[:, 256:]
    cat = np.concatenate([wa[:, :256], pe, pe, pe[:, rot], pe[:, rot]], 1)
    r["mla_wa"] = fm(cat.T)
    r["mla_qg"] = a["L3_attn_q_a_gamma"].reshape(2, 96).T
    r["mla_kg"] = a["L3_attn_kv_a_gamma"].reshape(64, 1)
    inv = np.float32(1.0) / np.float32(10000.0) ** (np.arange(0, 64, 2, dtype=np.float32) / np.float32(64))
    ang = np.concatenate([np.arange(S, dtype=np.float32)[:, None] * inv] * 2, 1).T
    sign = np.where(np.arange(64) < 32, -1, 1).astype(np.float32)[:, None]
    r["c_cos2"] = np.concatenate([np.cos(ang)] * 2)
    r["c_sin2"] = np.concatenate([np.sin(ang) * sign] * 2)
    scale = np.float32(192 ** -0.5)
    r["c_qcos"] = np.concatenate([np.cos(ang)] * 2) * scale
    r["c_qsin"] = np.concatenate([np.sin(ang) * -sign] * 2) * scale
    wq = a["L3_attn_w_qb"].reshape(2, 96, 16, 192)
    r["mla_wqp"] = wq[..., 128:].transpose(1, 0, 2, 3)
    r["mla_wqn"] = wq[..., :128].transpose(3, 2, 0, 1).reshape(128, 16, 192)
    wkv = a["L3_attn_w_kvb"].reshape(64, 16, 256).transpose(2, 1, 0)
    r["mla_wk"] = wkv[:128]
    r["mla_wv"] = np.concatenate([wkv[128:]] * 2, -1)
    r["mla_wo"] = a["L3_attn_w_o"].reshape(16, P, D).transpose(1, 0, 2)
    r["c_later"] = np.where(i[None, :] > i[:, None], np.float32(-1e30), np.float32(0))
    r["te_wg"] = fm(a["L3_ffn_Wg"])
    r["te_wa"] = np.stack([fm(a["L3_ffn_W0a"]), fm(a["L3_ffn_W1a"])], 1)
    r["te_wb"] = np.stack([a["L3_ffn_W0b"].T.reshape(4, P, D), a["L3_ffn_W1b"].T.reshape(4, P, D)]).transpose(2, 0, 1, 3)
    r["te_ba"] = np.stack([a["L3_ffn_b0a"].reshape(4, P), a["L3_ffn_b1a"].reshape(4, P)]).transpose(2, 0, 1)
    r["te_bb"] = np.stack([a["L3_ffn_b0b"], a["L3_ffn_b1b"]])
    return r


def kernel(**inputs):
    import concourse.bacc as _bacc
    from concourse.bass_utils import run_bass_kernel_spmd as _run

    nc = _bacc.Bacc("TRN2", target_bir_lowering=False, num_devices=1)
    arrays = {"in_" + k: np.ascontiguousarray(v) for k, v in layouts({k: np.asarray(v) for k, v in inputs.items()}).items()}
    d = {k[3:]: nc.dram_tensor(k, v.shape, mybir.dt.from_np(v.dtype), kind="ExternalInput").ap() for k, v in arrays.items()}
    d["out"] = nc.dram_tensor("out", (P, NT, D), F32, kind="ExternalOutput").ap()
    program(nc, d)
    r = _run(nc, [arrays], core_ids=[0])
    return np.asarray(r.results[0]["out"]).transpose(1, 0, 2).reshape(B, S, D)
```
